# Optimizing a Trainium2 kernel written in Bass

```python
import numpy as np
import jax
import jax.numpy as jnp

def _softmax(x, axis=-1):
    return jax.nn.softmax(x, axis=axis)

def _gelu(x):
    return jax.nn.gelu(x, approximate=True)

def _silu(x):
    return jax.nn.silu(x)

def _sigmoid(x):
    return jax.nn.sigmoid(x)

def _layernorm(x, axis=-1, eps=1e-05):
    m = jnp.mean(x, axis=axis, keepdims=True)
    v = jnp.var(x, axis=axis, keepdims=True)
    return (x - m) / jnp.sqrt(v + eps)

def _scatter_add(tgt, idx, src, axis=0):
    return tgt.at[idx].add(src)

def _segment_sum(src, seg, n):
    return jax.ops.segment_sum(src, seg, n)
kernel_name = 'mk_xattn_seq_d2_seqx_r8_2d439c'

def setup_inputs(seed: int=0):
    np.random.seed(seed)
    _w = jnp.asarray

    def _rec_inputs():
        import jax
        import jax.numpy as jnp
        _rk = jax.random.key(seed)
        x = -0.0003929 + 0.9999 * jax.random.normal(jax.random.fold_in(_rk, 1), (8, 56, 256), jnp.float32)
        _lenS = 56 - jax.random.randint(jax.random.fold_in(_rk, 7), (8,), 0, max(1, 56 // 4) + 1, jnp.int32)
        _lenS2 = 1500 - jax.random.randint(jax.random.fold_in(_rk, 8), (8,), 0, max(1, 1500 // 4) + 1, jnp.int32)
        _ctx_2048P = jax.random.normal(jax.random.fold_in(_rk, 11), (8, 16, 256), jnp.float32)
        _ctx_2048c = jax.random.dirichlet(jax.random.fold_in(_rk, 511), 0.3 * jnp.ones((16,), jnp.float32), (8, 1500))
        _ctx_2048t = jnp.einsum('bsk,bkd->bsd', _ctx_2048c, _ctx_2048P)
        _ctx_2048t = _ctx_2048t * jax.lax.rsqrt(jnp.mean(jnp.square(_ctx_2048t)) + 1e-12) * 0.953939
        ctx_2048 = -8.57375e-05 + 0.999917 * (_ctx_2048t + 0.3 * jax.random.normal(jax.random.fold_in(_rk, 611), (8, 1500, 256), jnp.float32))
        _validS = jnp.arange(56)[None, :] < _lenS[:, None]
        _validS2 = jnp.arange(1500)[None, :] < _lenS2[:, None]
        _causal = jnp.tril(jnp.ones((56, 56), dtype=bool))
        mask_BxS2_bf1 = jnp.ones((8, 1500), dtype=bool)
        return (x, ctx_2048, mask_BxS2_bf1)
    x, ctx_2048, mask_BxS2_bf1 = _rec_inputs()

    def _L0_xattn_setup():
        import jax, jax.numpy as jnp
        import numpy as np
        HIDDEN = 256
        HEADS = 16
        HEAD_DIM = HIDDEN // HEADS
        LN_EPS = 1e-05
        GATE_INIT = 0.5

        def _layer_norm(x, gamma, beta):
            mu = jnp.mean(x, axis=-1, keepdims=True)
            var = jnp.mean(jnp.square(x - mu), axis=-1, keepdims=True)
            return (x - mu) * jax.lax.rsqrt(var + LN_EPS) * gamma + beta
        key = jax.random.key(seed)
        ks = jax.random.split(key, 8)
        B, T_TEXT, T_AUDIO = (4, 256, 1500)
        s = 0.02
        return {'hidden_states': jax.random.normal(ks[0], (B, T_TEXT, HIDDEN), jnp.float32), 'audio_kv': jax.random.normal(ks[1], (B, T_AUDIO, HIDDEN), jnp.float32), 'audio_attention_mask': jnp.ones((B, T_AUDIO), dtype=bool), 'Wq': jax.random.normal(ks[2], (HIDDEN, HIDDEN), jnp.float32) * s, 'Wk': jax.random.normal(ks[3], (HIDDEN, HIDDEN), jnp.float32) * s, 'Wv': jax.random.normal(ks[4], (HIDDEN, HIDDEN), jnp.float32) * s, 'Wo': jax.random.normal(ks[5], (HIDDEN, HIDDEN), jnp.float32) * s, 'ln_gamma': jnp.ones((HIDDEN,), jnp.float32), 'ln_beta': jnp.zeros((HIDDEN,), jnp.float32), 'gate': jnp.array([GATE_INIT], jnp.float32)}
    _L0_xattn_all = _L0_xattn_setup()
    _L0_xattn_in = {k: v for k, v in _L0_xattn_all.items() if k in ('Wq', 'Wk', 'Wv', 'Wo', 'ln_gamma', 'ln_beta', 'gate')}
    del _L0_xattn_all

    def _L1_xattn_setup():
        import jax, jax.numpy as jnp
        import numpy as np
        B, Q, S1, S2 = (4, 32, 256, 256)
        D, H, K, F = (256, 16, 128, 1024)
        LN_EPS = 1e-05

        def _layer_norm(x, scale, offset):
            mu = jnp.mean(x, axis=-1, keepdims=True)
            var = jnp.var(x, axis=-1, keepdims=True)
            return (x - mu) * jax.lax.rsqrt(var + LN_EPS) * scale + offset

        def _cross_attention(q_in, kv_in, wq, bq, wk, bk, wv, bv, wo, bo, bias_k, bias_v):
            b, q_len, _ = q_in.shape
            t = kv_in.shape[1]
            qh = (q_in @ wq + bq).reshape(b, q_len, H, K)
            kh = (kv_in @ wk + bk).reshape(b, t, H, K)
            vh = (kv_in @ wv + bv).reshape(b, t, H, K)
            kh = jnp.concatenate([kh, jnp.broadcast_to(bias_k, (b, 1, H, K))], axis=1)
            vh = jnp.concatenate([vh, jnp.broadcast_to(bias_v, (b, 1, H, K))], axis=1)
            scale = jnp.sqrt(jnp.asarray(K, q_in.dtype))
            logits = jnp.einsum('bqhk,bthk->bhqt', qh, kh) / scale
            weights = jax.nn.softmax(logits, axis=-1)
            ctx = jnp.einsum('bhqt,bthk->bqhk', weights, vh).reshape(b, q_len, H * K)
            return ctx @ wo + bo

        def _forward(x, xf_1, xf_2, ln1_scale, ln1_offset, wq1, bq1, wk1, bk1, wv1, bv1, wo1, bo1, bias_k1, bias_v1, ln2_scale, ln2_offset, wq2, bq2, wk2, bk2, wv2, bv2, wo2, bo2, bias_k2, bias_v2, ln_mlp_scale, ln_mlp_offset, w_fc1, b_fc1, w_fc2, b_fc2):
            res = x
            h = _layer_norm(x, ln1_scale, ln1_offset)
            x = res + _cross_attention(h, xf_1, wq1, bq1, wk1, bk1, wv1, bv1, wo1, bo1, bias_k1, bias_v1)
            res = x
            h = _layer_norm(x, ln2_scale, ln2_offset)
            x = res + _cross_attention(h, xf_2, wq2, bq2, wk2, bk2, wv2, bv2, wo2, bo2, bias_k2, bias_v2)
            h = _layer_norm(x, ln_mlp_scale, ln_mlp_offset)
            h = jax.nn.gelu(h @ w_fc1 + b_fc1, approximate=False) @ w_fc2 + b_fc2
            return x + h
        key = jax.random.key(seed)
        ks = iter(jax.random.split(key, 64))

        def rn(shape, s=0.02):
            return jax.random.normal(next(ks), shape, jnp.float32) * s
        inp = {'x': rn((B, Q, D), 1.0), 'xf_1': rn((B, S1, D), 1.0), 'xf_2': rn((B, S2, D), 1.0)}
        for i in (1, 2):
            inp[f'ln{i}_scale'] = jnp.ones((D,), jnp.float32)
            inp[f'ln{i}_offset'] = jnp.zeros((D,), jnp.float32)
            inp[f'wq{i}'] = rn((D, H * K))
            inp[f'bq{i}'] = jnp.zeros((H * K,), jnp.float32)
            inp[f'wk{i}'] = rn((D, H * K))
            inp[f'bk{i}'] = jnp.zeros((H * K,), jnp.float32)
            inp[f'wv{i}'] = rn((D, H * K))
            inp[f'bv{i}'] = jnp.zeros((H * K,), jnp.float32)
            inp[f'wo{i}'] = rn((H * K, D))
            inp[f'bo{i}'] = jnp.zeros((D,), jnp.float32)
            inp[f'bias_k{i}'] = rn((1, 1, H, K))
            inp[f'bias_v{i}'] = rn((1, 1, H, K))
        inp['ln_mlp_scale'] = jnp.ones((D,), jnp.float32)
        inp['ln_mlp_offset'] = jnp.zeros((D,), jnp.float32)
        inp['w_fc1'] = rn((D, F))
        inp['b_fc1'] = jnp.zeros((F,), jnp.float32)
        inp['w_fc2'] = rn((F, D))
        inp['b_fc2'] = jnp.zeros((D,), jnp.float32)
        return inp
    _L1_xattn_all = _L1_xattn_setup()
    _L1_xattn_in = {k: v for k, v in _L1_xattn_all.items() if k in ('ln1_scale', 'ln1_offset', 'wq1', 'bq1', 'wk1', 'bk1', 'wv1', 'bv1', 'wo1', 'bo1', 'bias_k1', 'bias_v1', 'ln2_scale', 'ln2_offset', 'wq2', 'bq2', 'wk2', 'bk2', 'wv2', 'bv2', 'wo2', 'bo2', 'bias_k2', 'bias_v2', 'ln_mlp_scale', 'ln_mlp_offset', 'w_fc1', 'b_fc1', 'w_fc2', 'b_fc2')}
    del _L1_xattn_all
    return {'x': x, 'ctx_2048': ctx_2048, 'mask_BxS2_bf1': mask_BxS2_bf1, 'L0_xattn_Wq': _L0_xattn_in['Wq'], 'L0_xattn_Wk': _L0_xattn_in['Wk'], 'L0_xattn_Wv': _L0_xattn_in['Wv'], 'L0_xattn_Wo': _L0_xattn_in['Wo'], 'L0_xattn_ln_gamma': _L0_xattn_in['ln_gamma'], 'L0_xattn_ln_beta': _L0_xattn_in['ln_beta'], 'L0_xattn_gate': _L0_xattn_in['gate'], 'L1_xattn_ln1_scale': _L1_xattn_in['ln1_scale'], 'L1_xattn_ln1_offset': _L1_xattn_in['ln1_offset'], 'L1_xattn_wq1': _L1_xattn_in['wq1'], 'L1_xattn_bq1': _L1_xattn_in['bq1'], 'L1_xattn_wk1': _L1_xattn_in['wk1'], 'L1_xattn_bk1': _L1_xattn_in['bk1'], 'L1_xattn_wv1': _L1_xattn_in['wv1'], 'L1_xattn_bv1': _L1_xattn_in['bv1'], 'L1_xattn_wo1': _L1_xattn_in['wo1'], 'L1_xattn_bo1': _L1_xattn_in['bo1'], 'L1_xattn_bias_k1': _L1_xattn_in['bias_k1'], 'L1_xattn_bias_v1': _L1_xattn_in['bias_v1'], 'L1_xattn_ln2_scale': _L1_xattn_in['ln2_scale'], 'L1_xattn_ln2_offset': _L1_xattn_in['ln2_offset'], 'L1_xattn_wq2': _L1_xattn_in['wq2'], 'L1_xattn_bq2': _L1_xattn_in['bq2'], 'L1_xattn_wk2': _L1_xattn_in['wk2'], 'L1_xattn_bk2': _L1_xattn_in['bk2'], 'L1_xattn_wv2': _L1_xattn_in['wv2'], 'L1_xattn_bv2': _L1_xattn_in['bv2'], 'L1_xattn_wo2': _L1_xattn_in['wo2'], 'L1_xattn_bo2': _L1_xattn_in['bo2'], 'L1_xattn_bias_k2': _L1_xattn_in['bias_k2'], 'L1_xattn_bias_v2': _L1_xattn_in['bias_v2'], 'L1_xattn_ln_mlp_scale': _L1_xattn_in['ln_mlp_scale'], 'L1_xattn_ln_mlp_offset': _L1_xattn_in['ln_mlp_offset'], 'L1_xattn_w_fc1': _L1_xattn_in['w_fc1'], 'L1_xattn_b_fc1': _L1_xattn_in['b_fc1'], 'L1_xattn_w_fc2': _L1_xattn_in['w_fc2'], 'L1_xattn_b_fc2': _L1_xattn_in['b_fc2']}

def reference(x, ctx_2048, mask_BxS2_bf1, L0_xattn_Wq, L0_xattn_Wk, L0_xattn_Wv, L0_xattn_Wo, L0_xattn_ln_gamma, L0_xattn_ln_beta, L0_xattn_gate, L1_xattn_ln1_scale, L1_xattn_ln1_offset, L1_xattn_wq1, L1_xattn_bq1, L1_xattn_wk1, L1_xattn_bk1, L1_xattn_wv1, L1_xattn_bv1, L1_xattn_wo1, L1_xattn_bo1, L1_xattn_bias_k1, L1_xattn_bias_v1, L1_xattn_ln2_scale, L1_xattn_ln2_offset, L1_xattn_wq2, L1_xattn_bq2, L1_xattn_wk2, L1_xattn_bk2, L1_xattn_wv2, L1_xattn_bv2, L1_xattn_wo2, L1_xattn_bo2, L1_xattn_bias_k2, L1_xattn_bias_v2, L1_xattn_ln_mlp_scale, L1_xattn_ln_mlp_offset, L1_xattn_w_fc1, L1_xattn_b_fc1, L1_xattn_w_fc2, L1_xattn_b_fc2):
    import jax
    import jax.numpy as jnp

    def _L0_xattn_ref(hidden_states, audio_kv, audio_attention_mask, Wq, Wk, Wv, Wo, ln_gamma, ln_beta, gate):
        import jax, jax.numpy as jnp
        import numpy as np
        HIDDEN = 256
        HEADS = 16
        HEAD_DIM = HIDDEN // HEADS
        LN_EPS = 1e-05
        GATE_INIT = 0.5

        def _layer_norm(x, gamma, beta):
            mu = jnp.mean(x, axis=-1, keepdims=True)
            var = jnp.mean(jnp.square(x - mu), axis=-1, keepdims=True)
            return (x - mu) * jax.lax.rsqrt(var + LN_EPS) * gamma + beta
        B, Tt, D = hidden_states.shape
        Ta = audio_kv.shape[1]
        scale = HEAD_DIM ** (-0.5)
        a = _layer_norm(audio_kv, ln_gamma, ln_beta)
        Q = (hidden_states @ Wq.T).reshape(B, Tt, HEADS, HEAD_DIM).transpose(0, 2, 1, 3)
        K = (a @ Wk.T).reshape(B, Ta, HEADS, HEAD_DIM).transpose(0, 2, 1, 3)
        V = (a @ Wv.T).reshape(B, Ta, HEADS, HEAD_DIM).transpose(0, 2, 1, 3)
        scores = jnp.einsum('bhtd,bhsd->bhts', Q, K) * scale
        mask = audio_attention_mask[:, None, None, :]
        scores = jnp.where(mask, scores, jnp.float32(-jnp.inf))
        attn = jax.nn.softmax(scores, axis=-1)
        out = jnp.einsum('bhts,bhsd->bhtd', attn, V)
        out = out.transpose(0, 2, 1, 3).reshape(B, Tt, D)
        out = out @ Wo.T
        return hidden_states + jnp.tanh(gate) * out

    def _L1_xattn_ref(x, xf_1, xf_2, ln1_scale, ln1_offset, wq1, bq1, wk1, bk1, wv1, bv1, wo1, bo1, bias_k1, bias_v1, ln2_scale, ln2_offset, wq2, bq2, wk2, bk2, wv2, bv2, wo2, bo2, bias_k2, bias_v2, ln_mlp_scale, ln_mlp_offset, w_fc1, b_fc1, w_fc2, b_fc2):
        import jax, jax.numpy as jnp
        import numpy as np
        B, Q, S1, S2 = (4, 32, 256, 256)
        D, H, K, F = (256, 16, 128, 1024)
        LN_EPS = 1e-05

        def _layer_norm(x, scale, offset):
            mu = jnp.mean(x, axis=-1, keepdims=True)
            var = jnp.var(x, axis=-1, keepdims=True)
            return (x - mu) * jax.lax.rsqrt(var + LN_EPS) * scale + offset

        def _cross_attention(q_in, kv_in, wq, bq, wk, bk, wv, bv, wo, bo, bias_k, bias_v):
            b, q_len, _ = q_in.shape
            t = kv_in.shape[1]
            qh = (q_in @ wq + bq).reshape(b, q_len, H, K)
            kh = (kv_in @ wk + bk).reshape(b, t, H, K)
            vh = (kv_in @ wv + bv).reshape(b, t, H, K)
            kh = jnp.concatenate([kh, jnp.broadcast_to(bias_k, (b, 1, H, K))], axis=1)
            vh = jnp.concatenate([vh, jnp.broadcast_to(bias_v, (b, 1, H, K))], axis=1)
            scale = jnp.sqrt(jnp.asarray(K, q_in.dtype))
            logits = jnp.einsum('bqhk,bthk->bhqt', qh, kh) / scale
            weights = jax.nn.softmax(logits, axis=-1)
            ctx = jnp.einsum('bhqt,bthk->bqhk', weights, vh).reshape(b, q_len, H * K)
            return ctx @ wo + bo

        def _forward(x, xf_1, xf_2, ln1_scale, ln1_offset, wq1, bq1, wk1, bk1, wv1, bv1, wo1, bo1, bias_k1, bias_v1, ln2_scale, ln2_offset, wq2, bq2, wk2, bk2, wv2, bv2, wo2, bo2, bias_k2, bias_v2, ln_mlp_scale, ln_mlp_offset, w_fc1, b_fc1, w_fc2, b_fc2):
            res = x
            h = _layer_norm(x, ln1_scale, ln1_offset)
            x = res + _cross_attention(h, xf_1, wq1, bq1, wk1, bk1, wv1, bv1, wo1, bo1, bias_k1, bias_v1)
            res = x
            h = _layer_norm(x, ln2_scale, ln2_offset)
            x = res + _cross_attention(h, xf_2, wq2, bq2, wk2, bk2, wv2, bv2, wo2, bo2, bias_k2, bias_v2)
            h = _layer_norm(x, ln_mlp_scale, ln_mlp_offset)
            h = jax.nn.gelu(h @ w_fc1 + b_fc1, approximate=False) @ w_fc2 + b_fc2
            return x + h
        return _forward(x, xf_1, xf_2, ln1_scale, ln1_offset, wq1, bq1, wk1, bk1, wv1, bv1, wo1, bo1, bias_k1, bias_v1, ln2_scale, ln2_offset, wq2, bq2, wk2, bk2, wv2, bv2, wo2, bo2, bias_k2, bias_v2, ln_mlp_scale, ln_mlp_offset, w_fc1, b_fc1, w_fc2, b_fc2)
    x = _L0_xattn_ref(x, ctx_2048, mask_BxS2_bf1, L0_xattn_Wq, L0_xattn_Wk, L0_xattn_Wv, L0_xattn_Wo, L0_xattn_ln_gamma, L0_xattn_ln_beta, L0_xattn_gate)
    x = _L1_xattn_ref(x, ctx_2048, ctx_2048, L1_xattn_ln1_scale, L1_xattn_ln1_offset, L1_xattn_wq1, L1_xattn_bq1, L1_xattn_wk1, L1_xattn_bk1, L1_xattn_wv1, L1_xattn_bv1, L1_xattn_wo1, L1_xattn_bo1, L1_xattn_bias_k1, L1_xattn_bias_v1, L1_xattn_ln2_scale, L1_xattn_ln2_offset, L1_xattn_wq2, L1_xattn_bq2, L1_xattn_wk2, L1_xattn_bk2, L1_xattn_wv2, L1_xattn_bv2, L1_xattn_wo2, L1_xattn_bo2, L1_xattn_bias_k2, L1_xattn_bias_v2, L1_xattn_ln_mlp_scale, L1_xattn_ln_mlp_offset, L1_xattn_w_fc1, L1_xattn_b_fc1, L1_xattn_w_fc2, L1_xattn_b_fc2)
    return x

_drawn_inputs = setup_inputs


def setup_inputs(seed=0):
    import zlib

    import numpy as np

    out = dict(_drawn_inputs(seed))
    spreads = {'L0_xattn_ln_gamma': (1.0, 0.6),
     'L0_xattn_ln_beta': (0.0, 0.8),
     'L1_xattn_ln1_scale': (1.0, 0.6),
     'L1_xattn_ln1_offset': (0.0, 0.8),
     'L1_xattn_bq1': (0.0, 0.8),
     'L1_xattn_bk1': (0.0, 2.0),
     'L1_xattn_bv1': (0.0, 0.1),
     'L1_xattn_bo1': (0.0, 0.1),
     'L1_xattn_ln2_scale': (1.0, 0.6),
     'L1_xattn_ln2_offset': (0.0, 0.8),
     'L1_xattn_bq2': (0.0, 0.8),
     'L1_xattn_bk2': (0.0, 2.0),
     'L1_xattn_bv2': (0.0, 0.1),
     'L1_xattn_bo2': (0.0, 0.1),
     'L1_xattn_ln_mlp_scale': (1.0, 0.6),
     'L1_xattn_ln_mlp_offset': (0.0, 0.675),
     'L1_xattn_b_fc1': (0.0, 0.1),
     'L1_xattn_b_fc2': (0.0, 0.1)}
    factors = {'L0_xattn_Wq': 8.0,
     'L0_xattn_Wk': 8.0,
     'L1_xattn_wq1': 8.0,
     'L1_xattn_wk1': 8.0,
     'L1_xattn_bias_k1': 64.0,
     'L1_xattn_bias_v1': 64.0,
     'L1_xattn_wq2': 8.0,
     'L1_xattn_wk2': 8.0,
     'L1_xattn_bias_k2': 64.0,
     'L1_xattn_bias_v2': 64.0}
    for name, (base, spread) in spreads.items():
        noise = np.random.default_rng([zlib.crc32(name.encode()), seed]).standard_normal(out[name].shape)
        drawn = base * np.exp(spread * noise) if base else spread * noise
        out[name] = jnp.asarray(drawn.astype(out[name].dtype))
    for name, factor in factors.items():
        out[name] = (out[name] * factor).astype(out[name].dtype)
    return out
```

```python
from contextlib import ExitStack

import concourse.bass as bass
from concourse import mybir

F32 = mybir.dt.float32
F32R = mybir.dt.float32r
U8 = mybir.dt.uint8
ALU = mybir.AluOpType
ACT = mybir.ActivationFunctionType
AX = mybir.AxisListType

P = 128
B = 8
TQ = 56
D = 256
DH = D // P
S = 1500
H = 16
HD0 = D // H
K = 128
NQ = B * TQ
ROWS = H * TQ
TILES = ROWS // P
GT = B * TILES
CH = -(-S // P)
TAIL = S - (CH - 1) * P
SB = S // 3
GRP = CH // 3
F = 1024
EPS = 1e-5
PAD = P
QBUF = [t % 2 if t < TILES - 1 else 2 for t in range(TILES)]
HPC = P // HD0


def build(nc, io):
    with ExitStack() as ctx:
        def sb(name, shape, dt=F32):
            return ctx.enter_context(nc.sbuf_tensor(name, shape, dt))

        def sem(name):
            return ctx.enter_context(nc.semaphore(name))

        ps = ctx.enter_context(nc.psum_tensor("ps", [P, 8, 512], F32))

        qo = sb("qo", [P, DH, PAD + B * ROWS])
        xt = sb("xt", [P, DH, NQ])
        raw_t = sb("raw_t", [P, DH, S])
        raw = sb("raw", [P, CH, D])
        ct = sb("ct", [P, 2, DH, S], F32R)
        cx = sb("cx", [P, CH, 2 * D], F32R)
        ident = sb("ident", [P, P])
        mean_w = sb("mean_w", [P, P])
        head_rows = sb("head_rows", [P, HPC, 1])
        head_cols = sb("head_cols", [P, HPC, P])
        vec = sb("vec", [P, 64])
        gate_t = sb("gate_t", [P, 2])
        AR = 6144
        ar = sb("ar", [P, AR])
        RR = 7936
        rr = sb("rr", [P, RR], F32R)
        mx4 = sb("mx4", [P, 4])
        negm = sb("negm", [P, 1])
        rowsum = sb("rowsum", [P, 1])
        extra = sb("extra", [P, 1])
        total = sb("total", [P, 1])
        rinv = sb("rinv", [P, 1])
        lbq = sb("lbq", [P, GT])
        pbq = sb("pbq", [P, GT])
        o_low = sb("o_low", [P, D])
        o_row = sb("o_row", [P, D])
        bn = sb("bn", [P, CH, 6])
        mv = sb("mv", [P, 2, CH])
        mv_row = sb("mv_row", [2 * CH, P])
        mhalf = sb("mhalf", [P, CH])

        def at(t, off, *shape):
            n = 1
            for s in shape:
                n *= s
            v = t[:, off:off + n]
            if len(shape) == 2:
                v = v.rearrange("p (a b) -> p a b", b=shape[1])
            if len(shape) == 3:
                v = v.rearrange("p (a b c) -> p a b c", b=shape[1], c=shape[2])
            return v

        prob = at(ar, 0, CH * P)
        mask_b = at(ar, 1536, S)
        mu_b = at(ar, 1536 + 1500, S)
        rs_b = at(ar, 1536 + 3000, S)
        pt = at(rr, 0, 2, CH, P)
        qt = at(rr, 2 * CH * P, 6, DH, P)
        xc = at(ar, 0, DH, NQ)
        sq = at(ar, 896, DH, NQ)
        var = at(ar, 1792, NQ)
        dev = at(ar, 2240, NQ)
        tmp = at(ar, 2688, NQ)
        ht = at(ar, 3136, DH, NQ)
        w_raw = at(ar, 4032, 2, 512)
        dk_raw = at(ar, 5056, 2, 256)
        dk = at(ar, 5568, 2, P)
        dk_prod = at(ar, 5824, 2, P)
        g32 = at(ar, 0, 2, NQ)
        w_s = at(rr, 0, 4, 512)
        h1 = at(rr, 2048, 4, NQ)
        oh = at(rr, 3840, 2 * 2, DH * NQ)
        hs = at(rr, 3840, 2, DH, NQ)
        dv_m = at(rr, 3840 + 3584, 2, P)
        small = sb("small", [P, 2 * P + NQ])
        dv = small[0:80, 0:P]
        dv2 = small[0:80, P:2 * P]
        pb_f = small[0:80, 2 * P:2 * P + NQ]
        pb_s = sb("pb_s", [80, NQ], F32R)
        dvr = sb("dvr", [80, P])
        dv_hi = sb("dv_hi", [80, P], F32R)
        mask_u8 = sb("mask_u8", [P, S], U8)
        tmp16 = sb("tmp16", [H, 1])
        hsel = sb("hsel", [96, H])
        u_k = sb("u_k", [P, DH, H])
        cb = sb("cb", [H, 4 * P])
        cbv = sb("cbv", [H, 1])
        lb_s = sb("lb_s", [H, NQ])
        tiles_row = sb("tiles_row", [GT, P])

        NV = 0
        V = {}
        for n, w in (("g0", DH), ("b0", DH), ("s1", DH), ("o1", DH), ("s2", DH), ("o2", DH),
                     ("sm", DH), ("om", DH), ("bo1", DH), ("bo2", DH), ("bf2", DH), ("bf1", 8)):
            V[n] = vec[:, NV:NV + w]
            NV += w
        hb = sb("hb", [P, 4, H])
        gam_b = small[:, 0:D]
        bet_b = small[:, D:2 * D]

        names = """const_dma gate_dma seed fix ident_ready masks_ready gate_ready
            rawt_in raw_in stat_out stat_in mask_in mask_ready
            ct_hi ct_lo_v ct_lo_p cx_hi cx_lo
            bn_done aggr_done std_ready stat_t stat_row at_p at_ready a_half a_ready
            q_hi q_lo scores red neg_ready extra_exp exp_done sum_ready rinv_ready pb_ready
            tr p_hi p_lo pv o_low_ready o_ready o_t o_back
            w_in0 w_in1 w_split dk_in0 dk_in1 dk_ready prod_ready u_ready
            oh_hi oh_lo dv_ready m1 h1_hi h1_lo gelu_done m2 qe_act qe_dve y_done x_ready
            ln_pe ln_dve ln_act h_split small_in small_dve small_pe small_dma phase out_done
            w0_in w0_split w0_mask fix_v""".split()
        s = {n: sem(n) for n in names}

        W0_M = 0
        W0_S = 1024
        QT0 = 3072
        X0 = QT0 + 4 * NQ
        M2_0 = H
        M1_0 = 2 + H
        assert X0 + 4 * NQ <= RR
        LN_V = 12
        N_CONST = 20
        SUM0 = 3 * GT
        lb_d = io["lb_d"]
        pb_d = io["pb_d"]
        st_d = io["st_d"]

        block = ctx.enter_context(nc.Block())

        def f(v):
            return v.bitcast(F32)

        def wait_apart(eng, semaphore, value):
            value = value if isinstance(value, int) else eng.to_reg(value)
            eng.wait_ge(s["phase"], 4)
            eng.wait_ge(semaphore, value)

        def drain(eng, k):
            eng.drain().then_inc(s["phase"], 1)
            eng.wait_ge(s["phase"], 4 * k)

        A_BASE = {1: 0, 2: 32}
        O_BASE = {1: 16, 2: 48}
        O_BASE_I = {O_BASE[1]: 1, O_BASE[2]: 2}
        M_BASE = 64
        W1 = {("a", 1): ("wq1", "wk1"), ("a", 2): ("wq2", "wk2"), ("o", 1): ("wv1", "wo1"),
              ("o", 2): ("wv2", "wo2"), ("m", 0): ("fc1", "fc2")}
        SCALE = float(K) ** -0.5
        SCALE0 = float(HD0) ** -0.5

        def qo_tile(g):
            return qo[:, :, bass.ds(PAD + g * P, P)]

        def qo_head(h):
            v = qo[:, :, PAD:PAD + B * ROWS].rearrange("p e (b r) -> p e b r", b=B)
            return v[:, :, :, bass.ds(h * TQ, TQ)]

        @block.sync
        def _(sp):
            n_const = 0
            for name, dst in (("g0", V["g0"]), ("b0", V["b0"]), ("s1", V["s1"]), ("o1", V["o1"]),
                              ("s2", V["s2"]), ("o2", V["o2"]), ("sm", V["sm"]), ("om", V["om"]),
                              ("bo1", V["bo1"]), ("bo2", V["bo2"]), ("bf2", V["bf2"]), ("bf1", V["bf1"]),
                              ("bq1", hb[:, 0, :]), ("bv1", hb[:, 1, :]), ("bq2", hb[:, 2, :]),
                              ("bv2", hb[:, 3, :])):
                sp.dma_start(dst, io[name]).then_inc(s["const_dma"], 16)
                n_const += 1
            sp.dma_start(gate_t[:, 0:1], io["gate"].partition_broadcast(P)).then_inc(s["const_dma"], 16)
            sp.dma_start(gam_b[:, :], io["g0row"].partition_broadcast(P)).then_inc(s["const_dma"], 16)
            sp.dma_start(bet_b[:, :], io["b0row"].partition_broadcast(P)).then_inc(s["const_dma"], 16)
            sp.dma_start(xt[:, :, :], io["xt"].rearrange("(e p) q -> p e q", p=P)).then_inc(s["const_dma"], 16)
            assert n_const + 4 == N_CONST
            sp.dma_start(at(ar, 0, 2, D), io["wq0t"].rearrange("(e p) q -> p e q", p=P)).then_inc(s["w0_in"], 16)
            sp.dma_start(at(ar, 512, 2, D), io["wk0"].rearrange("(e p) q -> p e q", p=P)).then_inc(s["w0_in"], 16)

            def load_context(r, b, nxt):
                bc = r * B + nxt
                src = io["ctx_t"][bass.ds(b, 1), :, :].rearrange("o (e p) t -> p (o e) t", p=P)
                body = io["ctx"][bass.ds(b, 1), 0:(CH - 1) * P, :].rearrange("o (c p) d -> p (o c) d", p=P)
                tail = io["ctx"][bass.ds(b, 1), (CH - 1) * P:S, :].rearrange("o p d -> p o d")
                wait_apart(sp, s["ct_hi"], 3 * bc)
                wait_apart(sp, s["ct_lo_v"], 2 * bc)
                wait_apart(sp, s["ct_lo_p"], bc)
                sp.dma_start(raw_t[:, :, :], src).then_inc(s["rawt_in"], 16)
                wait_apart(sp, s["cx_hi"], 3 * bc)
                wait_apart(sp, s["cx_lo"], 3 * bc)
                sp.dma_start(raw[:, 0:CH - 1, :], body).then_inc(s["raw_in"], 16)
                sp.dma_start(raw[0:TAIL, CH - 1:CH, :], tail).then_inc(s["raw_in"], 16)

            def token_stats(b):
                wait_apart(sp, s["stat_row"], b + 1)
                sp.dma_start(st_d, mv_row[:, :]).then_inc(s["stat_out"], 16)
                wait_apart(sp, s["stat_out"], 16 * (b + 1))
                flat = st_d.rearrange("c p -> (c p)")
                wait_apart(sp, s["at_p"], 4 * b)
                sp.dma_start(mu_b, flat[0:S].partition_broadcast(P)).then_inc(s["stat_in"], 16)
                sp.dma_start(rs_b, flat[CH * P:CH * P + S].partition_broadcast(P)).then_inc(s["stat_in"], 16)

            def load_mask(b):
                src = io["mask"][bass.ds(b, 1), :].rearrange("o t -> (o t)").partition_broadcast(P)
                if not isinstance(b, int):
                    wait_apart(sp, s["mask_ready"], b)
                sp.dma_start(mask_u8[:, :], src)\
                    .then_inc(s["mask_in"], 16)

            sp.wait_ge(s["seed"], 1)
            load_context(0, 0, 0)
            sp.wait_ge(s["phase"], 8)
            load_mask(0)
            token_stats(0)
            with sp.Fori(0, B - 1) as b:
                load_mask(b + 1)
                load_context(0, b + 1, b + 1)
                token_stats(b + 1)

            def step_weights(kind, i, n, base, slot, fresh):
                first, second = W1[(kind, i)]
                w0 = io[first].rearrange("(e p) k -> p e k", p=P)[:, :, bass.ds(n * P, P)]
                w1 = io[second][bass.ds(n * P, P), :]
                if kind == "a":
                    rows = [io[f"{name}{i}"].rearrange("h k -> (h k)")[bass.ds(n * P, P)].partition_broadcast(P)
                            for name in ("biask", "bk")]
                if not fresh:
                    wait_apart(sp, s["w_split"], 2 * base + 2 * n - 2)
                    if kind == "a":
                        wait_apart(sp, s["prod_ready"], A_BASE[i] // 2 + n - 1)
                sp.dma_start(w_raw[:, slot, 0:D].rearrange("p (e k) -> p e k", e=DH), w0)\
                    .then_inc(s[f"w_in{slot}"], 16)
                sp.dma_start(w_raw[:, slot, D:2 * D], w1).then_inc(s[f"w_in{slot}"], 16)
                if kind == "a":
                    for c in (0, 1):
                        sp.dma_start(dk_raw[:, slot, c * P:(c + 1) * P], rows[c]).then_inc(s[f"dk_in{slot}"], 16)

            def weights(kind, i, steps, base):
                for n in (0, 1):
                    step_weights(kind, i, n, base, n, True)
                with sp.Fori(1, steps // 2) as m:
                    for slot in (0, 1):
                        step_weights(kind, i, 2 * m + slot, base, slot, False)

            load_context(1, 0, 0)
            sp.wait_ge(s["phase"], 12)
            sp.dma_start(at(ar, 0, 2, D), io["wv0t"].rearrange("(e p) q -> p e q", p=P)).then_inc(s["w0_in"], 16)
            sp.dma_start(at(ar, 512, 2, D), io["wo0t"].rearrange("(e p) q -> p e q", p=P)).then_inc(s["w0_in"], 16)
            sp.wait_ge(s["phase"], 16)
            for i in (1, 2):
                for n, name in enumerate((f"bq{i}h", f"biask{i}", f"bk{i}")):
                    sp.dma_start(cb[:, n * P:(n + 1) * P], io[name]).then_inc(s["small_in"], 16)
                weights("a", i, H, A_BASE[i])
                sp.wait_ge(s["small_dve"], 6 * (i - 1) + 2)
                sp.dma_start(lb_d.rearrange("(b h q) -> h b q", b=B, h=H),
                             lb_s[:, :].rearrange("h (b q) -> h b q", b=B)).then_inc(s["small_dma"], 16)
                sp.wait_ge(s["small_dma"], 96 * (i - 1) + 16)
                sp.dma_start(tiles_row[:, :], lb_d.rearrange("(g p) -> g p", p=P)).then_inc(s["small_dma"], 16)
                with sp.Fori(0, B - 1) as b:
                    load_context(i, b + 1, b + 1)
                if i == 1:
                    load_context(2, 0, 0)
                sp.wait_ge(s["phase"], 4 * (3 * i + 3))
                sp.wait_ge(s["small_dve"], 6 * (i - 1) + 4)
                sp.dma_start(pb_d.rearrange("(g p) -> g p", p=P), tiles_row[:, :]).then_inc(s["small_dma"], 16)
                sp.wait_ge(s["small_dma"], 96 * (i - 1) + 48)
                for p0 in (0, 32, 64):
                    sp.dma_start(pb_f[p0:p0 + H, :].rearrange("h (b q) -> h b q", b=B),
                                 pb_d.rearrange("(b h q) -> h b q", b=B, h=H)).then_inc(s["small_dma"], 16)
                    sp.dma_start(dv[p0:p0 + H, :], io[f"biasv{i}"]).then_inc(s["small_in"], 16)
                    sp.dma_start(dv2[p0:p0 + H, :], io[f"bv{i}h"]).then_inc(s["small_in"], 16)
                weights("o", i, H, O_BASE[i])
                sp.wait_ge(s["phase"], 4 * (3 * i + 4))
            weights("m", 0, F // P, M_BASE)
            sp.wait_ge(s["x_ready"], 8)
            sp.dma_start(io["out"].rearrange("(e p) q -> p e q", p=P), xt[:, :, :]).then_inc(s["out_done"], 16)
            sp.wait_ge(s["out_done"], 16)

        @block.gpsimd
        def _(pool):
            pool.memset(raw[:, CH - 1, :], 0.0).then_inc(s["seed"], 1)
            for t, v in ((ident[:, :], 0.0), (head_rows[:, :, 0], 1.0), (head_cols[:, :, :], 0.0),
                         (mean_w[:, :], 1.0 / D), (mhalf[:, :], -0.5), (o_row[:, :], 0.0), (mv[:, :, :], 1.0)):
                pool.memset(t, v).then_inc(s["fix"], 1)
            pool.wait_ge(s["fix"], 7)
            pool.affine_select(out=ident[:, :], in_=ident[:, :], compare_op=ALU.not_equal, fill=1.0,
                               base=0, pattern=[[-1, P]], channel_multiplier=1).then_inc(s["ident_ready"], 1)
            pool.affine_select(out=head_rows[:, :, 0], in_=head_rows[:, :, 0], compare_op=ALU.is_ge, fill=0.0,
                               base=0, pattern=[[-HD0, HPC]], channel_multiplier=1).then_inc(s["fix"], 1)
            pool.wait_ge(s["fix"], 8)
            pool.affine_select(out=head_rows[:, :, 0], in_=head_rows[:, :, 0], compare_op=ALU.is_ge, fill=0.0,
                               base=HD0 - 1, pattern=[[HD0, HPC]], channel_multiplier=-1).then_inc(s["fix"], 1)
            for m in range(HPC):
                pool.memset(head_cols[:, m, m * HD0:(m + 1) * HD0], 1.0).then_inc(s["fix"], 1)
            drain(pool, 1)

            def split0(base):
                pool.wait_ge(s["w0_in"], 32 * (base + 1))
                src = at(ar, 0, 4, D)
                hi = at(rr, W0_S, 4, 2 * D)[:, :, 0:D]
                lo = at(rr, W0_S, 4, 2 * D)[:, :, D:2 * D]
                pool.tensor_copy(hi, src).then_inc(s["w0_split"], 1)
                pool.wait_ge(s["w0_split"], 2 * base + 1)
                pool.tensor_tensor(lo, src, f(hi), ALU.subtract).then_inc(s["w0_split"], 1)
                pool.wait_ge(s["w0_split"], 2 * base + 2)

            split0(0)
            for jc in (0, 1):
                for n in range(HPC):
                    if 8 * jc + n >= 2:
                        pool.wait_ge(s["m2"], 8 * jc + n - 1)
                    pool.tensor_scalar(at(rr, W0_M + 512 * (n % 2), 512), f(at(rr, W0_S + 1024 + 512 * jc, 512)),
                                       head_rows[:, n, :], None, ALU.mult).then_inc(s["w0_mask"], 1)
            drain(pool, 2)

            def norm_context(b):
                wait_apart(pool, s["aggr_done"], b + 1)
                pool.tensor_scalar(mv[:, 1, :], mv[:, 1, :], EPS, None, ALU.add).then_inc(s["std_ready"], 1)
                pool.wait_ge(s["std_ready"], 2 * b + 1)
                pool.tensor_tensor(mv[:, 1, :], mv[:, 1, :], mhalf[:, :], ALU.pow).then_inc(s["std_ready"], 1)
                pool.wait_ge(s["stat_in"], 32 * (b + 1))
                pool.wait_ge(s["rawt_in"], 16 * (b + 1))
                for e in range(DH):
                    pool.tensor_tensor(raw_t[:, e, :], raw_t[:, e, :], mu_b, ALU.subtract).then_inc(s["at_p"], 1)
                for e in range(DH):
                    pool.wait_ge(s["at_p"], 4 * b + 1 + e)
                    pool.tensor_tensor(raw_t[:, e, :], raw_t[:, e, :], rs_b, ALU.mult).then_inc(s["at_p"], 1)

            def split_ct(r, b, g6):
                bc = r * B + b
                pool.wait_ge(s["ct_hi"], 3 * bc + 2)
                v = slice(SB, 2 * SB)
                pool.tensor_tensor(ct[:, 1, :, v], raw_t[:, :, v], f(ct[:, 0, :, v]), ALU.subtract)\
                    .then_inc(s["ct_lo_p"], 1)

            def split_cx(r, b):
                bc = r * B + b
                for k in range(3):
                    v = slice(GRP * k, GRP * (k + 1))
                    pool.wait_ge(s["cx_hi"], 3 * bc + k + 1)
                    pool.tensor_tensor(cx[:, v, D:2 * D], raw[:, v, :], f(cx[:, v, 0:D]), ALU.subtract)\
                        .then_inc(s["cx_lo"], 1)

            def run(r):
                if r == 0:
                    norm_context(0)
                split_ct(r, 0, None)
                split_cx(r, 0)
                with pool.Fori(0, B - 1) as b:
                    if r == 0:
                        norm_context(b + 1)
                    split_ct(r, b + 1, None)
                    split_cx(r, b + 1)

            def step_splits(kind, i, steps, base):
                def step(n, slot, first):
                    pool.wait_ge(s[f"w_in{slot}"], 16 * base + 16 * n + (32 if slot == 0 else 16))
                    if not first:
                        wait_apart(pool, s["m2"], M2_0 + base + n - 1)
                    pool.tensor_copy(w_s[:, 2 * slot, :], w_raw[:, slot, :]).then_inc(s["w_split"], 1)
                    pool.wait_ge(s["w_split"], 2 * base + 2 * n + 1)
                    pool.tensor_tensor(w_s[:, 2 * slot + 1, :], w_raw[:, slot, :], f(w_s[:, 2 * slot, :]),
                                       ALU.subtract).then_inc(s["w_split"], 1)
                    if kind == "a":
                        pool.wait_ge(s[f"dk_in{slot}"], 16 * A_BASE[i] // 2 + 16 * n + (32 if slot == 0 else 16))
                        if not first:
                            pool.wait_ge(s["prod_ready"], A_BASE[i] // 2 + n - 1)
                        pool.tensor_tensor(dk[:, slot, :], dk_raw[:, slot, 0:P], dk_raw[:, slot, P:2 * P],
                                           ALU.subtract).then_inc(s["dk_ready"], 1)
                for n in (0, 1):
                    step(n, n, True)
                with pool.Fori(1, steps // 2) as m:
                    for slot in (0, 1):
                        step(2 * m + slot, slot, False)

            run(0)
            drain(pool, 3)
            split0(1)
            for jc in (0, 1):
                for n in range(HPC):
                    if 8 * jc + n >= 2:
                        pool.wait_ge(s["m1"], M1_0 - 16 + 8 * jc + n - 1)
                    src = f(at(rr, W0_S, 4, D))[:, :, P * jc:P * (jc + 1)]
                    pool.tensor_tensor(at(rr, W0_M + 512 * (n % 2), 4, P), src,
                                       head_cols[:, n:n + 1, :].to_broadcast([P, 4, P]), ALU.mult)\
                        .then_inc(s["w0_mask"], 1)
            drain(pool, 4)
            for i in (1, 2):
                step_splits("a", i, H, A_BASE[i])
                drain(pool, 3 * i + 2)
                run(i)
                drain(pool, 3 * i + 3)
                step_splits("o", i, H, O_BASE[i])
                drain(pool, 3 * i + 4)
            step_splits("m", 0, F // P, M_BASE)
            drain(pool, 11)

        def three(eng, out, w_hi, w_lo, x_hi, x_lo, start, stop):
            eng.matmul(out, w_hi, x_hi, start=start, stop=False, skip_group_check=True)
            eng.matmul(out, w_hi, x_lo, start=False, stop=False, skip_group_check=True)
            return eng.matmul(out, w_lo, x_hi, start=False, stop=stop, skip_group_check=True)

        @block.tensor
        def _(pe):
            drain(pe, 1)
            wq = at(rr, W0_S, 2, 2 * D)
            xs = at(rr, X0, 2, DH * NQ)
            pe.wait_ge(s["w0_split"], 2)
            pe.wait_ge(s["h_split"], 2)
            for jc in range(2):
                for e in range(DH):
                    mm = three(pe, ps[:, jc, 0:NQ], wq[:, e, P * jc:P * jc + P], wq[:, e, D + P * jc:D + P * jc + P],
                               xs[:, 0, e * NQ:(e + 1) * NQ], xs[:, 1, e * NQ:(e + 1) * NQ], e == 0, e == DH - 1)
                mm.then_inc(s["m1"], 1)
            for h in range(H):
                jc = h // HPC
                q_s = at(rr, QT0, 2, 2 * NQ)
                wm = at(rr, W0_M + 512 * (h % 2), 512)
                pe.wait_ge(s["w0_mask"], h + 1)
                pe.wait_ge(s["h1_lo"], jc + 1)
                if h >= 2:
                    pe.wait_ge(s["qe_act"], h - 1)
                    pe.wait_ge(s["qe_dve"], h - 1)
                for e in range(DH):
                    mm = three(pe, ps[:, 2 + 2 * (h % 2) + e, 0:NQ], wm[:, e * P:e * P + P],
                               wm[:, D + e * P:D + e * P + P], q_s[:, 0, jc * NQ:(jc + 1) * NQ],
                               q_s[:, 1, jc * NQ:(jc + 1) * NQ], True, True)
                mm.then_inc(s["m2"], 1)
            drain(pe, 2)

            def scores(r, b, t, g, j):
                gg, bc = r * GT + g, r * B + b
                if j == 0:
                    pe.wait_ge(s["q_hi"], gg + 1)
                    pe.wait_ge(s["q_lo"], gg + 1)
                    if r == 0:
                        pe.wait_ge(s["red"], 3 * gg)
                    else:
                        pe.wait_ge(s["exp_done"], gg)
                if t == 0:
                    pe.wait_ge(s["ct_hi"], 3 * bc + j + 1)
                    if j == 1:
                        pe.wait_ge(s["ct_lo_p"], bc + 1)
                    else:
                        pe.wait_ge(s["ct_lo_v"], 2 * bc + 1 + j // 2)
                v = slice(SB * j, SB * (j + 1))
                q = QBUF[t]
                for e in range(DH):
                    mm = three(pe, ps[:, j, 0:SB], qt[:, 2 * q, e, :], qt[:, 2 * q + 1, e, :],
                               ct[:, 0, e, v], ct[:, 1, e, v], e == 0, e == DH - 1)
                mm.then_inc(s["scores"], 1)

            def transposes(r, g, k):
                gg = r * GT + g
                if k == 0:
                    pe.wait_ge(s["exp_done"], gg + 1)
                for c in range(GRP * k, GRP * (k + 1)):
                    mm = pe.transpose(ps[:, 3 + k, (c % GRP) * P:(c % GRP) * P + P], prob[:, c * P:(c + 1) * P],
                                      ident[:, :])
                mm.then_inc(s["tr"], 1)

            def turn_output(r, g):
                n = r * (GT + 1) + g + 1
                pe.wait_ge(s["o_ready"], n + 1)
                pe.wait_ge(s["o_back"], n + 1)
                for e in range(DH):
                    mm = pe.transpose(ps[:, 7, e * P:(e + 1) * P], o_row[:, e * P:(e + 1) * P], ident[:, :])
                mm.then_inc(s["o_t"], 1)

            def turn_stats(b, outputs):
                pe.wait_ge(s["std_ready"], 2 * b + 2)
                pe.wait_ge(s["o_back"], outputs + 1)
                pe.transpose(ps[0:2 * CH, 7, 256:256 + P], mv[:, :, :].rearrange("p a c -> p (a c)"), ident[:, :])\
                    .then_inc(s["stat_t"], 1)

            def weighted(r, b, t, g):
                gg, bc = r * GT + g, r * B + b
                pe.wait_ge(s["o_ready"], r * (GT + 1) + g + 1)
                for c in range(CH):
                    n = P if c < CH - 1 else TAIL
                    if c % GRP == 0:
                        pe.wait_ge(s["p_hi"], 3 * gg + c // GRP + 1)
                        pe.wait_ge(s["p_lo"], 3 * gg + c // GRP + 1)
                        if t == 0:
                            pe.wait_ge(s["cx_hi"], 3 * bc + c // GRP + 1)
                            pe.wait_ge(s["cx_lo"], 3 * bc + c // GRP + 1)
                    pe.matmul(ps[:, 6, :], pt[0:n, 0, c, :], cx[0:n, c, :], start=c == 0, stop=False,
                              skip_group_check=True)
                    mm = pe.matmul(ps[:, 6, 0:D], pt[0:n, 1, c, :], cx[0:n, c, 0:D], start=False,
                                   stop=c == CH - 1, skip_group_check=True)
                mm.then_inc(s["pv"], 1)

            def batch(r, b, last):
                for t in range(TILES):
                    g = TILES * b + t
                    nb, nt = (b, t + 1) if t < TILES - 1 else (b + 1, 0)
                    for k in range(3):
                        if not (last and t == TILES - 1):
                            scores(r, nb, nt, g + 1, k)
                        transposes(r, g, k)
                    if r == 0 and t == 4 and not last:
                        turn_stats(b + 1, r * (GT + 1) + g)
                    turn_output(r, g - 1)
                    weighted(r, b, t, g)

            def run(r):
                if r == 0:
                    turn_stats(0, 0)
                for j in range(3):
                    scores(r, 0, 0, 0, j)
                if r == 0:
                    pe.wait_ge(s["stat_row"], 1)
                with pe.Fori(0, B - 1) as b:
                    batch(r, b, False)
                batch(r, B - 1, True)
                turn_output(r, GT - 1)

            run(0)
            drain(pe, 3)
            pe.wait_ge(s["w0_split"], 4)
            for h in range(H):
                jc = h // HPC
                wm = at(rr, W0_M + 512 * (h % 2), 4, P)
                ohs = at(rr, X0, 2, DH * NQ)
                pe.wait_ge(s["w0_mask"], H + h + 1)
                pe.wait_ge(s["oh_hi"], h + 1)
                pe.wait_ge(s["oh_lo"], h + 1)
                for e in range(DH):
                    mm = three(pe, ps[:, jc, 0:NQ], wm[:, 2 * e, :], wm[:, 2 * e + 1, :],
                               ohs[:, 0, e * NQ:(e + 1) * NQ], ohs[:, 1, e * NQ:(e + 1) * NQ],
                               h % HPC == 0 and e == 0, h % HPC == HPC - 1 and e == DH - 1)
                mm.then_inc(s["m1"], 1)
            pe.wait_ge(s["h1_lo"], 4)
            wo = at(rr, W0_S + 1024, 2, 2 * D)
            o_s = at(rr, QT0, 2, 2 * NQ)
            for e in range(DH):
                for jc in (0, 1):
                    mm = three(pe, ps[:, 2 + e, 0:NQ], wo[:, jc, e * P:e * P + P], wo[:, jc, D + e * P:D + e * P + P],
                               o_s[:, 0, jc * NQ:(jc + 1) * NQ], o_s[:, 1, jc * NQ:(jc + 1) * NQ], jc == 0, jc == 1)
            mm.then_inc(s["y_done"], 1)
            drain(pe, 4)

            def norm(n):
                for e in range(DH):
                    mm = pe.matmul(ps[:, 0, 0:NQ], mean_w[:, :], xt[:, e, :], start=e == 0, stop=e == DH - 1)
                mm.then_inc(s["ln_pe"], 1)
                pe.wait_ge(s["ln_dve"], LN_V * n + 2)
                for e in range(DH):
                    mm = pe.matmul(ps[:, 1, 0:NQ], mean_w[:, :], sq[:, e, :], start=e == 0, stop=e == DH - 1)
                mm.then_inc(s["ln_pe"], 1)
                pe.wait_ge(s["h_split"], 2 + 2 * (n + 1))

            def first_product(kind, base, n, slot, fresh):
                pe.wait_ge(s["w_split"], 2 * base + 2 * n + 2)
                if not fresh:
                    pe.wait_ge(s["h1_lo"], 4 + base + n - 1)
                out = ps[:, slot, 0:NQ]
                w = w_s[:, 2 * slot:2 * slot + 2, 0:D]
                if kind == "o":
                    i = O_BASE_I[base]
                    pe.wait_ge(s["oh_hi"], H * i + n + 1)
                    pe.wait_ge(s["oh_lo"], H * i + n + 1)
                    x = oh[:, 2 * slot:2 * slot + 2, :]
                else:
                    x = hs[:, :, :, :].rearrange("p s e q -> p s (e q)")
                for e in range(DH):
                    mm = three(pe, out, w[:, 0, e * P:e * P + P], w[:, 1, e * P:e * P + P],
                               x[:, 0, e * NQ:(e + 1) * NQ], x[:, 1, e * NQ:(e + 1) * NQ], e == 0,
                               e == DH - 1 and kind != "o")
                if kind == "o":
                    pe.wait_ge(s["dv_ready"], H * (i - 1) + n + 1)
                    mm = pe.matmul(out, dv_m[0:80, slot, :], pb_s[:, :], start=False, stop=True, skip_group_check=True)
                mm.then_inc(s["m1"], 1)

            def second_product(kind, i, base, n, slot, first, last, fresh):
                pe.wait_ge(s["h1_lo"], 4 + base + n + 1)
                w = w_s[:, 2 * slot:2 * slot + 2, D:2 * D]
                if kind == "a" and not fresh:
                    pe.wait_ge(s["qe_act"], H * i + n - 1)
                    pe.wait_ge(s["qe_dve"], H * i + n - 1)
                for e in range(DH):
                    out = ps[:, 2 + 2 * slot + e, 0:NQ] if kind == "a" else ps[:, 6 + e, 0:NQ]
                    mm = three(pe, out, w[:, 0, e * P:e * P + P], w[:, 1, e * P:e * P + P], h1[:, 2 * slot, :],
                               h1[:, 2 * slot + 1, :], kind == "a" or first, kind == "a" or last)
                mm.then_inc(s["m2"], 1)

            def products(kind, i, steps, base):
                def pair(m, first, last):
                    for slot in (0, 1):
                        n = 2 * m + slot
                        if not (last and slot):
                            first_product(kind, base, n + 1, 1 - slot, first and slot == 0)
                        second_product(kind, i, base, n, slot, first and slot == 0, last and slot == 1, first)
                first_product(kind, base, 0, 0, True)
                pair(0, True, False)
                with pe.Fori(1, steps // 2 - 1) as m:
                    pair(m, False, False)
                pair(steps // 2 - 1, False, True)

            for i in (1, 2):
                norm(i - 1)
                products("a", i, H, A_BASE[i])
                pe.wait_ge(s["u_ready"], H * i)
                pe.wait_ge(s["qe_act"], H * i + H)
                pe.wait_ge(s["qe_dve"], H * i + H)
                for e in range(DH):
                    mm = pe.matmul(ps[0:H, 2, 0:NQ], u_k[:, e, :], ht[:, e, :], start=e == 0, stop=e == DH - 1)
                mm.then_inc(s["small_pe"], 1)
                pe.wait_ge(s["small_dma"], 96 * (i - 1) + 32)
                pe.transpose(ps[:, 3, 0:GT], tiles_row[:, :], ident[0:GT, 0:GT]).then_inc(s["small_pe"], 1)
                drain(pe, 3 * i + 2)
                run(i)
                drain(pe, 3 * i + 3)
                pe.transpose(ps[0:GT, 2, 0:P], pbq[:, :], ident[:, :]).then_inc(s["small_pe"], 1)
                pe.wait_ge(s["small_dve"], 6 * (i - 1) + 5)
                pe.wait_ge(s["small_dve"], 6 * (i - 1) + 6)
                products("o", i, H, O_BASE[i])
                drain(pe, 3 * i + 4)
            norm(2)
            products("m", 0, F // P, M_BASE)
            drain(pe, 11)

        @block.scalar
        def _(act):
            act.wait_ge(s["const_dma"], 16 * N_CONST)
            act.activation(gate_t[:, 1:2], gate_t[:, 0:1], ACT.Tanh).then_inc(s["o_back"], 1)
            drain(act, 1)
            act.activation(at(rr, X0, 2, DH * NQ)[:, 0, :], xt[:, :, :].rearrange("p e q -> p (e q)"), ACT.Copy)\
                .then_inc(s["h_split"], 1)
            for jc in (0, 1):
                act.wait_ge(s["m1"], jc + 1)
                act.activation(at(rr, QT0, 4, NQ)[:, jc, :], ps[:, jc, 0:NQ], ACT.Copy, scale=SCALE0)\
                    .then_inc(s["h1_hi"], 1)

            def q_back(h, bank, scale, done):
                dst = qo_head(h)[:, 0, :, :]
                wait_apart(act, s["m2"], done)
                act.activation(dst, ps[:, bank, 0:NQ].rearrange("p (b q) -> p b q", b=B), ACT.Copy, scale=scale)\
                    .then_inc(s["qe_act"], 1)

            for h in range(H):
                q_back(h, 2 + 2 * (h % 2), 1.0, h + 1)
            drain(act, 2)

            def split_ct(r, b):
                bc = r * B + b
                if r == 0:
                    act.wait_ge(s["at_ready"], 2 * bc + 2)
                else:
                    act.wait_ge(s["rawt_in"], 16 * (bc + 1))
                for j in range(3):
                    v = slice(SB * j, SB * (j + 1))
                    if not isinstance(b, int):
                        act.wait_ge(s["scores"], r * 3 * GT + 3 * TILES * b - 2 + j)
                    act.activation(ct[:, 0, :, v], raw_t[:, :, v], ACT.Copy).then_inc(s["ct_hi"], 1)

            def split_cx(r, b):
                bc = r * B + b
                if r:
                    act.wait_ge(s["raw_in"], 32 * (bc + 1))
                act.wait_ge(s["pv"], r * GT + TILES * b)
                for k in range(3):
                    if r == 0:
                        act.wait_ge(s["a_ready"], 3 * bc + k + 1)
                    v = slice(GRP * k, GRP * (k + 1))
                    act.activation(cx[:, v, 0:D], raw[:, v, :], ACT.Copy).then_inc(s["cx_hi"], 1)

            def split_q(r, t, g):
                src = qo_tile(g)
                if not isinstance(g, int) or g >= 2:
                    wait_apart(act, s["scores"], 3 * (r * GT + g - 1))
                act.activation(qt[:, 2 * QBUF[t], :, :], src, ACT.Copy).then_inc(s["q_hi"], 1)

            def softmax(r, g):
                gg = r * GT + g
                logit = lbq[:, bass.ds(g, 1)]
                act.wait_ge(s["rinv_ready"], gg)
                wait_apart(act, s["neg_ready"], gg + 1)
                if r:
                    act.activation(extra[:, :], logit, ACT.Exp, bias=negm[:, :])\
                        .then_inc(s["extra_exp"], 1)
                    act.wait_ge(s["tr"], 3 * gg)
                    src = ps[:, 0:3, 0:SB]
                else:
                    src = prob[:, 0:S].rearrange("p (j t) -> p j t", j=3)
                act.activation(prob[:, 0:S].rearrange("p (j t) -> p j t", j=3), src, ACT.Exp,
                               bias=negm[:, :], accum_out=rowsum[:, :]).then_inc(s["exp_done"], 1)

            def turn_output(r, g, stats_of=None):
                n = r * (GT + 1) + g + 1
                if stats_of is not None:
                    act.wait_ge(s["o_t"], n + 1)
                    turn_stats(stats_of)
                dst = qo_tile(g)
                wait_apart(act, s["o_t"], n + 1)
                act.activation(dst,
                               ps[:, 7, 0:D].rearrange("p (e r) -> p e r", e=DH), ACT.Copy).then_inc(s["o_back"], 1)

            def turn_stats(b):
                act.wait_ge(s["stat_t"], b + 1)
                act.wait_ge(s["stat_out"], 16 * b)
                act.activation(mv_row[:, :], ps[0:2 * CH, 7, 256:256 + P], ACT.Copy).then_inc(s["stat_row"], 1)

            def batch(r, b, last):
                for t in range(TILES):
                    g = TILES * b + t
                    gg = r * GT + g
                    for k in range(3):
                        act.wait_ge(s["tr"], 3 * gg + k + 1)
                        act.activation(pt[:, 0, GRP * k:GRP * (k + 1), :],
                                       ps[:, 3 + k, :].rearrange("p (c q) -> p c q", q=P), ACT.Copy)\
                            .then_inc(s["p_hi"], 1)
                    if not (last and t >= TILES - 2):
                        split_q(r, (t + 2) % TILES, g + 2)
                    turn_output(r, g - 1, b + 1 if r == 0 and t == 4 and not last else None)
                    if not (last and t == TILES - 1):
                        softmax(r, g + 1)
                    if t == 5 and not last:
                        split_ct(r, b + 1)
                    act.wait_ge(s["pv"], gg + 1)
                    act.wait_ge(s["rinv_ready"], gg + 1)
                    act.wait_ge(s["o_ready"], r * (GT + 1) + g + 1)
                    act.activation(o_low[:, :], ps[:, 6, D:2 * D], ACT.Copy, scale=rinv[:, :])\
                        .then_inc(s["o_low_ready"], 1)
                    if t == 6 and not last:
                        split_cx(r, b + 1)

            def run(r):
                split_q(r, 0, 0)
                split_q(r, 1, 1)
                if r == 0:
                    turn_stats(0)
                split_ct(r, 0)
                softmax(r, 0)
                split_cx(r, 0)
                with act.Fori(0, B - 1) as b:
                    batch(r, b, False)
                batch(r, B - 1, True)
                turn_output(r, GT - 1)

            def split_heads(i, n, slot, fresh):
                dst = at(rr, X0, 2, DH * NQ)[:, 0, :] if i == 0 else oh[:, 2 * slot, :]
                src = qo_head(n)
                if not fresh:
                    wait_apart(act, s["m1"], (2 if i == 0 else M1_0 + O_BASE[i]) + n - (0 if i == 0 else 1))
                act.activation(dst.rearrange("p (e b q) -> p e b q", e=DH, b=B), src, ACT.Copy)\
                    .then_inc(s["oh_hi"], 1)

            run(0)
            drain(act, 3)
            for h in range(H):
                split_heads(0, h, 0, h == 0)
            for jc in (0, 1):
                act.wait_ge(s["m1"], 2 + HPC * (jc + 1))
                act.activation(at(rr, QT0, 4, NQ)[:, jc, :], ps[:, jc, 0:NQ], ACT.Copy).then_inc(s["h1_hi"], 1)
            drain(act, 4)

            def norm(n):
                act.wait_ge(s["ln_dve"], LN_V * n + 3)
                act.activation(dev, var, ACT.Sqrt).then_inc(s["ln_act"], 1)
                act.wait_ge(s["ln_dve"], LN_V * n + 12)
                act.activation(hs[:, 0, :, :], ht, ACT.Copy).then_inc(s["h_split"], 1)

            def first_split(kind, i, base, n, slot, fresh):
                src = ps[:, slot, 0:NQ]
                if kind == "m":
                    if not fresh:
                        act.wait_ge(s["h1_lo"], 4 + base + n - 1)
                    col = V["bf1"][:, bass.ds(n, 1)]
                    wait_apart(act, s["m1"], M1_0 + base + n + 1)
                    act.activation(g32[:, slot, :], src, ACT.Gelu, bias=col)\
                        .then_inc(s["h1_hi"], 1)
                else:
                    if not fresh:
                        act.wait_ge(s["m2"], M2_0 + base + n - 1)
                    col = hb[:, 2 * (i - 1) + (kind == "o"), bass.ds(n, 1)]
                    wait_apart(act, s["m1"], M1_0 + base + n + 1)
                    act.activation(h1[:, 2 * slot, :], src, ACT.Identity, bias=col).then_inc(s["h1_hi"], 1)

            def products(kind, i, steps, base):
                def pair(m, first, last):
                    for slot in (0, 1):
                        n = 2 * m + slot
                        if kind == "o" and not last:
                            split_heads(i, n + 2, slot, False)
                        if not (last and slot):
                            first_split(kind, i, base, n + 1, 1 - slot, first and slot == 0)
                        if kind == "a":
                            q_back(n, 2 + 2 * slot, SCALE, M2_0 + base + n + 1)
                if kind == "o":
                    split_heads(i, 0, 0, True)
                    split_heads(i, 1, 1, True)
                first_split(kind, i, base, 0, 0, True)
                pair(0, True, False)
                with act.Fori(1, steps // 2 - 1) as m:
                    pair(m, False, False)
                pair(steps // 2 - 1, False, True)

            for i in (1, 2):
                norm(i - 1)
                products("a", i, H, A_BASE[i])
                drain(act, 3 * i + 2)
                run(i)
                drain(act, 3 * i + 3)
                products("o", i, H, O_BASE[i])
                drain(act, 3 * i + 4)
            norm(2)
            products("m", 0, F // P, M_BASE)
            drain(act, 11)

        @block.vector
        def _(dve):
            drain(dve, 1)
            for p0 in (0, 32, 64):
                dve.tensor_copy(hsel[p0:p0 + 32, :], ident[p0:p0 + 32, p0:p0 + H])
            x_s = at(rr, X0, 2, DH * NQ)
            dve.wait_ge(s["h_split"], 1)
            dve.tensor_tensor(x_s[:, 1, :], xt[:, :, :].rearrange("p e q -> p (e q)"), f(x_s[:, 0, :]), ALU.subtract)\
                .then_inc(s["h_split"], 1)
            q_s = at(rr, QT0, 4, NQ)
            for jc in (0, 1):
                dve.wait_ge(s["h1_hi"], jc + 1)
                dve.scalar_tensor_tensor(out=q_s[:, 2 + jc, :], in0=ps[:, jc, 0:NQ], scalar=SCALE0,
                                         in1=f(q_s[:, jc, :]), op0=ALU.mult, op1=ALU.subtract)\
                    .then_inc(s["h1_lo"], 1)

            def q_back(h, bank, scale):
                dve.tensor_scalar(qo_head(h)[:, 1, :, :], ps[:, bank, 0:NQ].rearrange("p (b q) -> p b q", b=B),
                                  scale, None, ALU.mult).then_inc(s["qe_dve"], 1)

            for h in range(H):
                dve.wait_ge(s["m2"], h + 1)
                q_back(h, 3 + 2 * (h % 2), 1.0)
            drain(dve, 2)

            def load_stats(b, c0, c1):
                if c0 == 0:
                    dve.wait_ge(s["raw_in"], 32 * (b + 1))
                    dve.wait_ge(s["stat_t"], b)
                for c in range(c0, c1):
                    ins = dve.bn_stats(bn[:, c, :], raw[:, c, :])
                if c1 == CH:
                    ins.then_inc(s["bn_done"], 1)
                    wait_apart(dve, s["bn_done"], b + 1)
                    for c in range(CH):
                        ins = dve.bn_aggr(mv[:, :, c], bn[:, c, :])
                    ins.then_inc(s["aggr_done"], 1)

            def norm_tokens(b, k):
                if k == 0:
                    dve.wait_ge(s["std_ready"], 2 * b + 2)
                for c in range(GRP * k, GRP * (k + 1)):
                    ins = dve.scalar_tensor_tensor(out=raw[:, c, :], in0=raw[:, c, :], scalar=mv[:, 0, c:c + 1],
                                                   in1=gam_b[:, :], op0=ALU.subtract, op1=ALU.mult)
                ins.then_inc(s["a_half"], 1)
                dve.wait_ge(s["a_half"], 3 * b + k + 1)
                for c in range(GRP * k, GRP * (k + 1)):
                    ins = dve.scalar_tensor_tensor(out=raw[:, c, :], in0=raw[:, c, :], scalar=mv[:, 1, c:c + 1],
                                                   in1=bet_b[:, :], op0=ALU.mult, op1=ALU.add)
                ins.then_inc(s["a_ready"], 1)

            def norm_transposed(b):
                for e in range(DH):
                    dve.wait_ge(s["at_p"], 4 * b + 3 + e)
                    dve.tensor_scalar(raw_t[:, e, :], raw_t[:, e, :], V["g0"][:, e:e + 1], V["b0"][:, e:e + 1],
                                      ALU.mult, ALU.add).then_inc(s["at_ready"], 1)

            def mask_bias(b):
                dve.wait_ge(s["mask_in"], 16 * (b + 1))
                dve.tensor_scalar(mask_b, mask_u8[:, :], -1.0, 3e38, ALU.add, ALU.mult).then_inc(s["mask_ready"], 1)
                dve.wait_ge(s["mask_ready"], b + 1)

            def split_ct(r, b):
                bc = r * B + b
                for j in (0, 2):
                    v = slice(SB * j, SB * (j + 1))
                    dve.wait_ge(s["ct_hi"], 3 * bc + j + 1)
                    dve.tensor_tensor(ct[:, 1, :, v], raw_t[:, :, v], f(ct[:, 0, :, v]), ALU.subtract)\
                        .then_inc(s["ct_lo_v"], 1)

            def split_q(r, t, g):
                gg = r * GT + g
                dve.wait_ge(s["q_hi"], gg + 1)
                q = QBUF[t]
                dve.tensor_tensor(qt[:, 2 * q + 1, :, :], qo_tile(g), f(qt[:, 2 * q, :, :]), ALU.subtract)\
                    .then_inc(s["q_lo"], 1)

            def row_max(r, g, j):
                gg = r * GT + g
                dve.wait_ge(s["scores"], 3 * gg + j + 1)
                if r == 0:
                    v = prob[:, SB * j:SB * (j + 1)]
                    if not isinstance(g, int) or g:
                        dve.wait_ge(s["tr"], 3 * gg - 2 + j)
                    dve.tensor_tensor(v, ps[:, j, 0:SB], mask_b[:, SB * j:SB * (j + 1)], ALU.add)\
                        .then_inc(s["red"], 1)
                    dve.wait_ge(s["red"], 3 * gg + j + 1)
                    dve.tensor_reduce(mx4[:, j:j + 1], v, AX.X, ALU.max).then_inc(s["sum_ready"], 1)
                else:
                    dve.tensor_reduce(mx4[:, j:j + 1], ps[:, j, 0:SB], AX.X, ALU.max).then_inc(s["red"], 1)

            def neg_max(r, g):
                gg = r * GT + g
                n = 3
                if r == 0:
                    dve.wait_ge(s["sum_ready"], 3 * gg + 3)
                else:
                    n = 4
                    dve.tensor_copy(mx4[:, 3:4], lbq[:, bass.ds(g, 1)]).then_inc(s["sum_ready"], 1)
                    dve.wait_ge(s["sum_ready"], SUM0 + 2 * (gg - GT) + 1)
                    dve.wait_ge(s["red"], 3 * gg + 3)
                dve.tensor_reduce(negm[:, :], mx4[:, 0:n], AX.X, ALU.max, negate=True).then_inc(s["neg_ready"], 1)

            def sums(r, g):
                gg = r * GT + g
                dve.wait_ge(s["exp_done"], gg + 1)
                dve.wait_ge(s["o_ready"], r * (GT + 1) + g + 1)
                if r == 0:
                    dve.reciprocal(rinv[:, :], rowsum[:, :]).then_inc(s["rinv_ready"], 1)
                else:
                    dve.tensor_tensor(total[:, :], rowsum[:, :], extra[:, :], ALU.add).then_inc(s["sum_ready"], 1)
                    dve.wait_ge(s["sum_ready"], SUM0 + 2 * (gg - GT) + 2)
                    dve.reciprocal(rinv[:, :], total[:, :]).then_inc(s["pb_ready"], 1)
                    dve.wait_ge(s["pb_ready"], gg - GT + 1)
                    dve.tensor_tensor(pbq[:, bass.ds(g, 1)], extra[:, :], rinv[:, :], ALU.mult)\
                        .then_inc(s["rinv_ready"], 1)

            def low_probs(r, g, k):
                gg = r * GT + g
                dve.wait_ge(s["p_hi"], 3 * gg + k + 1)
                v = slice(GRP * k, GRP * (k + 1))
                dve.tensor_tensor(pt[:, 1, v, :], ps[:, 3 + k, :].rearrange("p (c q) -> p c q", q=P),
                                  f(pt[:, 0, v, :]), ALU.subtract).then_inc(s["p_lo"], 1)

            def batch(r, b, last):
                for t in range(TILES):
                    g = TILES * b + t
                    gg = r * GT + g
                    end = last and t == TILES - 1
                    if r == 0 and t == TILES - 1 and not last:
                        mask_bias(b + 1)
                    for k in range(3):
                        if not end:
                            row_max(r, g + 1, k)
                        if k == 2 and not end:
                            neg_max(r, g + 1)
                        low_probs(r, g, k)
                    if not (last and t >= TILES - 2):
                        split_q(r, (t + 2) % TILES, g + 2)
                    if r == 0 and not last:
                        if 1 <= t <= 3:
                            load_stats(b + 1, GRP * (t - 1), GRP * t)
                        if t == 5:
                            norm_transposed(b + 1)
                    if t == 5 and not last:
                        split_ct(r, b + 1)
                    dve.wait_ge(s["o_low_ready"], gg + 1)
                    dve.wait_ge(s["rinv_ready"], gg + 1)
                    dve.wait_ge(s["o_t"], r * (GT + 1) + g + 1)
                    dve.scalar_tensor_tensor(out=o_row[:, :], in0=ps[:, 6, 0:D], scalar=rinv[:, :], in1=o_low[:, :],
                                             op0=ALU.mult, op1=ALU.add).then_inc(s["o_ready"], 1)
                    if not end:
                        sums(r, g + 1)
                    if r == 0 and not last and t >= 4:
                        norm_tokens(b + 1, t - 4)

            def run(r):
                dve.memset(prob[:, S:CH * P], 0.0)
                dve.memset(o_row[:, :], 0.0).then_inc(s["o_ready"], 1)
                split_q(r, 0, 0)
                split_q(r, 1, 1)
                if r == 0:
                    load_stats(0, 0, CH)
                    norm_transposed(0)
                    for k in range(3):
                        norm_tokens(0, k)
                    mask_bias(0)
                split_ct(r, 0)
                for k in range(3):
                    row_max(r, 0, k)
                neg_max(r, 0)
                sums(r, 0)
                with dve.Fori(0, B - 1) as b:
                    batch(r, b, False)
                batch(r, B - 1, True)

            def split_heads(i, n, slot):
                dve.wait_ge(s["oh_hi"], H * i + n + 1)
                v = at(rr, X0, 2, DH * NQ)[:, 0:2, :] if i == 0 else oh[:, 2 * slot:2 * slot + 2, :]
                v = v.rearrange("p s (e b q) -> p s e b q", e=DH, b=B)
                for e in range(DH):
                    ins = dve.tensor_tensor(v[:, 1, e, :, :], qo_head(n)[:, e, :, :], f(v[:, 0, e, :, :]), ALU.subtract)
                ins.then_inc(s["oh_lo"], 1)

            run(0)
            drain(dve, 3)
            for h in range(H):
                split_heads(0, h, 0)
            for jc in (0, 1):
                dve.wait_ge(s["h1_hi"], 2 + jc + 1)
                dve.tensor_tensor(q_s[:, 2 + jc, :], ps[:, jc, 0:NQ], f(q_s[:, jc, :]), ALU.subtract)\
                    .then_inc(s["h1_lo"], 1)
            dve.wait_ge(s["y_done"], 1)
            for e in range(DH):
                dve.scalar_tensor_tensor(out=xt[:, e, :], in0=ps[:, 2 + e, 0:NQ], scalar=gate_t[:, 1:2],
                                         in1=xt[:, e, :], op0=ALU.mult, op1=ALU.add).then_inc(s["x_ready"], 1)
            drain(dve, 4)

            def norm(n, scale, offset):
                k = [LN_V * n]

                def link(ins):
                    k[0] += 1
                    ins.then_inc(s["ln_dve"], 1)

                def settled():
                    dve.wait_ge(s["ln_dve"], k[0])
                dve.wait_ge(s["ln_pe"], 2 * n + 1)
                dve.tensor_tensor(xc, xt[:, :, :], ps[:, 0:1, 0:NQ].to_broadcast([P, DH, NQ]), ALU.subtract)\
                    .then_inc(s["ln_dve"], 1)
                k[0] += 1
                settled()
                link(dve.tensor_tensor(sq, xc, xc, ALU.mult))
                dve.wait_ge(s["ln_pe"], 2 * n + 2)
                link(dve.tensor_scalar(var, ps[:, 1, 0:NQ], EPS, None, ALU.add))
                dve.wait_ge(s["ln_act"], n + 1)
                link(dve.reciprocal(dev, dev))
                settled()
                link(dve.tensor_tensor(tmp, dev, dev, ALU.mult))
                settled()
                link(dve.tensor_tensor(tmp, tmp, var, ALU.mult))
                settled()
                link(dve.tensor_scalar(tmp, tmp, -0.5, 1.5, ALU.mult, ALU.add))
                settled()
                link(dve.tensor_tensor(dev, dev, tmp, ALU.mult))
                settled()
                for e in range(DH):
                    link(dve.tensor_tensor(ht[:, e, :], xc[:, e, :], dev, ALU.mult))
                settled()
                for e in range(DH):
                    link(dve.tensor_scalar(ht[:, e, :], ht[:, e, :], scale[:, e:e + 1], offset[:, e:e + 1],
                                           ALU.mult, ALU.add))
                assert k[0] == LN_V * (n + 1)
                dve.wait_ge(s["h_split"], 2 + 2 * n + 1)
                dve.tensor_tensor(hs[:, 1, :, :], ht, f(hs[:, 0, :, :]), ALU.subtract).then_inc(s["h_split"], 1)

            def first_split(kind, i, base, n, slot, fresh):
                dve.wait_ge(s["h1_hi"], 4 + base + n + 1)
                if kind == "m":
                    if not fresh:
                        dve.wait_ge(s["m2"], M2_0 + base + n - 1)
                    dve.tensor_copy(h1[:, 2 * slot, :], g32[:, slot, :]).then_inc(s["gelu_done"], 1)
                    dve.wait_ge(s["gelu_done"], n + 1)
                    dve.tensor_tensor(h1[:, 2 * slot + 1, :], g32[:, slot, :], f(h1[:, 2 * slot, :]), ALU.subtract)\
                        .then_inc(s["h1_lo"], 1)
                else:
                    col = hb[:, 2 * (i - 1) + (kind == "o"), bass.ds(n, 1)]
                    dve.scalar_tensor_tensor(out=h1[:, 2 * slot + 1, :], in0=ps[:, slot, 0:NQ], scalar=col,
                                             in1=f(h1[:, 2 * slot, :]), op0=ALU.add, op1=ALU.subtract)\
                        .then_inc(s["h1_lo"], 1)

            def extra_key(i, n, slot):
                j = A_BASE[i] // 2 + n
                dve.wait_ge(s["dk_ready"], j + 1)
                if not isinstance(j, int) or j:
                    dve.wait_ge(s["u_ready"], j)
                dve.tensor_tensor(dk_prod, w_raw[:, slot, 0:D].rearrange("p (e k) -> p e k", e=DH),
                                  dk[:, slot:slot + 1, :].to_broadcast([P, DH, P]), ALU.mult).then_inc(s["prod_ready"], 1)
                dve.wait_ge(s["prod_ready"], j + 1)
                dve.tensor_reduce(u_k[:, :, bass.ds(n, 1)], dk_prod, AX.X, ALU.add).then_inc(s["u_ready"], 1)

            def extra_value(i, n, slot, fresh):
                if not fresh:
                    dve.wait_ge(s["m1"], M1_0 + O_BASE[i] + n - 1)
                dve.tensor_scalar(dv_m[0:80, slot, :], dvr[:, :], hsel[0:80, bass.ds(n, 1)], None, ALU.mult)\
                    .then_inc(s["dv_ready"], 1)

            def products(kind, i, steps, base):
                def pair(m, first, last):
                    for slot in (0, 1):
                        n = 2 * m + slot
                        if kind == "o" and not last:
                            split_heads(i, n + 2, slot)
                            extra_value(i, n + 2, slot, False)
                        if not (last and slot):
                            first_split(kind, i, base, n + 1, 1 - slot, first and slot == 0)
                        if kind == "a":
                            dve.wait_ge(s["m2"], M2_0 + base + n + 1)
                            q_back(n, 3 + 2 * slot, SCALE)
                            extra_key(i, n, slot)
                if kind == "o":
                    for n in (0, 1):
                        split_heads(i, n, n)
                        extra_value(i, n, n, True)
                first_split(kind, i, base, 0, 0, True)
                pair(0, True, False)
                with dve.Fori(1, steps // 2 - 1) as m:
                    pair(m, False, False)
                pair(steps // 2 - 1, False, True)

            def add_output(bias, base, steps):
                dve.wait_ge(s["m2"], M2_0 + base + steps)
                for e in range(DH):
                    dve.scalar_tensor_tensor(out=xt[:, e, :], in0=ps[:, 6 + e, 0:NQ], scalar=bias[:, e:e + 1],
                                             in1=xt[:, e, :], op0=ALU.add, op1=ALU.add).then_inc(s["x_ready"], 1)

            for i in (1, 2):
                norm(i - 1, V[f"s{i}"], V[f"o{i}"])
                products("a", i, H, A_BASE[i])
                sd = 6 * (i - 1)
                dve.wait_ge(s["small_in"], 144 * (i - 1) + 48)
                dve.tensor_tensor(cb[:, 3 * P:4 * P], cb[:, P:2 * P], cb[:, 2 * P:3 * P], ALU.subtract)\
                    .then_inc(s["fix_v"], 1)
                dve.wait_ge(s["fix_v"], 9 * (i - 1) + 1)
                dve.tensor_tensor(cb[:, 3 * P:4 * P], cb[:, 3 * P:4 * P], cb[:, 0:P], ALU.mult).then_inc(s["fix_v"], 1)
                dve.wait_ge(s["fix_v"], 9 * (i - 1) + 2)
                dve.tensor_reduce(cbv[:, :], cb[:, 3 * P:4 * P], AX.X, ALU.add).then_inc(s["small_dve"], 1)
                dve.wait_ge(s["small_dve"], sd + 1)
                dve.wait_ge(s["small_pe"], 3 * (i - 1) + 1)
                dve.tensor_scalar(lb_s[:, :], ps[0:H, 2, 0:NQ], cbv[:, :], SCALE, ALU.add, ALU.mult)\
                    .then_inc(s["small_dve"], 1)
                dve.wait_ge(s["small_pe"], 3 * (i - 1) + 2)
                dve.tensor_copy(lbq[:, :], ps[:, 3, 0:GT]).then_inc(s["small_dve"], 1)
                dve.wait_ge(s["small_dve"], sd + 3)
                drain(dve, 3 * i + 2)
                run(i)
                drain(dve, 3 * i + 3)
                for v in (dv, dv2, pb_f):
                    dve.memset(v, 0.0).then_inc(s["fix_v"], 1)
                dve.wait_ge(s["fix_v"], 9 * (i - 1) + 5)
                dve.wait_ge(s["small_pe"], 3 * (i - 1) + 3)
                dve.tensor_copy(tiles_row[:, :], ps[0:GT, 2, 0:P]).then_inc(s["small_dve"], 1)
                dve.wait_ge(s["small_in"], 144 * i)
                dve.wait_ge(s["small_dma"], 96 * i)
                dve.tensor_copy(pb_s[:, :], pb_f).then_inc(s["fix_v"], 1)
                dve.tensor_tensor(dv2, dv, dv2, ALU.subtract).then_inc(s["fix_v"], 1)
                dve.wait_ge(s["fix_v"], 9 * (i - 1) + 7)
                dve.tensor_tensor(pb_s[32:64, :], pb_f[32:64, :], f(pb_s[32:64, :]), ALU.subtract)\
                    .then_inc(s["small_dve"], 1)
                dve.tensor_copy(dv_hi[:, :], dv2).then_inc(s["fix_v"], 1)
                dve.wait_ge(s["fix_v"], 9 * (i - 1) + 8)
                dve.tensor_copy(dvr[0:64, :], f(dv_hi[0:64, :]))
                dve.tensor_tensor(dvr[64:80, :], dv2[64:80, :], f(dv_hi[64:80, :]), ALU.subtract)\
                    .then_inc(s["fix_v"], 1)
                dve.wait_ge(s["fix_v"], 9 * (i - 1) + 9)
                dve.tensor_copy(tmp16[:, :], cbv[:, :]).then_inc(s["small_dve"], 1)
                products("o", i, H, O_BASE[i])
                add_output(V[f"bo{i}"], O_BASE[i], H)
                drain(dve, 3 * i + 4)
            norm(2, V["sm"], V["om"])
            products("m", 0, F // P, M_BASE)
            add_output(V["bf2"], M_BASE, F // P)
            drain(dve, 11)


def kernel(**inputs):
    import numpy as np
    import concourse.bacc as bacc
    from concourse.bass_utils import run_bass_kernel_spmd

    x = {k: np.asarray(v) for k, v in inputs.items()}
    l0, l1 = "L0_xattn_", "L1_xattn_"

    def cols(a, n):
        return np.ascontiguousarray(a.reshape(n, -1).T)

    ctx = x["ctx_2048"]
    arrays = {
        "xt": np.ascontiguousarray(x["x"].reshape(NQ, D).T),
        "ctx": np.ascontiguousarray(ctx),
        "ctx_t": np.ascontiguousarray(ctx.transpose(0, 2, 1)),
        "mask": np.ascontiguousarray(x["mask_BxS2_bf1"]).view(np.uint8),
        "gate": x[l0 + "gate"].reshape(1),
        "wq0t": np.ascontiguousarray(x[l0 + "Wq"].T),
        "wk0": np.ascontiguousarray(x[l0 + "Wk"]),
        "wv0t": np.ascontiguousarray(x[l0 + "Wv"].T),
        "wo0t": np.ascontiguousarray(x[l0 + "Wo"].T),
        "g0row": x[l0 + "ln_gamma"], "b0row": x[l0 + "ln_beta"],
        "g0": cols(x[l0 + "ln_gamma"], 2), "b0": cols(x[l0 + "ln_beta"], 2),
        "sm": cols(x[l1 + "ln_mlp_scale"], 2), "om": cols(x[l1 + "ln_mlp_offset"], 2),
        "fc1": np.ascontiguousarray(x[l1 + "w_fc1"]), "fc2": np.ascontiguousarray(x[l1 + "w_fc2"]),
        "bf1": cols(x[l1 + "b_fc1"], 8), "bf2": cols(x[l1 + "b_fc2"], 2),
    }
    for i in (1, 2):
        arrays.update({
            f"s{i}": cols(x[f"{l1}ln{i}_scale"], 2), f"o{i}": cols(x[f"{l1}ln{i}_offset"], 2),
            f"wq{i}": np.ascontiguousarray(x[f"{l1}wq{i}"]),
            f"wk{i}": np.ascontiguousarray(x[f"{l1}wk{i}"].T),
            f"wv{i}": np.ascontiguousarray(x[f"{l1}wv{i}"]),
            f"wo{i}": np.ascontiguousarray(x[f"{l1}wo{i}"]),
            f"bq{i}": cols(x[f"{l1}bq{i}"], H), f"bv{i}": cols(x[f"{l1}bv{i}"], H),
            f"bq{i}h": x[f"{l1}bq{i}"].reshape(H, K), f"bv{i}h": x[f"{l1}bv{i}"].reshape(H, K),
            f"bk{i}": x[f"{l1}bk{i}"].reshape(H, K),
            f"biask{i}": x[f"{l1}bias_k{i}"].reshape(H, K), f"biasv{i}": x[f"{l1}bias_v{i}"].reshape(H, K),
            f"bo{i}": cols(x[f"{l1}bo{i}"], 2),
        })
    nc = bacc.Bacc("TRN2", target_bir_lowering=False, num_devices=1)
    io = {}
    for name, a in arrays.items():
        io[name] = nc.dram_tensor(f"in_{name}", a.shape, mybir.dt.from_np(a.dtype), kind="ExternalInput").ap()
    io["out"] = nc.dram_tensor("out_yt", (D, NQ), F32, kind="ExternalOutput").ap()
    io["lb_d"] = nc.dram_tensor("lb_scratch", (B * ROWS,), F32).ap()
    io["pb_d"] = nc.dram_tensor("pb_scratch", (B * ROWS,), F32).ap()
    io["st_d"] = nc.dram_tensor("stat_scratch", (2 * CH, P), F32).ap()
    build(nc, io)
    r = run_bass_kernel_spmd(nc, [{f"in_{n}": a for n, a in arrays.items()}], core_ids=[0])
    return np.ascontiguousarray(r.results[0]["out_yt"].T).reshape(B, TQ, D)
```

```python
from contextlib import ExitStack

import concourse.bass as bass
from concourse import mybir

F32 = mybir.dt.float32
F32R = mybir.dt.float32r
U8 = mybir.dt.uint8
ALU = mybir.AluOpType
ACT = mybir.ActivationFunctionType
AX = mybir.AxisListType

P = 128
B = 8
TQ = 56
D = 256
DH = D // P
S = 1500
H = 16
HD0 = D // H
K = 128
NQ = B * TQ
ROWS = H * TQ
TILES = ROWS // P
GT = B * TILES
CH = -(-S // P)
TAIL = S - (CH - 1) * P
SB = S // 3
GRP = CH // 3
F = 1024
EPS = 1e-5
NS = 4
PAD = P
QBUF = [t % 2 if t < TILES - 1 else 2 for t in range(TILES)]
HPC = P // HD0


def build(nc, io):
    with ExitStack() as ctx:
        def sb(name, shape, dt=F32):
            return ctx.enter_context(nc.sbuf_tensor(name, shape, dt))

        def sem(name):
            return ctx.enter_context(nc.semaphore(name))

        ps = ctx.enter_context(nc.psum_tensor("ps", [P, 8, 512], F32))

        qo = sb("qo", [P, DH, PAD + B * ROWS])
        xt = sb("xt", [P, DH, NQ])
        raw_t = sb("raw_t", [P, DH, S])
        raw = sb("raw", [P, CH, D])
        ct = sb("ct", [P, 2, DH, S], F32R)
        cx = sb("cx", [P, CH, 2 * D], F32R)
        ident = sb("ident", [P, P])
        mean_w = sb("mean_w", [P, P])
        head_rows = sb("head_rows", [P, HPC, 1])
        spare = sb("spare", [P, NS, 2 * P])
        vec = sb("vec", [P, 64])
        gate_t = sb("gate_t", [P, 2])
        AR = 6144
        ar = sb("ar", [P, AR])
        RR = 7936
        rr = sb("rr", [P, RR], F32R)
        mx4 = sb("mx4", [P, 4])
        negm = sb("negm", [P, 1])
        rowsum = sb("rowsum", [P, 1])
        extra = sb("extra", [P, 1])
        total = sb("total", [P, 1])
        rinv = sb("rinv", [P, 1])
        lbq = sb("lbq", [P, GT])
        pbq = sb("pbq", [P, GT])
        o_low = sb("o_low", [P, D])
        o_row = sb("o_row", [P, D])
        bn = sb("bn", [P, CH, 6])
        mv = sb("mv", [P, 2, CH])
        mv_row = sb("mv_row", [CH, P])
        wsum = sb("wsum", [P, 2])
        bias0 = sb("bias0", [P, 2])
        mhalf = sb("mhalf", [P, CH])

        def at(t, off, *shape):
            n = 1
            for s in shape:
                n *= s
            v = t[:, off:off + n]
            if len(shape) == 2:
                v = v.rearrange("p (a b) -> p a b", b=shape[1])
            if len(shape) == 3:
                v = v.rearrange("p (a b c) -> p a b c", b=shape[1], c=shape[2])
            return v

        prob = at(ar, 0, CH * P)
        mask_b = at(ar, 1536, S)
        rs_b = at(ar, 1536 + 1500, S)
        pt = at(rr, 0, 2, CH, P)
        qt = at(rr, 2 * CH * P, 6, DH, P)
        w0 = at(ar, 4536, 6, D)
        xc = at(ar, 0, DH, NQ)
        sq = at(ar, 896, DH, NQ)
        var = at(ar, 1792, NQ)
        dev = at(ar, 2240, NQ)
        tmp = at(ar, 2688, NQ)
        ht = at(ar, 3136, DH, NQ)
        w_raw = at(ar, 4032, NS, 512)
        head_cols = spare[:, :, :].rearrange("p n (c k) -> p (n c) k", k=P)
        dk_raw = spare
        dk_prod = at(ar, 0, 2, P)
        g32 = at(ar, 0, 2, NQ)
        w_s = at(ct[:, :, :, :].rearrange("p s e t -> p (s e t)"), 0, 2 * NS, 512)
        h1 = at(rr, 2048, 4, NQ)
        oh0 = at(ct[:, :, :, :].rearrange("p s e t -> p (s e t)"), 0, 2 * 2, DH * NQ)
        oh = at(rr, 3840, 2 * 2, DH * NQ)
        hs = at(rr, 3840, 2, DH, NQ)
        dv_m = at(rr, 3840 + 3584, 2, P)
        small = sb("small", [P, 2 * P + NQ])
        dv = small[0:80, 0:P]
        dv2 = small[0:80, P:2 * P]
        pb_f = small[0:80, 2 * P:2 * P + NQ]
        pb_s = sb("pb_s", [80, NQ], F32R)
        dvr = sb("dvr", [80, P])
        dv_hi = sb("dv_hi", [80, P], F32R)
        mask_u8 = sb("mask_u8", [P, S], U8)
        tmp16 = sb("tmp16", [H, 1])
        hsel = sb("hsel", [96, H])
        u_k = sb("u_k", [P, DH, H])
        cb = sb("cb", [H, 4 * P])
        cbv = sb("cbv", [H, 1])
        lb_s = sb("lb_s", [H, NQ])
        tiles_row = sb("tiles_row", [GT, P])

        NV = 0
        V = {}
        for n, w in (("g0", DH), ("b0", DH), ("s1", DH), ("o1", DH), ("s2", DH), ("o2", DH),
                     ("sm", DH), ("om", DH), ("bo1", DH), ("bo2", DH), ("bf2", DH), ("bf1", 8)):
            V[n] = vec[:, NV:NV + w]
            NV += w
        hb = sb("hb", [P, 4, H])
        gam_b = small[:, 0:D]

        names = """const_dma gate_dma seed fix ident_ready masks_ready gate_ready
            rawt_in raw_in stat_out stat_in mask_in mask_ready
            ct_hi ct_lo_v ct_lo_p cx_hi cx_lo_p cx_lo_v
            bn_done aggr_done std_ready stat_t stat_row at_p a_ready
            q_hi q_lo scores red neg_ready extra_exp exp_done sum_ready rinv_ready pb_ready
            tr p_hi p_lo pv o_low_ready o_ready o_t o_back
            w_in0 w_in1 w_in2 w_in3 w_hi w_lo dk_in0 dk_in1 dk_in2 dk_in3 dk_ready prod_ready u_ready
            oh_hi oh_lo dv_ready m1 h1_hi h1_lo gelu_done m2 qe_act qe_dve y_done x_ready
            ln_pe ln_dve ln_act h_split small_in small_dve small_pe small_dma phase out_done
            w0_in w0_even w0_hi w0_lo w0_mask w0_mean x_in fix_v""".split()
        s = {n: sem(n) for n in names}

        W0_M = 0
        W0_S = 1024
        QT0 = 3072
        X0 = QT0 + 4 * NQ
        M2_0 = H
        M1_0 = 2 + H
        assert X0 + 4 * NQ <= RR
        LN_V = 12
        N_CONST = 17
        lb_d = io["lb_d"]
        pb_d = io["pb_d"]
        st_d = io["st_d"]

        block = ctx.enter_context(nc.Block())

        def f(v):
            return v.bitcast(F32)

        def wait_apart(eng, semaphore, value):
            value = value if isinstance(value, int) else eng.to_reg(value)
            eng.wait_ge(s["phase"], 4)
            eng.wait_ge(semaphore, value)

        def groups(eng, steps, group):
            last = steps // NS - 1
            group(0, True, False)
            if last > 1:
                with eng.Fori(1, last) as m:
                    group(m, False, False)
            group(last, False, True)

        def drain(eng, k):
            eng.drain().then_inc(s["phase"], 1)
            eng.wait_ge(s["phase"], 4 * k)

        A_BASE = {1: 0, 2: 32}
        O_BASE = {1: 16, 2: 48}
        O_BASE_I = {O_BASE[1]: 1, O_BASE[2]: 2}
        M_BASE = 64
        W1 = {("a", 1): ("wq1", "wk1"), ("a", 2): ("wq2", "wk2"), ("o", 1): ("wv1", "wo1"),
              ("o", 2): ("wv2", "wo2"), ("m", 0): ("fc1", "fc2")}
        SCALE = float(K) ** -0.5
        SCALE0 = float(HD0) ** -0.5

        def qo_tile(g):
            return qo[:, :, bass.ds(PAD + g * P, P)]

        def qo_head(h):
            v = qo[:, :, PAD:PAD + B * ROWS].rearrange("p e (b r) -> p e b r", b=B)
            return v[:, :, :, bass.ds(h * TQ, TQ)]

        @block.sync
        def _(sp):
            sp.dma_start(xt[:, :, :], io["xt"].rearrange("(e p) q -> p e q", p=P)).then_inc(s["x_in"], 16)
            sp.dma_start(w0[:, 0:2, :], io["wq0t"].rearrange("(e p) q -> p e q", p=P)).then_inc(s["w0_in"], 16)
            sp.dma_start(w0[:, 2:4, :], io["wk0"].rearrange("(e p) q -> p e q", p=P)).then_inc(s["w0_in"], 16)
            sp.dma_start(gam_b[:, :], io["g0row"].partition_broadcast(P)).then_inc(s["w0_in"], 16)

            def constants():
                n_const = 1
                for name, dst in (("g0", V["g0"]), ("b0", V["b0"]), ("s1", V["s1"]), ("o1", V["o1"]),
                                  ("s2", V["s2"]), ("o2", V["o2"]), ("sm", V["sm"]), ("om", V["om"]),
                                  ("bo1", V["bo1"]), ("bo2", V["bo2"]), ("bf2", V["bf2"]), ("bf1", V["bf1"]),
                                  ("bq1", hb[:, 0, :]), ("bv1", hb[:, 1, :]), ("bq2", hb[:, 2, :]),
                                  ("bv2", hb[:, 3, :])):
                    sp.dma_start(dst, io[name]).then_inc(s["const_dma"], 16)
                    n_const += 1
                sp.dma_start(gate_t[:, 0:1], io["gate"].partition_broadcast(P)).then_inc(s["const_dma"], 16)
                assert n_const == N_CONST

            def load_context(r, b, nxt):
                bc = r * B + nxt
                src = io["ctx_t"][bass.ds(b, 1), :, :].rearrange("o (e p) t -> p (o e) t", p=P)
                body = io["ctx"][bass.ds(b, 1), 0:(CH - 1) * P, :].rearrange("o (c p) d -> p (o c) d", p=P)
                tail = io["ctx"][bass.ds(b, 1), (CH - 1) * P:S, :].rearrange("o p d -> p o d")
                wait_apart(sp, s["ct_hi"], 3 * bc)
                wait_apart(sp, s["ct_lo_v"], 2 * bc)
                wait_apart(sp, s["ct_lo_p"], bc)
                sp.dma_start(raw_t[:, :, :], src).then_inc(s["rawt_in"], 16)
                wait_apart(sp, s["cx_hi"], 3 * bc)
                wait_apart(sp, s["cx_lo_p"], 2 * bc)
                wait_apart(sp, s["cx_lo_v"], bc)
                sp.dma_start(raw[:, 0:CH - 1, :], body).then_inc(s["raw_in"], 16)
                sp.dma_start(raw[0:TAIL, CH - 1:CH, :], tail).then_inc(s["raw_in"], 16)

            def token_stats(b):
                wait_apart(sp, s["stat_row"], b + 1)
                sp.dma_start(st_d, mv_row[:, :]).then_inc(s["stat_out"], 16)
                wait_apart(sp, s["stat_out"], 16 * (b + 1))
                flat = st_d.rearrange("c p -> (c p)")
                wait_apart(sp, s["at_p"], 2 * b)
                sp.dma_start(rs_b, flat[0:S].partition_broadcast(P)).then_inc(s["stat_in"], 16)

            def load_mask(b):
                src = io["mask"][bass.ds(b, 1), :].rearrange("o t -> (o t)").partition_broadcast(P)
                if not isinstance(b, int):
                    wait_apart(sp, s["mask_ready"], b)
                sp.dma_start(mask_u8[:, :], src)\
                    .then_inc(s["mask_in"], 16)

            sp.wait_ge(s["seed"], 1)
            load_context(0, 0, 0)
            constants()
            load_mask(0)
            sp.wait_ge(s["phase"], 8)
            sp.dma_start(w0[:, 0:2, :], io["wv0t"].rearrange("(e p) q -> p e q", p=P)).then_inc(s["w0_in"], 16)
            sp.dma_start(w0[:, 2:4, :], io["wo0t"].rearrange("(e p) q -> p e q", p=P)).then_inc(s["w0_in"], 16)
            token_stats(0)
            with sp.Fori(0, B - 1) as b:
                load_mask(b + 1)
                load_context(0, b + 1, b + 1)
                token_stats(b + 1)

            def step_weights(kind, i, n, base, slot, fresh):
                first, second = W1[(kind, i)]
                w0 = io[first].rearrange("(e p) k -> p e k", p=P)[:, :, bass.ds(n * P, P)]
                w1 = io[second][bass.ds(n * P, P), :]
                if kind == "a":
                    rows = [io[f"{name}{i}"].rearrange("h k -> (h k)")[bass.ds(n * P, P)].partition_broadcast(P)
                            for name in ("biask", "bk")]
                if not fresh:
                    wait_apart(sp, s["w_hi"], base + n - NS + 1)
                    wait_apart(sp, s["w_lo"], base + n - NS + 1)
                if not fresh and kind == "a" or kind == "o":
                    wait_apart(sp, s["prod_ready"], A_BASE[i] // 2 + (n - NS + 1 if kind == "a" else H))
                sp.dma_start(w_raw[:, slot, 0:D].rearrange("p (e k) -> p e k", e=DH), w0)\
                    .then_inc(s[f"w_in{slot}"], 16)
                sp.dma_start(w_raw[:, slot, D:2 * D], w1).then_inc(s[f"w_in{slot}"], 16)
                if kind == "a":
                    for c in (0, 1):
                        sp.dma_start(dk_raw[:, slot, c * P:(c + 1) * P], rows[c]).then_inc(s[f"dk_in{slot}"], 16)

            def weights(kind, i, steps, base):
                for n in range(NS):
                    step_weights(kind, i, n, base, n, base == 0)
                with sp.Fori(1, steps // NS) as m:
                    for slot in range(NS):
                        step_weights(kind, i, NS * m + slot, base, slot, False)

            load_context(1, 0, 0)
            sp.wait_ge(s["phase"], 16)
            for i in (1, 2):
                weights("a", i, H, A_BASE[i])
                for n, name in enumerate((f"bq{i}h", f"biask{i}", f"bk{i}")):
                    sp.dma_start(cb[:, n * P:(n + 1) * P], io[name]).then_inc(s["small_in"], 16)
                sp.wait_ge(s["small_dve"], 6 * (i - 1) + 2)
                sp.dma_start(lb_d.rearrange("(b h q) -> h b q", b=B, h=H),
                             lb_s[:, :].rearrange("h (b q) -> h b q", b=B)).then_inc(s["small_dma"], 16)
                sp.wait_ge(s["small_dma"], 96 * (i - 1) + 16)
                sp.dma_start(tiles_row[:, :], lb_d.rearrange("(g p) -> g p", p=P)).then_inc(s["small_dma"], 16)
                with sp.Fori(0, B - 1) as b:
                    load_context(i, b + 1, b + 1)
                if i == 1:
                    load_context(2, 0, 0)
                sp.wait_ge(s["phase"], 4 * (3 * i + 3))
                sp.wait_ge(s["small_dve"], 6 * (i - 1) + 4)
                sp.dma_start(pb_d.rearrange("(g p) -> g p", p=P), tiles_row[:, :]).then_inc(s["small_dma"], 16)
                sp.wait_ge(s["small_dma"], 96 * (i - 1) + 48)
                for p0 in (0, 32, 64):
                    sp.dma_start(pb_f[p0:p0 + H, :].rearrange("h (b q) -> h b q", b=B),
                                 pb_d.rearrange("(b h q) -> h b q", b=B, h=H)).then_inc(s["small_dma"], 16)
                    sp.dma_start(dv[p0:p0 + H, :], io[f"biasv{i}"]).then_inc(s["small_in"], 16)
                    sp.dma_start(dv2[p0:p0 + H, :], io[f"bv{i}h"]).then_inc(s["small_in"], 16)
                weights("o", i, H, O_BASE[i])
                sp.wait_ge(s["phase"], 4 * (3 * i + 4))
            weights("m", 0, F // P, M_BASE)
            sp.wait_ge(s["x_ready"], 8)
            sp.dma_start(io["out"].rearrange("(e p) q -> p e q", p=P), xt[:, :, :]).then_inc(s["out_done"], 16)
            sp.wait_ge(s["out_done"], 16)

        @block.gpsimd
        def _(pool):
            pool.memset(raw[:, CH - 1, :], 0.0).then_inc(s["seed"], 1)
            for t, v in ((ident[:, :], 0.0), (head_rows[:, :, 0], 1.0), (head_cols[:, :, :], 0.0),
                         (mean_w[:, :], 1.0 / D), (mhalf[:, :], -0.5), (o_row[:, :], 0.0), (mv[:, :, :], 1.0)):
                pool.memset(t, v).then_inc(s["fix"], 1)
            pool.wait_ge(s["fix"], 7)
            pool.affine_select(out=ident[:, :], in_=ident[:, :], compare_op=ALU.not_equal, fill=1.0,
                               base=0, pattern=[[-1, P]], channel_multiplier=1).then_inc(s["ident_ready"], 1)
            pool.affine_select(out=head_rows[:, :, 0], in_=head_rows[:, :, 0], compare_op=ALU.is_ge, fill=0.0,
                               base=0, pattern=[[-HD0, HPC]], channel_multiplier=1).then_inc(s["fix"], 1)
            pool.wait_ge(s["fix"], 8)
            pool.affine_select(out=head_rows[:, :, 0], in_=head_rows[:, :, 0], compare_op=ALU.is_ge, fill=0.0,
                               base=HD0 - 1, pattern=[[HD0, HPC]], channel_multiplier=-1).then_inc(s["fix"], 1)
            for m in range(HPC):
                pool.memset(head_cols[:, m, m * HD0:(m + 1) * HD0], 1.0).then_inc(s["fix"], 1)
            drain(pool, 1)

            def low0(n, src):
                pool.wait_ge(s["w0_hi"], n + 1)
                v = at(rr, W0_S, 4, 2 * D)[:, 2 * (n % 2):2 * (n % 2) + 2, :]
                pool.tensor_tensor(v[:, :, D:2 * D], src, f(v[:, :, 0:D]), ALU.subtract).then_inc(s["w0_lo"], 1)

            low0(0, w0[:, 0:2, :])
            low0(1, w0[:, 2:4, :])
            drain(pool, 2)

            def norm_context(b):
                wait_apart(pool, s["aggr_done"], b + 1)
                pool.tensor_scalar(mv[:, 1, :], mv[:, 1, :], EPS, None, ALU.add).then_inc(s["std_ready"], 1)
                pool.wait_ge(s["std_ready"], 2 * b + 1)
                pool.tensor_tensor(mv[:, 1, :], mv[:, 1, :], mhalf[:, :], ALU.pow).then_inc(s["std_ready"], 1)
                pool.wait_ge(s["stat_in"], 16 * (b + 1))
                pool.wait_ge(s["rawt_in"], 16 * (b + 1))
                for e in range(DH):
                    pool.tensor_tensor(raw_t[:, e, :], raw_t[:, e, :], rs_b, ALU.mult).then_inc(s["at_p"], 1)

            def split_ct(r, b, g6):
                bc = r * B + b
                pool.wait_ge(s["ct_hi"], 3 * bc + 2)
                v = slice(SB, 2 * SB)
                pool.tensor_tensor(ct[:, 1, :, v], raw_t[:, :, v], f(ct[:, 0, :, v]), ALU.subtract)\
                    .then_inc(s["ct_lo_p"], 1)

            def split_cx(r, b):
                bc = r * B + b
                for k in (0, 2):
                    v = slice(GRP * k, GRP * (k + 1))
                    pool.wait_ge(s["cx_hi"], 3 * bc + k + 1)
                    pool.tensor_tensor(cx[:, v, D:2 * D], raw[:, v, :], f(cx[:, v, 0:D]), ALU.subtract)\
                        .then_inc(s["cx_lo_p"], 1)

            def run(r):
                if r == 0:
                    norm_context(0)
                split_ct(r, 0, None)
                split_cx(r, 0)
                with pool.Fori(0, B - 1) as b:
                    if r == 0:
                        norm_context(b + 1)
                    split_ct(r, b + 1, None)
                    split_cx(r, b + 1)

            def step_splits(kind, i, steps, base):
                def group(m):
                    for slot in range(NS):
                        n = NS * m + slot
                        pool.wait_ge(s["w_hi"], base + n + 1)
                        pool.tensor_tensor(w_s[:, 2 * slot + 1, :], w_raw[:, slot, :], f(w_s[:, 2 * slot, :]),
                                           ALU.subtract).then_inc(s["w_lo"], 1)
                        if kind == "a":
                            pool.wait_ge(s[f"dk_in{slot}"], 32 * (A_BASE[i] // 2 // NS + m + 1))
                            pool.tensor_tensor(dk_raw[:, slot, 0:P], dk_raw[:, slot, 0:P], dk_raw[:, slot, P:2 * P],
                                               ALU.subtract).then_inc(s["dk_ready"], 1)
                group(0)
                with pool.Fori(1, steps // NS) as m:
                    group(m)

            run(0)
            drain(pool, 3)
            low0(2, w0[:, 4:6, :])
            low0(3, w0[:, 2:4, :])
            pool.wait_ge(s["w0_lo"], 3)
            for jc in (0, 1):
                for n in range(HPC):
                    if 8 * jc + n >= 2:
                        pool.wait_ge(s["m1"], M1_0 - 16 + 8 * jc + n - 1)
                    src = f(at(rr, W0_S, 4, D))[:, :, P * jc:P * (jc + 1)]
                    pool.tensor_tensor(at(rr, W0_M + 512 * (n % 2), 4, P), src,
                                       head_cols[:, n:n + 1, :].to_broadcast([P, 4, P]), ALU.mult)\
                        .then_inc(s["w0_mask"], 1)
            drain(pool, 4)
            for i in (1, 2):
                step_splits("a", i, H, A_BASE[i])
                drain(pool, 3 * i + 2)
                run(i)
                drain(pool, 3 * i + 3)
                step_splits("o", i, H, O_BASE[i])
                drain(pool, 3 * i + 4)
            step_splits("m", 0, F // P, M_BASE)
            drain(pool, 11)

        def three(eng, out, w_hi, w_lo, x_hi, x_lo, start, stop):
            eng.matmul(out, w_hi, x_hi, start=start, stop=False, skip_group_check=True)
            eng.matmul(out, w_hi, x_lo, start=False, stop=False, skip_group_check=True)
            return eng.matmul(out, w_lo, x_hi, start=False, stop=stop, skip_group_check=True)

        @block.tensor
        def _(pe):
            drain(pe, 1)
            wq = at(rr, W0_S, 2, 2 * D)
            xs = at(rr, X0, 2, DH * NQ)
            pe.wait_ge(s["w0_lo"], 1)
            pe.wait_ge(s["h_split"], 2)
            for jc in range(2):
                for e in range(DH):
                    mm = three(pe, ps[:, jc, 0:NQ], wq[:, e, P * jc:P * jc + P], wq[:, e, D + P * jc:D + P * jc + P],
                               xs[:, 0, e * NQ:(e + 1) * NQ], xs[:, 1, e * NQ:(e + 1) * NQ], e == 0, e == DH - 1)
                mm.then_inc(s["m1"], 1)
            for h in range(H):
                jc = h // HPC
                q_s = at(rr, QT0, 2, 2 * NQ)
                wm = at(rr, W0_M + 512 * (h % 2), 512)
                pe.wait_ge(s["w0_mask"], h + 1)
                pe.wait_ge(s["h1_lo"], jc + 1)
                if h >= 2:
                    pe.wait_ge(s["qe_act"], h - 1)
                    pe.wait_ge(s["qe_dve"], h - 1)
                for e in range(DH):
                    mm = three(pe, ps[:, 2 + 2 * (h % 2) + e, 0:NQ], wm[:, e * P:e * P + P],
                               wm[:, D + e * P:D + e * P + P], q_s[:, 0, jc * NQ:(jc + 1) * NQ],
                               q_s[:, 1, jc * NQ:(jc + 1) * NQ], True, True)
                mm.then_inc(s["m2"], 1)
            drain(pe, 2)

            def scores(r, b, t, g, j):
                gg, bc = r * GT + g, r * B + b
                if j == 0:
                    pe.wait_ge(s["q_hi"], gg + 1)
                    pe.wait_ge(s["q_lo"], gg + 1)
                    if r == 0:
                        pe.wait_ge(s["red"], 3 * gg)
                    else:
                        pe.wait_ge(s["exp_done"], gg)
                if t == 0:
                    pe.wait_ge(s["ct_hi"], 3 * bc + j + 1)
                    if j == 1:
                        pe.wait_ge(s["ct_lo_p"], bc + 1)
                    else:
                        pe.wait_ge(s["ct_lo_v"], 2 * bc + 1 + j // 2)
                v = slice(SB * j, SB * (j + 1))
                q = QBUF[t]
                for e in range(DH):
                    mm = three(pe, ps[:, j, 0:SB], qt[:, 2 * q, e, :], qt[:, 2 * q + 1, e, :],
                               ct[:, 0, e, v], ct[:, 1, e, v], e == 0, e == DH - 1)
                mm.then_inc(s["scores"], 1)

            def transposes(r, g, k):
                gg = r * GT + g
                if k == 0:
                    pe.wait_ge(s["exp_done"], gg + 1)
                for c in range(GRP * k, GRP * (k + 1)):
                    mm = pe.transpose(ps[:, 3 + k, (c % GRP) * P:(c % GRP) * P + P], prob[:, c * P:(c + 1) * P],
                                      ident[:, :])
                mm.then_inc(s["tr"], 1)

            def turn_output(r, g):
                n = r * (GT + 1) + g + 1
                pe.wait_ge(s["o_ready"], n + 1)
                pe.wait_ge(s["o_back"], n + 1)
                for e in range(DH):
                    mm = pe.transpose(ps[:, 7, e * P:(e + 1) * P], o_row[:, e * P:(e + 1) * P], ident[:, :])
                mm.then_inc(s["o_t"], 1)

            def turn_stats(b, outputs):
                pe.wait_ge(s["std_ready"], 2 * b + 2)
                pe.wait_ge(s["o_back"], outputs + 1)
                pe.transpose(ps[0:CH, 7, 256:256 + P], mv[:, 1, :], ident[:, :])\
                    .then_inc(s["stat_t"], 1)

            def weighted(r, b, t, g):
                gg, bc = r * GT + g, r * B + b
                pe.wait_ge(s["o_ready"], r * (GT + 1) + g + 1)
                for c in range(CH):
                    n = P if c < CH - 1 else TAIL
                    if c % GRP == 0:
                        pe.wait_ge(s["p_hi"], 3 * gg + c // GRP + 1)
                        pe.wait_ge(s["p_lo"], 3 * gg + c // GRP + 1)
                        if t == 0:
                            pe.wait_ge(s["cx_hi"], 3 * bc + c // GRP + 1)
                            if c // GRP == 1:
                                pe.wait_ge(s["cx_lo_v"], bc + 1)
                            else:
                                pe.wait_ge(s["cx_lo_p"], 2 * bc + 1 + c // GRP // 2)
                    pe.matmul(ps[:, 6, :], pt[0:n, 0, c, :], cx[0:n, c, :], start=c == 0, stop=False,
                              skip_group_check=True)
                    mm = pe.matmul(ps[:, 6, 0:D], pt[0:n, 1, c, :], cx[0:n, c, 0:D], start=False,
                                   stop=c == CH - 1, skip_group_check=True)
                mm.then_inc(s["pv"], 1)

            def batch(r, b, last):
                for t in range(TILES):
                    g = TILES * b + t
                    nb, nt = (b, t + 1) if t < TILES - 1 else (b + 1, 0)
                    for k in range(3):
                        if not (last and t == TILES - 1):
                            scores(r, nb, nt, g + 1, k)
                        transposes(r, g, k)
                    if r == 0 and t == 3 and not last:
                        turn_stats(b + 1, r * (GT + 1) + g)
                    turn_output(r, g - 1)
                    weighted(r, b, t, g)

            def run(r):
                if r == 0:
                    turn_stats(0, 0)
                for j in range(3):
                    scores(r, 0, 0, 0, j)
                if r == 0:
                    pe.wait_ge(s["stat_row"], 1)
                with pe.Fori(0, B - 1) as b:
                    batch(r, b, False)
                batch(r, B - 1, True)
                turn_output(r, GT - 1)

            run(0)
            drain(pe, 3)
            pe.wait_ge(s["w0_even"], 4)
            for e in range(DH):
                pe.matmul(ps[:, 4, 0:D], mean_w[:, :], w0[:, 4 + e, :], start=e == 0, stop=e == DH - 1)
            for jc in (0, 1):
                for e in range(DH):
                    mm = pe.matmul(ps[:, 5, jc:jc + 1], w0[:, e, P * jc:P * jc + P], V["b0"][:, e:e + 1],
                                   start=e == 0, stop=e == DH - 1)
            mm.then_inc(s["w0_mean"], 1)
            for h in range(H):
                jc = h // HPC
                wm = at(rr, W0_M + 512 * (h % 2), 4, P)
                ohs = oh0[:, 2 * (h % 2):2 * (h % 2) + 2, :]
                pe.wait_ge(s["w0_mask"], H + h + 1)
                pe.wait_ge(s["oh_hi"], h + 1)
                pe.wait_ge(s["oh_lo"], h + 1)
                for e in range(DH):
                    mm = three(pe, ps[:, jc, 0:NQ], wm[:, 2 * e, :], wm[:, 2 * e + 1, :],
                               ohs[:, 0, e * NQ:(e + 1) * NQ], ohs[:, 1, e * NQ:(e + 1) * NQ],
                               h % HPC == 0 and e == 0, h % HPC == HPC - 1 and e == DH - 1)
                mm.then_inc(s["m1"], 1)
            pe.wait_ge(s["h1_lo"], 4)
            pe.wait_ge(s["w0_lo"], 4)
            wo = at(rr, W0_S + 1024, 2, 2 * D)
            o_s = at(rr, QT0, 2, 2 * NQ)
            for e in range(DH):
                for jc in (0, 1):
                    mm = three(pe, ps[:, 2 + e, 0:NQ], wo[:, jc, e * P:e * P + P], wo[:, jc, D + e * P:D + e * P + P],
                               o_s[:, 0, jc * NQ:(jc + 1) * NQ], o_s[:, 1, jc * NQ:(jc + 1) * NQ], jc == 0, jc == 1)
            mm.then_inc(s["y_done"], 1)
            drain(pe, 4)

            def norm(n):
                for e in range(DH):
                    mm = pe.matmul(ps[:, 0, 0:NQ], mean_w[:, :], xt[:, e, :], start=e == 0, stop=e == DH - 1)
                mm.then_inc(s["ln_pe"], 1)
                pe.wait_ge(s["ln_dve"], LN_V * n + 2)
                for e in range(DH):
                    mm = pe.matmul(ps[:, 1, 0:NQ], mean_w[:, :], sq[:, e, :], start=e == 0, stop=e == DH - 1)
                mm.then_inc(s["ln_pe"], 1)
                pe.wait_ge(s["h_split"], 2 + 2 * (n + 1))

            def first_product(kind, base, n, slot, fresh):
                pe.wait_ge(s["w_lo"], base + n + 1)
                if not fresh:
                    pe.wait_ge(s["h1_lo"], 4 + base + n - 1)
                w = w_s[:, 2 * slot:2 * slot + 2, 0:D]
                slot %= 2
                out = ps[:, slot, 0:NQ]
                if kind == "o":
                    i = O_BASE_I[base]
                    pe.wait_ge(s["oh_hi"], H * i + n + 1)
                    pe.wait_ge(s["oh_lo"], H * i + n + 1)
                    x = oh[:, 2 * slot:2 * slot + 2, :]
                else:
                    x = hs[:, :, :, :].rearrange("p s e q -> p s (e q)")
                for e in range(DH):
                    mm = three(pe, out, w[:, 0, e * P:e * P + P], w[:, 1, e * P:e * P + P],
                               x[:, 0, e * NQ:(e + 1) * NQ], x[:, 1, e * NQ:(e + 1) * NQ], e == 0,
                               e == DH - 1 and kind != "o")
                if kind == "o":
                    pe.wait_ge(s["dv_ready"], H * (i - 1) + n + 1)
                    mm = pe.matmul(out, dv_m[0:80, slot, :], pb_s[:, :], start=False, stop=True, skip_group_check=True)
                mm.then_inc(s["m1"], 1)

            def second_product(kind, i, base, n, slot, first, last, fresh):
                pe.wait_ge(s["h1_lo"], 4 + base + n + 1)
                w = w_s[:, 2 * slot:2 * slot + 2, D:2 * D]
                slot %= 2
                if kind == "a" and not fresh:
                    pe.wait_ge(s["qe_act"], H * i + n - 1)
                    pe.wait_ge(s["qe_dve"], H * i + n - 1)
                for e in range(DH):
                    out = ps[:, 2 + 2 * slot + e, 0:NQ] if kind == "a" else ps[:, 6 + e, 0:NQ]
                    mm = three(pe, out, w[:, 0, e * P:e * P + P], w[:, 1, e * P:e * P + P], h1[:, 2 * slot, :],
                               h1[:, 2 * slot + 1, :], kind == "a" or first, kind == "a" or last)
                mm.then_inc(s["m2"], 1)

            def products(kind, i, steps, base):
                def group(m, first, last):
                    for slot in range(NS):
                        n = NS * m + slot
                        end = last and slot == NS - 1
                        if not end:
                            first_product(kind, base, n + 1, (slot + 1) % NS, first and slot == 0)
                        second_product(kind, i, base, n, slot, first and slot == 0, end, first and slot < 2)
                first_product(kind, base, 0, 0, True)
                groups(pe, steps, group)

            for i in (1, 2):
                norm(i - 1)
                products("a", i, H, A_BASE[i])
                pe.wait_ge(s["u_ready"], H * i)
                pe.wait_ge(s["qe_act"], H * i + H)
                pe.wait_ge(s["qe_dve"], H * i + H)
                for e in range(DH):
                    mm = pe.matmul(ps[0:H, 2, 0:NQ], u_k[:, e, :], ht[:, e, :], start=e == 0, stop=e == DH - 1)
                mm.then_inc(s["small_pe"], 1)
                pe.wait_ge(s["small_dma"], 96 * (i - 1) + 32)
                pe.transpose(ps[:, 3, 0:GT], tiles_row[:, :], ident[0:GT, 0:GT]).then_inc(s["small_pe"], 1)
                drain(pe, 3 * i + 2)
                run(i)
                drain(pe, 3 * i + 3)
                pe.transpose(ps[0:GT, 2, 0:P], pbq[:, :], ident[:, :]).then_inc(s["small_pe"], 1)
                pe.wait_ge(s["small_dve"], 6 * (i - 1) + 5)
                pe.wait_ge(s["small_dve"], 6 * (i - 1) + 6)
                products("o", i, H, O_BASE[i])
                drain(pe, 3 * i + 4)
            norm(2)
            products("m", 0, F // P, M_BASE)
            drain(pe, 11)

        @block.scalar
        def _(act):
            drain(act, 1)
            act.wait_ge(s["x_in"], 16)
            act.activation(at(rr, X0, 2, DH * NQ)[:, 0, :], xt[:, :, :].rearrange("p e q -> p (e q)"), ACT.Copy)\
                .then_inc(s["h_split"], 1)

            def high0(n, src):
                v = at(rr, W0_S, 4, 2 * D)[:, 2 * (n % 2):2 * (n % 2) + 2, 0:D]
                act.activation(v, src, ACT.Copy).then_inc(s["w0_hi"], 1)

            act.wait_ge(s["w0_in"], 48)
            high0(0, w0[:, 0:2, :])
            act.wait_ge(s["w0_even"], 3)
            high0(1, w0[:, 2:4, :])
            for jc in (0, 1):
                act.wait_ge(s["m1"], jc + 1)
                act.activation(at(rr, QT0, 4, NQ)[:, jc, :], ps[:, jc, 0:NQ], ACT.Copy, scale=SCALE0)\
                    .then_inc(s["h1_hi"], 1)

            def q_back(h, bank, scale, done):
                dst = qo_head(h)[:, 0, :, :]
                wait_apart(act, s["m2"], done)
                act.activation(dst, ps[:, bank, 0:NQ].rearrange("p (b q) -> p b q", b=B), ACT.Copy, scale=scale)\
                    .then_inc(s["qe_act"], 1)

            for h in range(H):
                q_back(h, 2 + 2 * (h % 2), 1.0, h + 1)
            act.wait_ge(s["const_dma"], 16 * N_CONST)
            act.activation(gate_t[:, 1:2], gate_t[:, 0:1], ACT.Tanh).then_inc(s["o_back"], 1)
            drain(act, 2)

            def split_ct(r, b, thirds):
                bc = r * B + b
                for j in thirds:
                    if r == 0:
                        act.wait_ge(s["at_p"], 2 * bc + 2)
                    else:
                        act.wait_ge(s["rawt_in"], 16 * (bc + 1))
                    v = slice(SB * j, SB * (j + 1))
                    if not isinstance(b, int):
                        act.wait_ge(s["scores"], r * 3 * GT + 3 * TILES * b - 2 + j)
                    act.activation(ct[:, 0, :, v], raw_t[:, :, v], ACT.Copy).then_inc(s["ct_hi"], 1)

            def split_cx(r, b):
                bc = r * B + b
                if r:
                    act.wait_ge(s["raw_in"], 32 * (bc + 1))
                act.wait_ge(s["pv"], r * GT + TILES * b)
                for k in range(3):
                    if r == 0:
                        act.wait_ge(s["a_ready"], 3 * bc + k + 1)
                    v = slice(GRP * k, GRP * (k + 1))
                    act.activation(cx[:, v, 0:D], raw[:, v, :], ACT.Copy).then_inc(s["cx_hi"], 1)

            def split_q(r, t, g):
                src = qo_tile(g)
                if not isinstance(g, int) or g >= 2:
                    wait_apart(act, s["scores"], 3 * (r * GT + g - 1))
                act.activation(qt[:, 2 * QBUF[t], :, :], src, ACT.Copy).then_inc(s["q_hi"], 1)

            def softmax(r, g):
                gg = r * GT + g
                logit = lbq[:, bass.ds(g, 1)]
                act.wait_ge(s["rinv_ready"], gg)
                wait_apart(act, s["neg_ready"], gg + 1)
                if r:
                    act.activation(extra[:, :], logit, ACT.Exp, bias=negm[:, :])\
                        .then_inc(s["extra_exp"], 1)
                    act.wait_ge(s["tr"], 3 * gg)
                    src = ps[:, 0:3, 0:SB]
                else:
                    src = prob[:, 0:S].rearrange("p (j t) -> p j t", j=3)
                act.activation(prob[:, 0:S].rearrange("p (j t) -> p j t", j=3), src, ACT.Exp,
                               bias=negm[:, :], accum_out=rowsum[:, :]).then_inc(s["exp_done"], 1)

            def turn_output(r, g, stats_of=None):
                n = r * (GT + 1) + g + 1
                if stats_of is not None:
                    act.wait_ge(s["o_t"], n + 1)
                    turn_stats(stats_of)
                dst = qo_tile(g)
                wait_apart(act, s["o_t"], n + 1)
                act.activation(dst,
                               ps[:, 7, 0:D].rearrange("p (e r) -> p e r", e=DH), ACT.Copy).then_inc(s["o_back"], 1)

            def turn_stats(b):
                act.wait_ge(s["stat_t"], b + 1)
                act.wait_ge(s["stat_out"], 16 * b)
                act.activation(mv_row[:, :], ps[0:CH, 7, 256:256 + P], ACT.Copy).then_inc(s["stat_row"], 1)

            def batch(r, b, last):
                for t in range(TILES):
                    g = TILES * b + t
                    gg = r * GT + g
                    for k in range(3):
                        act.wait_ge(s["tr"], 3 * gg + k + 1)
                        act.activation(pt[:, 0, GRP * k:GRP * (k + 1), :],
                                       ps[:, 3 + k, :].rearrange("p (c q) -> p c q", q=P), ACT.Copy)\
                            .then_inc(s["p_hi"], 1)
                        if t == TILES - 2 and not last and k < 2:
                            split_ct(r, b + 1, (k,))
                    if not (last and t >= TILES - 2):
                        split_q(r, (t + 2) % TILES, g + 2)
                    turn_output(r, g - 1, b + 1 if r == 0 and t == 3 and not last else None)
                    if not (last and t == TILES - 1):
                        softmax(r, g + 1)
                    if t == TILES - 2 and not last:
                        split_ct(r, b + 1, (2,))
                    act.wait_ge(s["pv"], gg + 1)
                    act.wait_ge(s["rinv_ready"], gg + 1)
                    act.wait_ge(s["o_ready"], r * (GT + 1) + g + 1)
                    act.activation(o_low[:, :], ps[:, 6, D:2 * D], ACT.Copy, scale=rinv[:, :])\
                        .then_inc(s["o_low_ready"], 1)
                    if t == 6 and not last:
                        split_cx(r, b + 1)

            def run(r):
                split_q(r, 0, 0)
                split_q(r, 1, 1)
                if r == 0:
                    turn_stats(0)
                split_ct(r, 0, range(3))
                softmax(r, 0)
                split_cx(r, 0)
                with act.Fori(0, B - 1) as b:
                    batch(r, b, False)
                batch(r, B - 1, True)
                turn_output(r, GT - 1)

            def split_heads(i, n, slot, fresh):
                dst = (oh if i else oh0)[:, 2 * slot, :]
                src = qo_head(n)
                if not fresh:
                    wait_apart(act, s["m1"], (M1_0 + O_BASE[i] if i else 2) + n - 1)
                act.activation(dst.rearrange("p (e b q) -> p e b q", e=DH, b=B), src, ACT.Copy)\
                    .then_inc(s["oh_hi"], 1)

            run(0)
            drain(act, 3)
            act.wait_ge(s["w0_even"], 5)
            high0(2, w0[:, 4:6, :])
            high0(3, w0[:, 2:4, :])
            for h in range(H):
                split_heads(0, h, h % 2, h < 2)
            for jc in (0, 1):
                act.wait_ge(s["m1"], 2 + HPC * (jc + 1))
                act.activation(at(rr, QT0, 4, NQ)[:, jc, :], ps[:, jc, 0:NQ], ACT.Identity, bias=bias0[:, jc:jc + 1])\
                    .then_inc(s["h1_hi"], 1)
            drain(act, 4)

            def norm(n):
                act.wait_ge(s["ln_dve"], LN_V * n + 3)
                act.activation(dev, var, ACT.Sqrt).then_inc(s["ln_act"], 1)
                act.wait_ge(s["ln_dve"], LN_V * (n + 1))
                act.activation(hs[:, 0, :, :], ht, ACT.Copy).then_inc(s["h_split"], 1)

            def first_split(kind, i, base, n, slot, fresh):
                src = ps[:, slot, 0:NQ]
                if kind == "m":
                    if not fresh:
                        act.wait_ge(s["h1_lo"], 4 + base + n - 1)
                    col = V["bf1"][:, bass.ds(n, 1)]
                    wait_apart(act, s["m1"], M1_0 + base + n + 1)
                    act.activation(g32[:, slot, :], src, ACT.Gelu, bias=col)\
                        .then_inc(s["h1_hi"], 1)
                else:
                    if not fresh:
                        act.wait_ge(s["m2"], M2_0 + base + n - 1)
                    col = hb[:, 2 * (i - 1) + (kind == "o"), bass.ds(n, 1)]
                    wait_apart(act, s["m1"], M1_0 + base + n + 1)
                    act.activation(h1[:, 2 * slot, :], src, ACT.Identity, bias=col).then_inc(s["h1_hi"], 1)

            def products(kind, i, steps, base):
                def high_weights(n, m, slot):
                    act.wait_ge(s[f"w_in{slot}"], 32 * (base // NS + m + 1))
                    if not isinstance(n, int) or n >= NS:
                        act.wait_ge(s["m2"], M2_0 + base + n - NS + 1)
                    act.activation(w_s[:, 2 * slot, :], w_raw[:, slot, :], ACT.Copy).then_inc(s["w_hi"], 1)

                def group(m, first, last):
                    for slot in range(NS):
                        n = NS * m + slot
                        if kind == "o" and not (last and slot >= NS - 2):
                            split_heads(i, n + 2, slot % 2, False)
                        if not (last and slot == NS - 1):
                            first_split(kind, i, base, n + 1, (slot + 1) % 2, first and slot == 0)
                        if not (last and slot):
                            high_weights(n + NS - 1, m + (1 if slot else 0), (slot + NS - 1) % NS)
                        if kind == "a":
                            q_back(n, 2 + 2 * (slot % 2), SCALE, M2_0 + base + n + 1)
                for n in range(NS - 1):
                    high_weights(n, 0, n)
                if kind == "o":
                    split_heads(i, 0, 0, True)
                    split_heads(i, 1, 1, True)
                first_split(kind, i, base, 0, 0, True)
                groups(act, steps, group)

            for i in (1, 2):
                norm(i - 1)
                products("a", i, H, A_BASE[i])
                drain(act, 3 * i + 2)
                run(i)
                drain(act, 3 * i + 3)
                products("o", i, H, O_BASE[i])
                drain(act, 3 * i + 4)
            norm(2)
            products("m", 0, F // P, M_BASE)
            drain(act, 11)

        @block.vector
        def _(dve):
            drain(dve, 1)
            for p0 in (0, 32, 64):
                dve.tensor_copy(hsel[p0:p0 + 32, :], ident[p0:p0 + 32, p0:p0 + H])
            wk = w0[:, 2:4, :]
            dve.wait_ge(s["w0_in"], 48)
            dve.tensor_tensor(wk, wk, gam_b[:, :].rearrange("p (o d) -> p o d", o=1).to_broadcast([P, 2, D]), ALU.mult)\
                .then_inc(s["w0_even"], 1)
            dve.wait_ge(s["w0_even"], 1)
            dve.tensor_reduce(wsum[:, :], wk, AX.X, ALU.add).then_inc(s["w0_even"], 1)
            dve.wait_ge(s["w0_even"], 2)
            dve.scalar_tensor_tensor(out=wk, in0=wsum[:, :].rearrange("p (e o) -> p e o", o=1).to_broadcast([P, 2, D]),
                                     scalar=-1.0 / D, in1=wk, op0=ALU.mult, op1=ALU.add).then_inc(s["w0_even"], 1)
            x_s = at(rr, X0, 2, DH * NQ)
            dve.wait_ge(s["h_split"], 1)
            dve.tensor_tensor(x_s[:, 1, :], xt[:, :, :].rearrange("p e q -> p (e q)"), f(x_s[:, 0, :]), ALU.subtract)\
                .then_inc(s["h_split"], 1)
            q_s = at(rr, QT0, 4, NQ)

            def mask_rows(h):
                dve.tensor_scalar(at(rr, W0_M + 512 * (h % 2), 512), f(at(rr, W0_S + 1024 + 512 * (h // HPC), 512)),
                                  head_rows[:, h % HPC, :], None, ALU.mult).then_inc(s["w0_mask"], 1)

            dve.wait_ge(s["w0_lo"], 2)
            mask_rows(0)
            mask_rows(1)
            for jc in (0, 1):
                dve.wait_ge(s["h1_hi"], jc + 1)
                dve.scalar_tensor_tensor(out=q_s[:, 2 + jc, :], in0=ps[:, jc, 0:NQ], scalar=SCALE0,
                                         in1=f(q_s[:, jc, :]), op0=ALU.mult, op1=ALU.subtract)\
                    .then_inc(s["h1_lo"], 1)

            def q_back(h, bank, scale):
                dve.tensor_scalar(qo_head(h)[:, 1, :, :], ps[:, bank, 0:NQ].rearrange("p (b q) -> p b q", b=B),
                                  scale, None, ALU.mult).then_inc(s["qe_dve"], 1)

            for h in range(H):
                dve.wait_ge(s["m2"], h + 1)
                if h < H - 2:
                    mask_rows(h + 2)
                q_back(h, 3 + 2 * (h % 2), 1.0)
            drain(dve, 2)

            def load_stats(b, c0, c1):
                if c0 == 0:
                    dve.wait_ge(s["raw_in"], 32 * (b + 1))
                    dve.wait_ge(s["stat_t"], b)
                for c in range(c0, c1):
                    ins = dve.bn_stats(bn[:, c, :], raw[:, c, :])
                if c1 == CH:
                    ins.then_inc(s["bn_done"], 1)
                    wait_apart(dve, s["bn_done"], b + 1)
                    for c in range(CH):
                        ins = dve.bn_aggr(mv[:, :, c], bn[:, c, :])
                    ins.then_inc(s["aggr_done"], 1)

            def scale_tokens(b, k):
                if k == 0:
                    dve.wait_ge(s["std_ready"], 2 * b + 2)
                for c in range(GRP * k, GRP * (k + 1)):
                    ins = dve.tensor_scalar(raw[:, c, :], raw[:, c, :], mv[:, 1, c:c + 1], None, ALU.mult)
                ins.then_inc(s["a_ready"], 1)

            def mask_bias(b):
                dve.wait_ge(s["mask_in"], 16 * (b + 1))
                dve.tensor_scalar(mask_b, mask_u8[:, :], -1.0, 3e38, ALU.add, ALU.mult).then_inc(s["mask_ready"], 1)
                dve.wait_ge(s["mask_ready"], b + 1)

            def split_ct(r, b):
                bc = r * B + b
                for j in (0, 2):
                    v = slice(SB * j, SB * (j + 1))
                    dve.wait_ge(s["ct_hi"], 3 * bc + j + 1)
                    dve.tensor_tensor(ct[:, 1, :, v], raw_t[:, :, v], f(ct[:, 0, :, v]), ALU.subtract)\
                        .then_inc(s["ct_lo_v"], 1)

            def split_cx(r, b):
                v = slice(GRP, 2 * GRP)
                dve.wait_ge(s["cx_hi"], 3 * (r * B + b) + 2)
                dve.tensor_tensor(cx[:, v, D:2 * D], raw[:, v, :], f(cx[:, v, 0:D]), ALU.subtract)\
                    .then_inc(s["cx_lo_v"], 1)

            def split_q(r, t, g):
                gg = r * GT + g
                dve.wait_ge(s["q_hi"], gg + 1)
                q = QBUF[t]
                dve.tensor_tensor(qt[:, 2 * q + 1, :, :], qo_tile(g), f(qt[:, 2 * q, :, :]), ALU.subtract)\
                    .then_inc(s["q_lo"], 1)

            def row_max(r, g, j):
                gg = r * GT + g
                if r:
                    dve.wait_ge(s["scores"], 3 * gg + j + 1)
                if r == 0:
                    v = prob[:, SB * j:SB * (j + 1)]
                    if not isinstance(g, int) or g:
                        dve.wait_ge(s["tr"], 3 * gg - 2 + j)
                    wait_apart(dve, s["scores"], 3 * gg + j + 1)
                    dve.tensor_tensor_reduce(out=v, in0=ps[:, j, 0:SB], in1=mask_b[:, SB * j:SB * (j + 1)], scale=1.0,
                                             scalar=-3.4e38, op0=ALU.add, op1=ALU.max, accum_out=mx4[:, j:j + 1])\
                        .then_inc(s["red"], 1)
                else:
                    dve.tensor_reduce(mx4[:, j:j + 1], ps[:, j, 0:SB], AX.X, ALU.max).then_inc(s["red"], 1)

            def neg_max(r, g):
                gg = r * GT + g
                n = 3
                if r:
                    n = 4
                    dve.tensor_copy(mx4[:, 3:4], lbq[:, bass.ds(g, 1)]).then_inc(s["sum_ready"], 1)
                    dve.wait_ge(s["sum_ready"], 2 * (gg - GT) + 1)
                dve.wait_ge(s["red"], 3 * gg + 3)
                dve.tensor_reduce(negm[:, :], mx4[:, 0:n], AX.X, ALU.max, negate=True).then_inc(s["neg_ready"], 1)

            def sums(r, g):
                gg = r * GT + g
                dve.wait_ge(s["exp_done"], gg + 1)
                dve.wait_ge(s["o_ready"], r * (GT + 1) + g + 1)
                if r == 0:
                    dve.reciprocal(rinv[:, :], rowsum[:, :]).then_inc(s["rinv_ready"], 1)
                else:
                    dve.tensor_tensor(total[:, :], rowsum[:, :], extra[:, :], ALU.add).then_inc(s["sum_ready"], 1)
                    dve.wait_ge(s["sum_ready"], 2 * (gg - GT) + 2)
                    dve.reciprocal(rinv[:, :], total[:, :]).then_inc(s["pb_ready"], 1)
                    dve.wait_ge(s["pb_ready"], gg - GT + 1)
                    dve.tensor_tensor(pbq[:, bass.ds(g, 1)], extra[:, :], rinv[:, :], ALU.mult)\
                        .then_inc(s["rinv_ready"], 1)

            def low_probs(r, g, k):
                gg = r * GT + g
                dve.wait_ge(s["p_hi"], 3 * gg + k + 1)
                v = slice(GRP * k, GRP * (k + 1))
                dve.tensor_tensor(pt[:, 1, v, :], ps[:, 3 + k, :].rearrange("p (c q) -> p c q", q=P),
                                  f(pt[:, 0, v, :]), ALU.subtract).then_inc(s["p_lo"], 1)

            def batch(r, b, last):
                for t in range(TILES):
                    g = TILES * b + t
                    gg = r * GT + g
                    end = last and t == TILES - 1
                    if r == 0 and t == TILES - 1 and not last:
                        mask_bias(b + 1)
                    for k in range(3):
                        if not end:
                            row_max(r, g + 1, k)
                        if k == 2 and not end:
                            neg_max(r, g + 1)
                        low_probs(r, g, k)
                    if not (last and t >= TILES - 2):
                        split_q(r, (t + 2) % TILES, g + 2)
                    if r == 0 and not last:
                        if t == 1:
                            load_stats(b + 1, 0, 5)
                        if t == 2:
                            load_stats(b + 1, 5, CH)
                    if t == 5 and not last:
                        split_ct(r, b + 1)
                    dve.wait_ge(s["o_low_ready"], gg + 1)
                    dve.wait_ge(s["rinv_ready"], gg + 1)
                    dve.wait_ge(s["o_t"], r * (GT + 1) + g + 1)
                    dve.scalar_tensor_tensor(out=o_row[:, :], in0=ps[:, 6, 0:D], scalar=rinv[:, :], in1=o_low[:, :],
                                             op0=ALU.mult, op1=ALU.add).then_inc(s["o_ready"], 1)
                    if not end:
                        sums(r, g + 1)
                    if r == 0 and not last and t >= 4:
                        scale_tokens(b + 1, t - 4)
                    if t == TILES - 1 and not last:
                        split_cx(r, b + 1)

            def run(r):
                dve.memset(prob[:, S:CH * P], 0.0)
                dve.memset(o_row[:, :], 0.0).then_inc(s["o_ready"], 1)
                split_q(r, 0, 0)
                split_q(r, 1, 1)
                if r == 0:
                    load_stats(0, 0, CH)
                    for k in range(3):
                        scale_tokens(0, k)
                    mask_bias(0)
                split_ct(r, 0)
                for k in range(3):
                    row_max(r, 0, k)
                neg_max(r, 0)
                sums(r, 0)
                split_cx(r, 0)
                with dve.Fori(0, B - 1) as b:
                    batch(r, b, False)
                batch(r, B - 1, True)

            def split_heads(i, n, slot):
                dve.wait_ge(s["oh_hi"], H * i + n + 1)
                v = (oh if i else oh0)[:, 2 * slot:2 * slot + 2, :]
                v = v.rearrange("p s (e b q) -> p s e b q", e=DH, b=B)
                for e in range(DH):
                    ins = dve.tensor_tensor(v[:, 1, e, :, :], qo_head(n)[:, e, :, :], f(v[:, 0, e, :, :]), ALU.subtract)
                ins.then_inc(s["oh_lo"], 1)

            run(0)
            drain(dve, 3)
            dve.wait_ge(s["w0_in"], 80)
            for e in range(DH):
                ins = dve.tensor_scalar(w0[:, 4 + e, :], w0[:, e, :], V["g0"][:, e:e + 1], None, ALU.mult)
            ins.then_inc(s["w0_even"], 1)
            dve.wait_ge(s["w0_mean"], 1)
            dve.tensor_copy(bias0[:, :], ps[:, 5, 0:2])
            dve.tensor_tensor(w0[:, 4:6, :], w0[:, 4:6, :], ps[:, 4:5, 0:D].to_broadcast([P, DH, D]), ALU.subtract)\
                .then_inc(s["w0_even"], 1)
            for h in range(H):
                split_heads(0, h, h % 2)
            for jc in (0, 1):
                dve.wait_ge(s["h1_hi"], 2 + jc + 1)
                dve.scalar_tensor_tensor(out=q_s[:, 2 + jc, :], in0=ps[:, jc, 0:NQ], scalar=bias0[:, jc:jc + 1],
                                         in1=f(q_s[:, jc, :]), op0=ALU.add, op1=ALU.subtract).then_inc(s["h1_lo"], 1)
            dve.wait_ge(s["y_done"], 1)
            for e in range(DH):
                dve.scalar_tensor_tensor(out=xt[:, e, :], in0=ps[:, 2 + e, 0:NQ], scalar=gate_t[:, 1:2],
                                         in1=xt[:, e, :], op0=ALU.mult, op1=ALU.add).then_inc(s["x_ready"], 1)
            drain(dve, 4)

            def norm(n, scale, offset):
                k = [LN_V * n]

                def link(ins):
                    k[0] += 1
                    ins.then_inc(s["ln_dve"], 1)

                def settled():
                    dve.wait_ge(s["ln_dve"], k[0])
                dve.wait_ge(s["ln_pe"], 2 * n + 1)
                dve.tensor_tensor(xc, xt[:, :, :], ps[:, 0:1, 0:NQ].to_broadcast([P, DH, NQ]), ALU.subtract)\
                    .then_inc(s["ln_dve"], 1)
                k[0] += 1
                settled()
                link(dve.tensor_tensor(sq, xc, xc, ALU.mult))
                dve.wait_ge(s["ln_pe"], 2 * n + 2)
                link(dve.tensor_scalar(var, ps[:, 1, 0:NQ], EPS, None, ALU.add))
                dve.wait_ge(s["ln_act"], n + 1)
                link(dve.reciprocal(dev, dev))
                settled()
                link(dve.tensor_tensor(tmp, dev, dev, ALU.mult))
                settled()
                link(dve.tensor_tensor(tmp, tmp, var, ALU.mult))
                settled()
                link(dve.tensor_scalar(tmp, tmp, -0.5, 1.5, ALU.mult, ALU.add))
                settled()
                link(dve.tensor_tensor(dev, dev, tmp, ALU.mult))
                settled()
                for e in range(DH):
                    link(dve.tensor_tensor(ht[:, e, :], xc[:, e, :], dev, ALU.mult))
                settled()
                for e in range(DH):
                    link(dve.tensor_scalar(ht[:, e, :], ht[:, e, :], scale[:, e:e + 1], offset[:, e:e + 1],
                                           ALU.mult, ALU.add))
                assert k[0] == LN_V * (n + 1)
                dve.wait_ge(s["h_split"], 2 + 2 * n + 1)
                dve.tensor_tensor(hs[:, 1, :, :], ht, f(hs[:, 0, :, :]), ALU.subtract).then_inc(s["h_split"], 1)

            def first_split(kind, i, base, n, slot, fresh):
                dve.wait_ge(s["h1_hi"], 4 + base + n + 1)
                if kind == "m":
                    if not fresh:
                        dve.wait_ge(s["m2"], M2_0 + base + n - 1)
                    dve.tensor_copy(h1[:, 2 * slot, :], g32[:, slot, :]).then_inc(s["gelu_done"], 1)
                    dve.wait_ge(s["gelu_done"], n + 1)
                    dve.tensor_tensor(h1[:, 2 * slot + 1, :], g32[:, slot, :], f(h1[:, 2 * slot, :]), ALU.subtract)\
                        .then_inc(s["h1_lo"], 1)
                else:
                    col = hb[:, 2 * (i - 1) + (kind == "o"), bass.ds(n, 1)]
                    dve.scalar_tensor_tensor(out=h1[:, 2 * slot + 1, :], in0=ps[:, slot, 0:NQ], scalar=col,
                                             in1=f(h1[:, 2 * slot, :]), op0=ALU.add, op1=ALU.subtract)\
                        .then_inc(s["h1_lo"], 1)

            def extra_key(i, n, slot):
                j = A_BASE[i] // 2 + n
                dve.wait_ge(s["dk_ready"], j + 1)
                if not isinstance(j, int) or j:
                    dve.wait_ge(s["u_ready"], j)
                dve.tensor_tensor(dk_prod, w_raw[:, slot, 0:D].rearrange("p (e k) -> p e k", e=DH),
                                  dk_raw[:, slot:slot + 1, 0:P].to_broadcast([P, DH, P]), ALU.mult).then_inc(s["prod_ready"], 1)
                dve.wait_ge(s["prod_ready"], j + 1)
                dve.tensor_reduce(u_k[:, :, bass.ds(n, 1)], dk_prod, AX.X, ALU.add).then_inc(s["u_ready"], 1)

            def extra_value(i, n, slot, fresh):
                if not fresh:
                    dve.wait_ge(s["m1"], M1_0 + O_BASE[i] + n - 1)
                dve.tensor_scalar(dv_m[0:80, slot, :], dvr[:, :], hsel[0:80, bass.ds(n, 1)], None, ALU.mult)\
                    .then_inc(s["dv_ready"], 1)

            def products(kind, i, steps, base):
                def group(m, first, last):
                    for slot in range(NS):
                        n = NS * m + slot
                        if kind == "o" and not (last and slot >= NS - 2):
                            split_heads(i, n + 2, slot % 2)
                            extra_value(i, n + 2, slot % 2, False)
                        if not (last and slot == NS - 1):
                            if kind == "a":
                                extra_key(i, n + 1, (slot + 1) % NS)
                            first_split(kind, i, base, n + 1, (slot + 1) % 2, first and slot == 0)
                        if kind == "a":
                            dve.wait_ge(s["m2"], M2_0 + base + n + 1)
                            q_back(n, 3 + 2 * (slot % 2), SCALE)
                if kind == "o":
                    for n in (0, 1):
                        split_heads(i, n, n)
                        extra_value(i, n, n, True)
                if kind == "a":
                    extra_key(i, 0, 0)
                first_split(kind, i, base, 0, 0, True)
                groups(dve, steps, group)

            def add_output(bias, base, steps):
                dve.wait_ge(s["m2"], M2_0 + base + steps)
                for e in range(DH):
                    dve.scalar_tensor_tensor(out=xt[:, e, :], in0=ps[:, 6 + e, 0:NQ], scalar=bias[:, e:e + 1],
                                             in1=xt[:, e, :], op0=ALU.add, op1=ALU.add).then_inc(s["x_ready"], 1)

            for i in (1, 2):
                norm(i - 1, V[f"s{i}"], V[f"o{i}"])
                products("a", i, H, A_BASE[i])
                sd = 6 * (i - 1)
                dve.wait_ge(s["small_in"], 144 * (i - 1) + 48)
                dve.tensor_tensor(cb[:, 3 * P:4 * P], cb[:, P:2 * P], cb[:, 2 * P:3 * P], ALU.subtract)\
                    .then_inc(s["fix_v"], 1)
                dve.wait_ge(s["fix_v"], 9 * (i - 1) + 1)
                dve.tensor_tensor(cb[:, 3 * P:4 * P], cb[:, 3 * P:4 * P], cb[:, 0:P], ALU.mult).then_inc(s["fix_v"], 1)
                dve.wait_ge(s["fix_v"], 9 * (i - 1) + 2)
                dve.tensor_reduce(cbv[:, :], cb[:, 3 * P:4 * P], AX.X, ALU.add).then_inc(s["small_dve"], 1)
                dve.wait_ge(s["small_dve"], sd + 1)
                dve.wait_ge(s["small_pe"], 3 * (i - 1) + 1)
                dve.tensor_scalar(lb_s[:, :], ps[0:H, 2, 0:NQ], cbv[:, :], SCALE, ALU.add, ALU.mult)\
                    .then_inc(s["small_dve"], 1)
                dve.wait_ge(s["small_pe"], 3 * (i - 1) + 2)
                dve.tensor_copy(lbq[:, :], ps[:, 3, 0:GT]).then_inc(s["small_dve"], 1)
                dve.wait_ge(s["small_dve"], sd + 3)
                drain(dve, 3 * i + 2)
                run(i)
                drain(dve, 3 * i + 3)
                for v in (dv, dv2, pb_f):
                    dve.memset(v, 0.0).then_inc(s["fix_v"], 1)
                dve.wait_ge(s["fix_v"], 9 * (i - 1) + 5)
                dve.wait_ge(s["small_pe"], 3 * (i - 1) + 3)
                dve.tensor_copy(tiles_row[:, :], ps[0:GT, 2, 0:P]).then_inc(s["small_dve"], 1)
                dve.wait_ge(s["small_in"], 144 * i)
                dve.wait_ge(s["small_dma"], 96 * i)
                dve.tensor_copy(pb_s[:, :], pb_f).then_inc(s["fix_v"], 1)
                dve.tensor_tensor(dv2, dv, dv2, ALU.subtract).then_inc(s["fix_v"], 1)
                dve.wait_ge(s["fix_v"], 9 * (i - 1) + 7)
                dve.tensor_tensor(pb_s[32:64, :], pb_f[32:64, :], f(pb_s[32:64, :]), ALU.subtract)\
                    .then_inc(s["small_dve"], 1)
                dve.tensor_copy(dv_hi[:, :], dv2).then_inc(s["fix_v"], 1)
                dve.wait_ge(s["fix_v"], 9 * (i - 1) + 8)
                dve.tensor_copy(dvr[0:64, :], f(dv_hi[0:64, :]))
                dve.tensor_tensor(dvr[64:80, :], dv2[64:80, :], f(dv_hi[64:80, :]), ALU.subtract)\
                    .then_inc(s["fix_v"], 1)
                dve.wait_ge(s["fix_v"], 9 * (i - 1) + 9)
                dve.tensor_copy(tmp16[:, :], cbv[:, :]).then_inc(s["small_dve"], 1)
                products("o", i, H, O_BASE[i])
                add_output(V[f"bo{i}"], O_BASE[i], H)
                drain(dve, 3 * i + 4)
            norm(2, V["sm"], V["om"])
            products("m", 0, F // P, M_BASE)
            add_output(V["bf2"], M_BASE, F // P)
            drain(dve, 11)


def kernel(**inputs):
    import numpy as np
    import concourse.bacc as bacc
    from concourse.bass_utils import run_bass_kernel_spmd

    x = {k: np.asarray(v) for k, v in inputs.items()}
    l0, l1 = "L0_xattn_", "L1_xattn_"

    def cols(a, n):
        return np.ascontiguousarray(a.reshape(n, -1).T)

    ctx = x["ctx_2048"]
    arrays = {
        "xt": np.ascontiguousarray(x["x"].reshape(NQ, D).T),
        "ctx": np.ascontiguousarray(ctx),
        "ctx_t": np.ascontiguousarray(ctx.transpose(0, 2, 1)),
        "mask": np.ascontiguousarray(x["mask_BxS2_bf1"]).view(np.uint8),
        "gate": x[l0 + "gate"].reshape(1),
        "wq0t": np.ascontiguousarray(x[l0 + "Wq"].T),
        "wk0": np.ascontiguousarray(x[l0 + "Wk"]),
        "wv0t": np.ascontiguousarray(x[l0 + "Wv"].T),
        "wo0t": np.ascontiguousarray(x[l0 + "Wo"].T),
        "g0row": x[l0 + "ln_gamma"],
        "g0": cols(x[l0 + "ln_gamma"], 2), "b0": cols(x[l0 + "ln_beta"], 2),
        "sm": cols(x[l1 + "ln_mlp_scale"], 2), "om": cols(x[l1 + "ln_mlp_offset"], 2),
        "fc1": np.ascontiguousarray(x[l1 + "w_fc1"]), "fc2": np.ascontiguousarray(x[l1 + "w_fc2"]),
        "bf1": cols(x[l1 + "b_fc1"], 8), "bf2": cols(x[l1 + "b_fc2"], 2),
    }
    for i in (1, 2):
        arrays.update({
            f"s{i}": cols(x[f"{l1}ln{i}_scale"], 2), f"o{i}": cols(x[f"{l1}ln{i}_offset"], 2),
            f"wq{i}": np.ascontiguousarray(x[f"{l1}wq{i}"]),
            f"wk{i}": np.ascontiguousarray(x[f"{l1}wk{i}"].T),
            f"wv{i}": np.ascontiguousarray(x[f"{l1}wv{i}"]),
            f"wo{i}": np.ascontiguousarray(x[f"{l1}wo{i}"]),
            f"bq{i}": cols(x[f"{l1}bq{i}"], H), f"bv{i}": cols(x[f"{l1}bv{i}"], H),
            f"bq{i}h": x[f"{l1}bq{i}"].reshape(H, K), f"bv{i}h": x[f"{l1}bv{i}"].reshape(H, K),
            f"bk{i}": x[f"{l1}bk{i}"].reshape(H, K),
            f"biask{i}": x[f"{l1}bias_k{i}"].reshape(H, K), f"biasv{i}": x[f"{l1}bias_v{i}"].reshape(H, K),
            f"bo{i}": cols(x[f"{l1}bo{i}"], 2),
        })
    nc = bacc.Bacc("TRN2", target_bir_lowering=False, num_devices=1)
    io = {}
    for name, a in arrays.items():
        io[name] = nc.dram_tensor(f"in_{name}", a.shape, mybir.dt.from_np(a.dtype), kind="ExternalInput").ap()
    io["out"] = nc.dram_tensor("out_yt", (D, NQ), F32, kind="ExternalOutput").ap()
    io["lb_d"] = nc.dram_tensor("lb_scratch", (B * ROWS,), F32).ap()
    io["pb_d"] = nc.dram_tensor("pb_scratch", (B * ROWS,), F32).ap()
    io["st_d"] = nc.dram_tensor("stat_scratch", (CH, P), F32).ap()
    build(nc, io)
    r = run_bass_kernel_spmd(nc, [{f"in_{n}": a for n, a in arrays.items()}], core_ids=[0])
    return np.ascontiguousarray(r.results[0]["out_yt"].T).reshape(B, TQ, D)
```

```python
from contextlib import ExitStack

import concourse.bass as bass
from concourse import mybir

F32 = mybir.dt.float32
F32R = mybir.dt.float32r
U8 = mybir.dt.uint8
ALU = mybir.AluOpType
ACT = mybir.ActivationFunctionType
AX = mybir.AxisListType

P = 128
B = 8
TQ = 56
D = 256
DH = D // P
S = 1500
H = 16
HD0 = D // H
K = 128
NQ = B * TQ
ROWS = H * TQ
TILES = ROWS // P
GT = B * TILES
CH = -(-S // P)
TAIL = S - (CH - 1) * P
SB = S // 3
GRP = CH // 3
F = 1024
EPS = 1e-5
QC = 2 * TQ
NS = 4
PAD = P
QBUF = [t % 2 if t < TILES - 1 else 2 for t in range(TILES)]
HPC = P // HD0


def build(nc, io):
    with ExitStack() as ctx:
        def sb(name, shape, dt=F32):
            return ctx.enter_context(nc.sbuf_tensor(name, shape, dt))

        def sem(name):
            return ctx.enter_context(nc.semaphore(name))

        ps = ctx.enter_context(nc.psum_tensor("ps", [P, 8, 512], F32))

        qo = sb("qo", [P, DH, PAD + B * ROWS])
        xt = sb("xt", [P, DH, NQ])
        raw_t = sb("raw_t", [P, DH, S])
        raw = sb("raw", [P, CH, D])
        ct = sb("ct", [P, 2, DH, S], F32R)
        cx = sb("cx", [P, CH, 2 * D], F32R)
        ident = sb("ident", [P, P])
        mean_w = sb("mean_w", [P, P])
        head_rows = sb("head_rows", [P, HPC, 1])
        spare = sb("spare", [P, NS, 2 * P])
        vec = sb("vec", [P, 64])
        gate_t = sb("gate_t", [P, 2])
        AR = 6144
        ar = sb("ar", [P, AR])
        RR = 7936
        rr = sb("rr", [P, RR], F32R)
        mx4 = sb("mx4", [P, 4])
        negm = sb("negm", [P, 1])
        rowsum = sb("rowsum", [P, 1])
        extra = sb("extra", [P, 1])
        total = sb("total", [P, 1])
        rinv = sb("rinv", [P, 1])
        lbq = sb("lbq", [P, GT])
        pbq = sb("pbq", [P, GT])
        o_low = sb("o_low", [P, D])
        o_row = sb("o_row", [P, D])
        bn = sb("bn", [P, CH, 6])
        mv = sb("mv", [P, 2, CH])
        mv_row = sb("mv_row", [CH, P])
        wsum = sb("wsum", [P, 2])
        bias0 = sb("bias0", [P, 2])
        mhalf = sb("mhalf", [P, CH])

        def at(t, off, *shape):
            n = 1
            for s in shape:
                n *= s
            v = t[:, off:off + n]
            if len(shape) == 2:
                v = v.rearrange("p (a b) -> p a b", b=shape[1])
            if len(shape) == 3:
                v = v.rearrange("p (a b c) -> p a b c", b=shape[1], c=shape[2])
            return v

        prob = at(ar, 0, CH * P)
        mask_b = at(ar, 1536, S)
        rs_b = at(ar, 1536 + 1500, S)
        pt = at(rr, 0, 2, CH, P)
        qt = at(rr, 2 * CH * P, 6, DH, P)
        w0 = at(ar, 4536, 6, D)
        xc = at(ar, 0, DH, NQ)
        sq = at(ar, 896, DH, NQ)
        diag = at(ar, 1792, NQ // QC, QC)[0:QC]
        rs4 = at(ar, 2240, NQ // QC)[0:QC]
        ht = at(ar, 3136, DH, NQ)
        w_raw = at(ar, 4032, NS, 512)
        head_cols = spare[:, :, :].rearrange("p n (c k) -> p (n c) k", k=P)
        dk_raw = spare
        dk_prod = at(ar, 0, 2, P)
        g32 = at(ar, 0, 2, NQ)
        cx_flat = cx[:, :, :].rearrange("p c d -> p (c d)")
        w_s = at(cx_flat, 0, 2 * NS, 512)
        h1 = at(rr, 2048, 4, NQ)
        oh0 = at(cx_flat, 0, 2 * 3, DH * NQ)
        oh = at(rr, 3840, 2 * 2, DH * NQ)
        hs = at(rr, 3840, 2, DH, NQ)
        dv_m = at(rr, 3840 + 3584, 2, P)
        small = sb("small", [P, 2 * P + NQ])
        dv = small[0:80, 0:P]
        dv2 = small[0:80, P:2 * P]
        pb_f = small[0:80, 2 * P:2 * P + NQ]
        pb_s = sb("pb_s", [80, NQ], F32R)
        dvr = sb("dvr", [80, P])
        dv_hi = sb("dv_hi", [80, P], F32R)
        mask_u8 = sb("mask_u8", [P, S], U8)
        hsel = sb("hsel", [96, H])
        u_k = sb("u_k", [P, DH, H])
        cb = sb("cb", [H, 4 * P])
        cbv = sb("cbv", [H, 1])
        lb_s = sb("lb_s", [H, NQ])
        tiles_row = sb("tiles_row", [GT, P])

        NV = 0
        V = {}
        for n, w in (("g0", DH), ("b0", DH), ("s1", DH), ("o1", DH), ("s2", DH), ("o2", DH),
                     ("sm", DH), ("om", DH), ("bo1", DH), ("bo2", DH), ("bf2", DH), ("bf1", 8)):
            V[n] = vec[:, NV:NV + w]
            NV += w
        hb = sb("hb", [P, 4, H])
        gam_b = small[:, 0:D]

        names = (
            "phase",
            "const_dma", "x_in", "mask_in", "rawt_in", "raw_in", "w0_in",
            "w_in0", "w_in1", "w_in2", "w_in3", "dk_in0", "dk_in1", "dk_in2", "dk_in3", "small_in",
            "seed", "fix",
            "ct_hi", "ct_lo_v", "ct_lo_p", "cx_hi", "cx_lo_p", "cx_lo_v",
            "bn_done", "aggr_done", "std_ready", "stat_t", "stat_row", "stat_out", "stat_in", "at_p", "a_ready",
            "mask_ready",
            "q_hi", "q_lo", "scores", "red", "neg_ready", "exp_done", "sum_ready", "pb_ready", "rinv_ready",
            "tr", "p_hi", "p_lo", "pv", "o_low_ready", "o_ready", "o_t", "o_back",
            "w0_centred", "w0_hi", "w0_lo", "w0_mask", "w0_mean",
            "w_hi", "w_lo", "dk_ready", "prod_ready", "u_ready", "oh_hi", "oh_lo", "dv_ready",
            "m1", "h1_hi", "h1_lo", "gelu_done", "m2", "qe_act", "qe_dve",
            "y_done", "x_ready", "ln_pe", "ln_dve", "ln_pow", "h_hi", "h_lo", "ht_ready", "h_split",
            "small_dve", "fix_v", "small_pe", "small_dma",
            "out_done",
        )
        s = {n: sem(n) for n in names}

        W0_M = 0
        W0_S = 1024
        QT0 = 3072
        X0 = QT0 + 4 * NQ
        M2_0 = H
        M1_0 = 2 + H
        assert X0 + 4 * NQ <= RR
        LN_V = 6
        STATS_AT = 1
        N_CONST = 17
        lb_d = io["lb_d"]
        pb_d = io["pb_d"]
        st_d = io["st_d"]

        block = ctx.enter_context(nc.Block())

        def f(v):
            return v.bitcast(F32)

        def wait_apart(eng, semaphore, value):
            value = value if isinstance(value, int) else eng.to_reg(value)
            eng.wait_ge(s["phase"], 4)
            eng.wait_ge(semaphore, value)

        def groups(eng, steps, group):
            last = steps // NS - 1
            group(0, True, False)
            if last > 1:
                with eng.Fori(1, last) as m:
                    group(m, False, False)
            group(last, False, True)

        def drain(eng, k):
            eng.drain().then_inc(s["phase"], 1)
            eng.wait_ge(s["phase"], 4 * k)

        A_BASE = {1: 0, 2: 32}
        O_BASE = {1: 16, 2: 48}
        O_BASE_I = {O_BASE[1]: 1, O_BASE[2]: 2}
        M_BASE = 64
        W1 = {("a", 1): ("wq1", "wk1"), ("a", 2): ("wq2", "wk2"), ("o", 1): ("wv1", "wo1"),
              ("o", 2): ("wv2", "wo2"), ("m", 0): ("fc1", "fc2")}
        SCALE = float(K) ** -0.5
        SCALE0 = float(HD0) ** -0.5

        def qo_tile(g):
            return qo[:, :, bass.ds(PAD + g * P, P)]

        def qo_head(h):
            v = qo[:, :, PAD:PAD + B * ROWS].rearrange("p e (b r) -> p e b r", b=B)
            return v[:, :, :, bass.ds(h * TQ, TQ)]

        @block.sync
        def _(sp):
            sp.dma_start(xt[:, :, :], io["xt"].rearrange("(e p) q -> p e q", p=P)).then_inc(s["x_in"], 16)
            sp.dma_start(w0[:, 0:2, :], io["wq0t"].rearrange("(e p) q -> p e q", p=P)).then_inc(s["w0_in"], 16)
            sp.dma_start(w0[:, 2:4, :], io["wk0"].rearrange("(e p) q -> p e q", p=P)).then_inc(s["w0_in"], 16)
            sp.dma_start(gam_b[:, :], io["g0row"].partition_broadcast(P)).then_inc(s["w0_in"], 16)

            def constants():
                n_const = 1
                for name, dst in (("g0", V["g0"]), ("b0", V["b0"]), ("s1", V["s1"]), ("o1", V["o1"]),
                                  ("s2", V["s2"]), ("o2", V["o2"]), ("sm", V["sm"]), ("om", V["om"]),
                                  ("bo1", V["bo1"]), ("bo2", V["bo2"]), ("bf2", V["bf2"]), ("bf1", V["bf1"]),
                                  ("bq1", hb[:, 0, :]), ("bv1", hb[:, 1, :]), ("bq2", hb[:, 2, :]),
                                  ("bv2", hb[:, 3, :])):
                    sp.dma_start(dst, io[name]).then_inc(s["const_dma"], 16)
                    n_const += 1
                sp.dma_start(gate_t[:, 0:1], io["gate"].partition_broadcast(P)).then_inc(s["const_dma"], 16)
                assert n_const == N_CONST

            def load_context(r, b, nxt):
                bc = r * B + nxt
                src = io["ctx_t"][bass.ds(b, 1), :, :].rearrange("o (e p) t -> p (o e) t", p=P)
                body = io["ctx"][bass.ds(b, 1), 0:(CH - 1) * P, :].rearrange("o (c p) d -> p (o c) d", p=P)
                tail = io["ctx"][bass.ds(b, 1), (CH - 1) * P:S, :].rearrange("o p d -> p o d")
                wait_apart(sp, s["ct_hi"], 3 * bc)
                wait_apart(sp, s["ct_lo_v"], 2 * bc)
                wait_apart(sp, s["ct_lo_p"], bc)
                sp.dma_start(raw_t[:, :, :], src).then_inc(s["rawt_in"], 16)
                wait_apart(sp, s["cx_hi"], 3 * bc)
                wait_apart(sp, s["cx_lo_p"], 2 * bc)
                wait_apart(sp, s["cx_lo_v"], bc)
                sp.dma_start(raw[:, 0:CH - 1, :], body).then_inc(s["raw_in"], 16)
                sp.dma_start(raw[0:TAIL, CH - 1:CH, :], tail).then_inc(s["raw_in"], 16)

            def token_stats(b):
                wait_apart(sp, s["stat_row"], b + 1)
                sp.dma_start(st_d, mv_row[:, :]).then_inc(s["stat_out"], 16)
                wait_apart(sp, s["stat_out"], 16 * (b + 1))
                flat = st_d.rearrange("c p -> (c p)")
                wait_apart(sp, s["at_p"], 2 * b)
                sp.dma_start(rs_b, flat[0:S].partition_broadcast(P)).then_inc(s["stat_in"], 16)

            def load_mask(b):
                src = io["mask"][bass.ds(b, 1), :].rearrange("o t -> (o t)").partition_broadcast(P)
                if not isinstance(b, int):
                    wait_apart(sp, s["mask_ready"], b)
                sp.dma_start(mask_u8[:, :], src)\
                    .then_inc(s["mask_in"], 16)

            sp.wait_ge(s["seed"], 1)
            load_context(0, 0, 0)
            constants()
            load_mask(0)
            token_stats(0)
            sp.wait_ge(s["phase"], 8)
            sp.dma_start(w0[:, 0:2, :], io["wv0t"].rearrange("(e p) q -> p e q", p=P)).then_inc(s["w0_in"], 16)
            sp.dma_start(w0[:, 2:4, :], io["wo0t"].rearrange("(e p) q -> p e q", p=P)).then_inc(s["w0_in"], 16)
            with sp.Fori(0, B - 1) as b:
                load_mask(b + 1)
                load_context(0, b + 1, b + 1)
                token_stats(b + 1)

            def step_weights(kind, i, n, base, slot, fresh):
                first, second = W1[(kind, i)]
                w0 = io[first].rearrange("(e p) k -> p e k", p=P)[:, :, bass.ds(n * P, P)]
                w1 = io[second][bass.ds(n * P, P), :]
                if kind == "a":
                    rows = [io[f"{name}{i}"].rearrange("h k -> (h k)")[bass.ds(n * P, P)].partition_broadcast(P)
                            for name in ("biask", "bk")]
                if not fresh:
                    wait_apart(sp, s["w_hi"], base + n - NS + 1)
                    wait_apart(sp, s["w_lo"], base + n - NS + 1)
                if not fresh and kind == "a" or kind == "o":
                    wait_apart(sp, s["prod_ready"], A_BASE[i] // 2 + (n - NS + 1 if kind == "a" else H))
                sp.dma_start(w_raw[:, slot, 0:D].rearrange("p (e k) -> p e k", e=DH), w0)\
                    .then_inc(s[f"w_in{slot}"], 16)
                sp.dma_start(w_raw[:, slot, D:2 * D], w1).then_inc(s[f"w_in{slot}"], 16)
                if kind == "a":
                    for c in (0, 1):
                        sp.dma_start(dk_raw[:, slot, c * P:(c + 1) * P], rows[c]).then_inc(s[f"dk_in{slot}"], 16)

            def first_weights(kind, i, base):
                for n in range(NS):
                    step_weights(kind, i, n, base, n, base == 0)

            def weights(kind, i, steps, base):
                with sp.Fori(1, steps // NS) as m:
                    for slot in range(NS):
                        step_weights(kind, i, NS * m + slot, base, slot, False)

            load_context(1, 0, 0)
            sp.wait_ge(s["w0_lo"], 4)
            for i in (1, 2):
                first_weights("a", i, A_BASE[i])
                for n, name in enumerate((f"bq{i}h", f"biask{i}", f"bk{i}")):
                    sp.dma_start(cb[:, n * P:(n + 1) * P], io[name]).then_inc(s["small_in"], 16)
                weights("a", i, H, A_BASE[i])
                sp.wait_ge(s["small_dve"], 5 * (i - 1) + 2)
                sp.dma_start(lb_d.rearrange("(b h q) -> h b q", b=B, h=H),
                             lb_s[:, :].rearrange("h (b q) -> h b q", b=B)).then_inc(s["small_dma"], 16)
                sp.wait_ge(s["small_dma"], 96 * (i - 1) + 16)
                sp.dma_start(tiles_row[:, :], lb_d.rearrange("(g p) -> g p", p=P)).then_inc(s["small_dma"], 16)
                first_weights("o", i, O_BASE[i])
                sp.wait_ge(s["fix_v"], 9 * (i - 1) + 5)
                for p0 in (0, 32, 64):
                    sp.dma_start(dv[p0:p0 + H, :], io[f"biasv{i}"]).then_inc(s["small_in"], 16)
                    sp.dma_start(dv2[p0:p0 + H, :], io[f"bv{i}h"]).then_inc(s["small_in"], 16)
                with sp.Fori(0, B - 1) as b:
                    load_context(i, b + 1, b + 1)
                if i == 1:
                    load_context(2, 0, 0)
                sp.wait_ge(s["phase"], 4 * (3 * i + 3))
                sp.wait_ge(s["small_dve"], 5 * (i - 1) + 4)
                sp.dma_start(pb_d.rearrange("(g p) -> g p", p=P), tiles_row[:, :]).then_inc(s["small_dma"], 16)
                sp.wait_ge(s["small_dma"], 96 * (i - 1) + 48)
                for p0 in (0, 32, 64):
                    sp.dma_start(pb_f[p0:p0 + H, :].rearrange("h (b q) -> h b q", b=B),
                                 pb_d.rearrange("(b h q) -> h b q", b=B, h=H)).then_inc(s["small_dma"], 16)
                weights("o", i, H, O_BASE[i])
                sp.wait_ge(s["phase"], 4 * (3 * i + 4))
            first_weights("m", 0, M_BASE)
            weights("m", 0, F // P, M_BASE)
            for e in range(DH):
                sp.wait_ge(s["x_ready"], 3 * DH + e + 1)
                sp.dma_start(io["out"][e * P:(e + 1) * P, :], xt[:, e, :]).then_inc(s["out_done"], 16)
            sp.wait_ge(s["out_done"], 16 * DH)

        @block.gpsimd
        def _(pool):
            pool.memset(raw[:, CH - 1, :], 0.0).then_inc(s["seed"], 1)
            for t, v in ((ident[:, :], 0.0), (head_rows[:, :, 0], 1.0), (head_cols[:, :, :], 0.0),
                         (mean_w[:, :], 1.0 / D), (mhalf[:, :], -0.5), (o_row[:, :], 0.0), (mv[:, :, :], 1.0)):
                pool.memset(t, v).then_inc(s["fix"], 1)
            pool.wait_ge(s["fix"], 7)
            pool.affine_select(out=ident[:, :], in_=ident[:, :], compare_op=ALU.not_equal, fill=1.0,
                               base=0, pattern=[[-1, P]], channel_multiplier=1).then_inc(s["fix"], 1)
            pool.affine_select(out=head_rows[:, :, 0], in_=head_rows[:, :, 0], compare_op=ALU.is_ge, fill=0.0,
                               base=0, pattern=[[-HD0, HPC]], channel_multiplier=1).then_inc(s["fix"], 1)
            pool.wait_ge(s["fix"], 9)
            pool.affine_select(out=head_rows[:, :, 0], in_=head_rows[:, :, 0], compare_op=ALU.is_ge, fill=0.0,
                               base=HD0 - 1, pattern=[[HD0, HPC]], channel_multiplier=-1).then_inc(s["fix"], 1)
            for m in range(HPC):
                pool.memset(head_cols[:, m, m * HD0:(m + 1) * HD0], 1.0).then_inc(s["fix"], 1)
            drain(pool, 1)

            def low0(n, src):
                pool.wait_ge(s["w0_hi"], n + 1)
                v = at(rr, W0_S, 4, 2 * D)[:, 2 * (n % 2):2 * (n % 2) + 2, :]
                pool.tensor_tensor(v[:, :, D:2 * D], src, f(v[:, :, 0:D]), ALU.subtract).then_inc(s["w0_lo"], 1)

            def norm_context(b):
                wait_apart(pool, s["aggr_done"], b + 1)
                pool.tensor_scalar(mv[:, 1, :], mv[:, 1, :], EPS, None, ALU.add).then_inc(s["std_ready"], 1)
                pool.wait_ge(s["std_ready"], 2 * b + 1)
                pool.tensor_tensor(mv[:, 1, :], mv[:, 1, :], mhalf[:, :], ALU.pow).then_inc(s["std_ready"], 1)
                pool.wait_ge(s["stat_in"], 16 * (b + 1))
                pool.wait_ge(s["rawt_in"], 16 * (b + 1))
                for e in range(DH):
                    pool.tensor_tensor(raw_t[:, e, :], raw_t[:, e, :], rs_b, ALU.mult).then_inc(s["at_p"], 1)

            low0(0, w0[:, 0:2, :])
            low0(1, w0[:, 2:4, :])
            norm_context(0)
            drain(pool, 2)

            def split_ct(r, b):
                bc = r * B + b
                pool.wait_ge(s["ct_hi"], 3 * bc + 2)
                v = slice(SB, 2 * SB)
                pool.tensor_tensor(ct[:, 1, :, v], raw_t[:, :, v], f(ct[:, 0, :, v]), ALU.subtract)\
                    .then_inc(s["ct_lo_p"], 1)

            def split_cx(r, b):
                bc = r * B + b
                for k in (0, 2):
                    v = slice(GRP * k, GRP * (k + 1))
                    pool.wait_ge(s["cx_hi"], 3 * bc + k + 1)
                    pool.tensor_tensor(cx[:, v, D:2 * D], raw[:, v, :], f(cx[:, v, 0:D]), ALU.subtract)\
                        .then_inc(s["cx_lo_p"], 1)

            def run(r):
                if r == 0:
                    split_ct(r, 0)
                split_cx(r, 0)
                with pool.Fori(0, B - 1) as b:
                    if r == 0:
                        norm_context(b + 1)
                    split_ct(r, b + 1)
                    split_cx(r, b + 1)

            def norm(n):
                pool.wait_ge(s["ln_dve"], LN_V * n + 3)
                pool.tensor_tensor(rs4, rs4, mhalf[0:QC, 0:NQ // QC], ALU.pow).then_inc(s["ln_pow"], 1)

            def whole_h(n, offset):
                for e in range(DH):
                    pool.wait_ge(s["h_lo"], DH * n + e + 1)
                    pool.tensor_scalar(ht[:, e, :], ht[:, e, :], offset[:, e:e + 1], None, ALU.add)\
                        .then_inc(s["ht_ready"], 1)

            def step_splits(kind, i, steps, base):
                def step(n, m, slot):
                    pool.wait_ge(s["w_hi"], base + n + 1)
                    pool.tensor_tensor(w_s[:, 2 * slot + 1, :], w_raw[:, slot, :], f(w_s[:, 2 * slot, :]),
                                       ALU.subtract).then_inc(s["w_lo"], 1)
                    if kind == "a":
                        pool.wait_ge(s[f"dk_in{slot}"], 32 * (A_BASE[i] // 2 // NS + m + 1))
                        pool.tensor_tensor(dk_raw[:, slot, 0:P], dk_raw[:, slot, 0:P], dk_raw[:, slot, P:2 * P],
                                           ALU.subtract).then_inc(s["dk_ready"], 1)
                if kind != "o":
                    norm(i - 1 if kind == "a" else 2)
                for n in range(NS - 1):
                    step(n, 0, n)
                if kind == "a":
                    split_ct(i, 0)
                step(NS - 1, 0, NS - 1)
                if kind == "a":
                    whole_h(i - 1, V[f"o{i}"])
                with pool.Fori(1, steps // NS) as m:
                    for slot in range(NS):
                        step(NS * m + slot, m, slot)

            run(0)
            drain(pool, 3)
            low0(2, w0[:, 4:6, :])
            pool.wait_ge(s["w0_lo"], 3)
            for jc in (0, 1):
                for n in range(HPC):
                    if 8 * jc + n >= 2:
                        pool.wait_ge(s["m1"], M1_0 - 16 + 8 * jc + n - 1)
                    src = f(at(rr, W0_S, 4, D))[:, :, P * jc:P * (jc + 1)]
                    pool.tensor_tensor(at(rr, W0_M + 512 * (n % 2), 4, P), src,
                                       head_cols[:, n:n + 1, :].to_broadcast([P, 4, P]), ALU.mult)\
                        .then_inc(s["w0_mask"], 1)
            low0(3, w0[:, 2:4, :])
            drain(pool, 4)
            for i in (1, 2):
                step_splits("a", i, H, A_BASE[i])
                drain(pool, 3 * i + 2)
                run(i)
                drain(pool, 3 * i + 3)
                step_splits("o", i, H, O_BASE[i])
                drain(pool, 3 * i + 4)
            step_splits("m", 0, F // P, M_BASE)
            drain(pool, 11)

        def three(eng, out, w_hi, w_lo, x_hi, x_lo, start, stop):
            eng.matmul(out, w_hi, x_hi, start=start, stop=False, skip_group_check=True)
            eng.matmul(out, w_hi, x_lo, start=False, stop=False, skip_group_check=True)
            return eng.matmul(out, w_lo, x_hi, start=False, stop=stop, skip_group_check=True)

        @block.tensor
        def _(pe):
            drain(pe, 1)
            def turn_stats(b, outputs):
                pe.wait_ge(s["std_ready"], 2 * b + 2)
                if outputs is not None:
                    pe.wait_ge(s["o_back"], outputs + 1)
                pe.transpose(ps[0:CH, 7, 256:256 + P], mv[:, 1, :], ident[:, :])\
                    .then_inc(s["stat_t"], 1)

            wq = at(rr, W0_S, 2, 2 * D)
            xs = at(rr, X0, 2, DH * NQ)
            pe.wait_ge(s["w0_lo"], 1)
            pe.wait_ge(s["h_split"], 2)
            for jc in range(2):
                for e in range(DH):
                    mm = three(pe, ps[:, jc, 0:NQ], wq[:, e, P * jc:P * jc + P], wq[:, e, D + P * jc:D + P * jc + P],
                               xs[:, 0, e * NQ:(e + 1) * NQ], xs[:, 1, e * NQ:(e + 1) * NQ], e == 0, e == DH - 1)
                mm.then_inc(s["m1"], 1)
            for h in range(H):
                jc = h // HPC
                q_s = at(rr, QT0, 2, 2 * NQ)
                wm = at(rr, W0_M + 512 * (h % 2), 512)
                pe.wait_ge(s["w0_mask"], h + 1)
                pe.wait_ge(s["h1_lo"], jc + 1)
                if h >= 2:
                    pe.wait_ge(s["qe_act"], h - 1)
                    pe.wait_ge(s["qe_dve"], h - 1)
                for e in range(DH):
                    mm = three(pe, ps[:, 2 + 2 * (h % 2) + e, 0:NQ], wm[:, e * P:e * P + P],
                               wm[:, D + e * P:D + e * P + P], q_s[:, 0, jc * NQ:(jc + 1) * NQ],
                               q_s[:, 1, jc * NQ:(jc + 1) * NQ], True, True)
                mm.then_inc(s["m2"], 1)
                if h == STATS_AT:
                    turn_stats(0, None)
            drain(pe, 2)

            def scores(r, b, t, g, j):
                gg, bc = r * GT + g, r * B + b
                if j == 0:
                    pe.wait_ge(s["q_hi"], gg + 1)
                    pe.wait_ge(s["q_lo"], gg + 1)
                    if r == 0:
                        pe.wait_ge(s["red"], 3 * gg)
                    else:
                        pe.wait_ge(s["exp_done"], gg)
                if t == 0:
                    pe.wait_ge(s["ct_hi"], 3 * bc + j + 1)
                    if j == 1:
                        pe.wait_ge(s["ct_lo_p"], bc + 1)
                    else:
                        pe.wait_ge(s["ct_lo_v"], 2 * bc + 1 + j // 2)
                v = slice(SB * j, SB * (j + 1))
                q = QBUF[t]
                for e in range(DH):
                    mm = three(pe, ps[:, j, 0:SB], qt[:, 2 * q, e, :], qt[:, 2 * q + 1, e, :],
                               ct[:, 0, e, v], ct[:, 1, e, v], e == 0, e == DH - 1)
                mm.then_inc(s["scores"], 1)

            def transposes(r, g, k):
                gg = r * GT + g
                if k == 0:
                    pe.wait_ge(s["exp_done"], gg + 1)
                for c in range(GRP * k, GRP * (k + 1)):
                    mm = pe.transpose(ps[:, 3 + k, (c % GRP) * P:(c % GRP) * P + P], prob[:, c * P:(c + 1) * P],
                                      ident[:, :])
                mm.then_inc(s["tr"], 1)

            def turn_output(r, g):
                n = r * (GT + 1) + g + 1
                pe.wait_ge(s["o_ready"], n + 1)
                pe.wait_ge(s["o_back"], n + 1)
                for e in range(DH):
                    mm = pe.transpose(ps[:, 7, e * P:(e + 1) * P], o_row[:, e * P:(e + 1) * P], ident[:, :])
                mm.then_inc(s["o_t"], 1)

            def weighted(r, b, t, g):
                gg, bc = r * GT + g, r * B + b
                pe.wait_ge(s["o_ready"], r * (GT + 1) + g + 1)
                for c in range(CH):
                    n = P if c < CH - 1 else TAIL
                    if c % GRP == 0:
                        pe.wait_ge(s["p_hi"], 3 * gg + c // GRP + 1)
                        pe.wait_ge(s["p_lo"], 3 * gg + c // GRP + 1)
                        if t == 0:
                            pe.wait_ge(s["cx_hi"], 3 * bc + c // GRP + 1)
                            if c // GRP == 1:
                                pe.wait_ge(s["cx_lo_v"], bc + 1)
                            else:
                                pe.wait_ge(s["cx_lo_p"], 2 * bc + 1 + c // GRP // 2)
                    pe.matmul(ps[:, 6, :], pt[0:n, 0, c, :], cx[0:n, c, :], start=c == 0, stop=False,
                              skip_group_check=True)
                    mm = pe.matmul(ps[:, 6, 0:D], pt[0:n, 1, c, :], cx[0:n, c, 0:D], start=False,
                                   stop=c == CH - 1, skip_group_check=True)
                mm.then_inc(s["pv"], 1)

            def batch(r, b, last):
                for t in range(TILES):
                    g = TILES * b + t
                    nb, nt = (b, t + 1) if t < TILES - 1 else (b + 1, 0)
                    for k in range(3):
                        if not (last and t == TILES - 1):
                            scores(r, nb, nt, g + 1, k)
                        transposes(r, g, k)
                    if r == 0 and t == 3 and not last:
                        turn_stats(b + 1, r * (GT + 1) + g)
                    turn_output(r, g - 1)
                    weighted(r, b, t, g)

            def run(r):
                if r:
                    pe.wait_ge(s["u_ready"], H * r)
                    pe.wait_ge(s["ht_ready"], DH * r)
                    for e in range(DH):
                        mm = pe.matmul(ps[0:H, 3, 0:NQ], u_k[:, e, :], ht[:, e, :], start=e == 0, stop=e == DH - 1)
                    mm.then_inc(s["small_pe"], 1)
                for j in range(3):
                    scores(r, 0, 0, 0, j)
                if r:
                    pe.wait_ge(s["small_dma"], 96 * (r - 1) + 32)
                    pe.transpose(ps[:, 3, 0:GT], tiles_row[:, :], ident[0:GT, 0:GT]).then_inc(s["small_pe"], 1)
                with pe.Fori(0, B - 1) as b:
                    batch(r, b, False)
                batch(r, B - 1, True)
                turn_output(r, GT - 1)

            run(0)
            drain(pe, 3)
            pe.wait_ge(s["w0_centred"], 4)
            for e in range(DH):
                pe.matmul(ps[:, 4, 0:D], mean_w[:, :], w0[:, 4 + e, :], start=e == 0, stop=e == DH - 1)
            for jc in (0, 1):
                for e in range(DH):
                    mm = pe.matmul(ps[:, 5, jc:jc + 1], w0[:, e, P * jc:P * jc + P], V["b0"][:, e:e + 1],
                                   start=e == 0, stop=e == DH - 1)
            mm.then_inc(s["w0_mean"], 1)
            for h in range(H):
                jc = h // HPC
                wm = at(rr, W0_M + 512 * (h % 2), 4, P)
                ohs = oh0[:, 2 * (h % 3):2 * (h % 3) + 2, :]
                pe.wait_ge(s["w0_mask"], H + h + 1)
                pe.wait_ge(s["oh_hi"], h + 1)
                pe.wait_ge(s["oh_lo"], h + 1)
                for e in range(DH):
                    mm = three(pe, ps[:, jc, 0:NQ], wm[:, 2 * e, :], wm[:, 2 * e + 1, :],
                               ohs[:, 0, e * NQ:(e + 1) * NQ], ohs[:, 1, e * NQ:(e + 1) * NQ],
                               h % HPC == 0 and e == 0, h % HPC == HPC - 1 and e == DH - 1)
                mm.then_inc(s["m1"], 1)
            pe.wait_ge(s["h1_lo"], 4)
            pe.wait_ge(s["w0_lo"], 4)
            wo = at(rr, W0_S + 1024, 2, 2 * D)
            o_s = at(rr, QT0, 2, 2 * NQ)
            for e in range(DH):
                for jc in (0, 1):
                    mm = three(pe, ps[:, 2 + e, 0:NQ], wo[:, jc, e * P:e * P + P], wo[:, jc, D + e * P:D + e * P + P],
                               o_s[:, 0, jc * NQ:(jc + 1) * NQ], o_s[:, 1, jc * NQ:(jc + 1) * NQ], jc == 0, jc == 1)
            mm.then_inc(s["y_done"], 1)
            drain(pe, 4)

            def norm(n):
                for e in range(DH):
                    mm = pe.matmul(ps[:, 0, 0:NQ], mean_w[:, :], xt[:, e, :], start=e == 0, stop=e == DH - 1)
                mm.then_inc(s["ln_pe"], 1)
                pe.wait_ge(s["ln_dve"], LN_V * n + 2)
                for c in range(NQ // QC):
                    for e in range(DH):
                        mm = pe.matmul(ps[0:QC, 1, c:c + 1], sq[:, e, QC * c:QC * (c + 1)], mean_w[:, 0:1],
                                       start=e == 0, stop=e == DH - 1)
                mm.then_inc(s["ln_pe"], 1)
                pe.wait_ge(s["ln_dve"], LN_V * n + 4)
                pe.matmul(ps[:, 2, 0:NQ], mean_w[0:QC, :], diag.rearrange("p c q -> p (c q)"), start=True, stop=True)\
                    .then_inc(s["ln_pe"], 1)
                pe.wait_ge(s["h_lo"], DH * (n + 1))

            def first_product(kind, base, n, slot, fresh):
                pe.wait_ge(s["w_lo"], base + n + 1)
                if not fresh:
                    pe.wait_ge(s["h1_lo"], 4 + base + n - 1)
                w = w_s[:, 2 * slot:2 * slot + 2, 0:D]
                slot %= 2
                out = ps[:, slot, 0:NQ]
                if kind == "o":
                    i = O_BASE_I[base]
                    pe.wait_ge(s["oh_hi"], H * i + n + 1)
                    pe.wait_ge(s["oh_lo"], H * i + n + 1)
                    x = oh[:, 2 * slot:2 * slot + 2, :]
                else:
                    x = hs[:, :, :, :].rearrange("p s e q -> p s (e q)")
                for e in range(DH):
                    mm = three(pe, out, w[:, 0, e * P:e * P + P], w[:, 1, e * P:e * P + P],
                               x[:, 0, e * NQ:(e + 1) * NQ], x[:, 1, e * NQ:(e + 1) * NQ], e == 0,
                               e == DH - 1 and kind != "o")
                if kind != "o":
                    mm.then_inc(s["m1"], 1)

            def extra_product(i, n, slot):
                pe.wait_ge(s["dv_ready"], H * (i - 1) + n + 1)
                pe.matmul(ps[:, slot % 2, 0:NQ], dv_m[0:80, slot % 2, :], pb_s[:, :], start=False, stop=True,
                          skip_group_check=True).then_inc(s["m1"], 1)

            def second_product(kind, i, base, n, slot, first, last, fresh):
                pe.wait_ge(s["h1_lo"], 4 + base + n + 1)
                w = w_s[:, 2 * slot:2 * slot + 2, D:2 * D]
                slot %= 2
                if kind == "a" and not fresh:
                    pe.wait_ge(s["qe_act"], H * i + n - 1)
                    pe.wait_ge(s["qe_dve"], H * i + n - 1)
                for e in range(DH):
                    out = ps[:, 2 + 2 * slot + e, 0:NQ] if kind == "a" else ps[:, 6 + e, 0:NQ]
                    mm = three(pe, out, w[:, 0, e * P:e * P + P], w[:, 1, e * P:e * P + P], h1[:, 2 * slot, :],
                               h1[:, 2 * slot + 1, :], kind == "a" or first, kind == "a" or last)
                mm.then_inc(s["m2"], 1)

            def products(kind, i, steps, base):
                def group(m, first, last):
                    for slot in range(NS):
                        n = NS * m + slot
                        end = last and slot == NS - 1
                        if not end:
                            if not (kind == "o" and first and slot == 0):
                                first_product(kind, base, n + 1, (slot + 1) % NS, first and slot == 0)
                            if kind == "o":
                                extra_product(i, n + 1, (slot + 1) % NS)
                        second_product(kind, i, base, n, slot, first and slot == 0, end, first and slot < 2)
                first_product(kind, base, 0, 0, True)
                if kind == "o":
                    first_product(kind, base, 1, 1, True)
                    pe.wait_ge(s["small_dve"], 5 * i)
                    extra_product(i, 0, 0)
                groups(pe, steps, group)

            for i in (1, 2):
                norm(i - 1)
                products("a", i, H, A_BASE[i])
                drain(pe, 3 * i + 2)
                run(i)
                drain(pe, 3 * i + 3)
                pe.transpose(ps[0:GT, 2, 0:P], pbq[:, :], ident[:, :]).then_inc(s["small_pe"], 1)
                products("o", i, H, O_BASE[i])
                drain(pe, 3 * i + 4)
            norm(2)
            products("m", 0, F // P, M_BASE)
            drain(pe, 11)

        @block.scalar
        def _(act):
            drain(act, 1)
            act.wait_ge(s["x_in"], 16)
            act.activation(at(rr, X0, 2, DH * NQ)[:, 0, :], xt[:, :, :].rearrange("p e q -> p (e q)"), ACT.Copy)\
                .then_inc(s["h_split"], 1)

            def high0(n, src):
                v = at(rr, W0_S, 4, 2 * D)[:, 2 * (n % 2):2 * (n % 2) + 2, 0:D]
                act.activation(v, src, ACT.Copy).then_inc(s["w0_hi"], 1)

            act.wait_ge(s["w0_in"], 48)
            high0(0, w0[:, 0:2, :])
            act.wait_ge(s["w0_centred"], 3)
            high0(1, w0[:, 2:4, :])
            for jc in (0, 1):
                act.wait_ge(s["m1"], jc + 1)
                act.activation(at(rr, QT0, 4, NQ)[:, jc, :], ps[:, jc, 0:NQ], ACT.Copy, scale=SCALE0)\
                    .then_inc(s["h1_hi"], 1)

            def q_back(h, bank, scale, done):
                dst = qo_head(h)[:, 0, :, :]
                wait_apart(act, s["m2"], done)
                act.activation(dst, ps[:, bank, 0:NQ].rearrange("p (b q) -> p b q", b=B), ACT.Copy, scale=scale)\
                    .then_inc(s["qe_act"], 1)

            def turn_stats(b):
                act.wait_ge(s["stat_t"], b + 1)
                act.wait_ge(s["stat_out"], 16 * b)
                act.activation(mv_row[:, :], ps[0:CH, 7, 256:256 + P], ACT.Copy).then_inc(s["stat_row"], 1)

            for h in range(H):
                q_back(h, 2 + 2 * (h % 2), 1.0, h + 1)
                if h == STATS_AT:
                    turn_stats(0)
            act.wait_ge(s["const_dma"], 16 * N_CONST)
            act.activation(gate_t[:, 1:2], gate_t[:, 0:1], ACT.Tanh).then_inc(s["o_back"], 1)
            drain(act, 2)

            def split_ct(r, b, thirds):
                bc = r * B + b
                for j in thirds:
                    if r == 0:
                        act.wait_ge(s["at_p"], 2 * bc + 2)
                    else:
                        act.wait_ge(s["rawt_in"], 16 * (bc + 1))
                    v = slice(SB * j, SB * (j + 1))
                    if not isinstance(b, int):
                        act.wait_ge(s["scores"], r * 3 * GT + 3 * TILES * b - 2 + j)
                    act.activation(ct[:, 0, :, v], raw_t[:, :, v], ACT.Copy).then_inc(s["ct_hi"], 1)

            def split_cx(r, b):
                bc = r * B + b
                if r:
                    act.wait_ge(s["raw_in"], 32 * (bc + 1))
                if not isinstance(b, int):
                    act.wait_ge(s["pv"], r * GT + TILES * b)
                for k in range(3):
                    if r == 0:
                        act.wait_ge(s["a_ready"], 3 * bc + k + 1)
                    v = slice(GRP * k, GRP * (k + 1))
                    act.activation(cx[:, v, 0:D], raw[:, v, :], ACT.Copy).then_inc(s["cx_hi"], 1)

            def split_q(r, t, g):
                src = qo_tile(g)
                if not isinstance(g, int) or g >= 2:
                    wait_apart(act, s["scores"], 3 * (r * GT + g - 1))
                act.activation(qt[:, 2 * QBUF[t], :, :], src, ACT.Copy).then_inc(s["q_hi"], 1)

            def softmax(r, g):
                gg = r * GT + g
                logit = lbq[:, bass.ds(g, 1)]
                act.wait_ge(s["rinv_ready"], gg)
                wait_apart(act, s["neg_ready"], gg + 1)
                if r:
                    act.activation(extra[:, :], logit, ACT.Exp, bias=negm[:, :])
                    act.wait_ge(s["tr"], 3 * gg)
                    src = ps[:, 0:3, 0:SB]
                else:
                    src = prob[:, 0:S].rearrange("p (j t) -> p j t", j=3)
                act.activation(prob[:, 0:S].rearrange("p (j t) -> p j t", j=3), src, ACT.Exp,
                               bias=negm[:, :], accum_out=rowsum[:, :]).then_inc(s["exp_done"], 1)

            def turn_output(r, g, stats_of=None):
                n = r * (GT + 1) + g + 1
                if stats_of is not None:
                    act.wait_ge(s["o_t"], n + 1)
                    turn_stats(stats_of)
                dst = qo_tile(g)
                wait_apart(act, s["o_t"], n + 1)
                act.activation(dst,
                               ps[:, 7, 0:D].rearrange("p (e r) -> p e r", e=DH), ACT.Copy).then_inc(s["o_back"], 1)

            def batch(r, b, last):
                for t in range(TILES):
                    g = TILES * b + t
                    gg = r * GT + g
                    for k in range(3):
                        act.wait_ge(s["tr"], 3 * gg + k + 1)
                        act.activation(pt[:, 0, GRP * k:GRP * (k + 1), :],
                                       ps[:, 3 + k, :].rearrange("p (c q) -> p c q", q=P), ACT.Copy)\
                            .then_inc(s["p_hi"], 1)
                        if t == TILES - 2 and not last and k < 2:
                            split_ct(r, b + 1, (k,))
                    if not (last and t >= TILES - 2):
                        split_q(r, (t + 2) % TILES, g + 2)
                    turn_output(r, g - 1, b + 1 if r == 0 and t == 3 and not last else None)
                    if not (last and t == TILES - 1):
                        softmax(r, g + 1)
                    if t == TILES - 2 and not last:
                        split_ct(r, b + 1, (2,))
                    act.wait_ge(s["pv"], gg + 1)
                    act.wait_ge(s["rinv_ready"], gg + 1)
                    act.wait_ge(s["o_ready"], r * (GT + 1) + g + 1)
                    act.activation(o_low[:, :], ps[:, 6, D:2 * D], ACT.Copy, scale=rinv[:, :])\
                        .then_inc(s["o_low_ready"], 1)
                    if t == 6 and not last:
                        split_cx(r, b + 1)

            def run(r):
                split_q(r, 0, 0)
                split_q(r, 1, 1)
                if r == 0:
                    split_ct(r, 0, range(3))
                split_cx(r, 0)
                softmax(r, 0)
                with act.Fori(0, B - 1) as b:
                    batch(r, b, False)
                batch(r, B - 1, True)
                turn_output(r, GT - 1)

            def split_heads(i, n, slot, fresh):
                dst = (oh if i else oh0)[:, 2 * slot, :]
                src = qo_head(n)
                if not fresh:
                    wait_apart(act, s["m1"], M1_0 + O_BASE[i] + n - 1 if i else 2 + n - 2)
                act.activation(dst.rearrange("p (e b q) -> p e b q", e=DH, b=B), src, ACT.Copy)\
                    .then_inc(s["oh_hi"], 1)

            run(0)
            drain(act, 3)
            act.wait_ge(s["w0_centred"], 5)
            high0(2, w0[:, 4:6, :])
            for h in range(H):
                split_heads(0, h, h % 3, h < 3)
                if h == 0:
                    high0(3, w0[:, 2:4, :])
            for jc in (0, 1):
                act.wait_ge(s["m1"], 2 + HPC * (jc + 1))
                act.activation(at(rr, QT0, 4, NQ)[:, jc, :], ps[:, jc, 0:NQ], ACT.Identity, bias=bias0[:, jc:jc + 1])\
                    .then_inc(s["h1_hi"], 1)
            drain(act, 4)

            def norm(n, offset):
                for e in range(DH):
                    act.wait_ge(s["ln_dve"], LN_V * n + 5 + e)
                    act.activation(hs[:, 0, e, :], ht[:, e, :], ACT.Identity, bias=offset[:, e:e + 1])\
                        .then_inc(s["h_hi"], 1)

            def first_split(kind, i, base, n, slot, fresh):
                src = ps[:, slot, 0:NQ]
                if kind == "m":
                    if not fresh:
                        act.wait_ge(s["h1_lo"], 4 + base + n - 1)
                    col = V["bf1"][:, bass.ds(n, 1)]
                    wait_apart(act, s["m1"], M1_0 + base + n + 1)
                    act.activation(g32[:, slot, :], src, ACT.Gelu, bias=col)\
                        .then_inc(s["h1_hi"], 1)
                else:
                    if not fresh:
                        act.wait_ge(s["m2"], M2_0 + base + n - 1)
                    col = hb[:, 2 * (i - 1) + (kind == "o"), bass.ds(n, 1)]
                    wait_apart(act, s["m1"], M1_0 + base + n + 1)
                    act.activation(h1[:, 2 * slot, :], src, ACT.Identity, bias=col).then_inc(s["h1_hi"], 1)

            def products(kind, i, steps, base):
                def high_weights(n, m, slot):
                    act.wait_ge(s[f"w_in{slot}"], 32 * (base // NS + m + 1))
                    if not isinstance(n, int) or n >= NS:
                        act.wait_ge(s["m2"], M2_0 + base + n - NS + 1)
                    act.activation(w_s[:, 2 * slot, :], w_raw[:, slot, :], ACT.Copy).then_inc(s["w_hi"], 1)

                def group(m, first, last):
                    for slot in range(NS):
                        n = NS * m + slot
                        if kind == "o" and not (last and slot >= NS - 2):
                            split_heads(i, n + 2, slot % 2, False)
                        if not (last and slot == NS - 1):
                            first_split(kind, i, base, n + 1, (slot + 1) % 2, first and slot == 0)
                        if not (last and slot):
                            high_weights(n + NS - 1, m + (1 if slot else 0), (slot + NS - 1) % NS)
                        if kind == "a":
                            q_back(n, 2 + 2 * (slot % 2), SCALE, M2_0 + base + n + 1)
                for n in range(NS - 1):
                    high_weights(n, 0, n)
                if kind == "a":
                    split_ct(i, 0, range(3))
                    norm(i - 1, V[f"o{i}"])
                if kind == "m":
                    act.activation(gate_t[:, 0:1], gate_t[:, 0:1], ACT.Gelu)
                    norm(2, V["om"])
                if kind == "o":
                    split_heads(i, 0, 0, True)
                    split_heads(i, 1, 1, True)
                first_split(kind, i, base, 0, 0, True)
                groups(act, steps, group)

            for i in (1, 2):
                products("a", i, H, A_BASE[i])
                drain(act, 3 * i + 2)
                run(i)
                drain(act, 3 * i + 3)
                products("o", i, H, O_BASE[i])
                drain(act, 3 * i + 4)
            products("m", 0, F // P, M_BASE)
            drain(act, 11)

        @block.vector
        def _(dve):
            drain(dve, 1)
            for p0 in (0, 32, 64):
                dve.tensor_copy(hsel[p0:p0 + 32, :], ident[p0:p0 + 32, p0:p0 + H])
            wk = w0[:, 2:4, :]
            dve.wait_ge(s["w0_in"], 48)
            dve.tensor_tensor(wk, wk, gam_b[:, :].rearrange("p (o d) -> p o d", o=1).to_broadcast([P, 2, D]), ALU.mult)\
                .then_inc(s["w0_centred"], 1)
            dve.wait_ge(s["w0_centred"], 1)
            dve.tensor_reduce(wsum[:, :], wk, AX.X, ALU.add).then_inc(s["w0_centred"], 1)
            dve.wait_ge(s["w0_centred"], 2)
            dve.scalar_tensor_tensor(out=wk, in0=wsum[:, :].rearrange("p (e o) -> p e o", o=1).to_broadcast([P, 2, D]),
                                     scalar=-1.0 / D, in1=wk, op0=ALU.mult, op1=ALU.add).then_inc(s["w0_centred"], 1)
            x_s = at(rr, X0, 2, DH * NQ)
            dve.wait_ge(s["h_split"], 1)
            dve.tensor_tensor(x_s[:, 1, :], xt[:, :, :].rearrange("p e q -> p (e q)"), f(x_s[:, 0, :]), ALU.subtract)\
                .then_inc(s["h_split"], 1)
            q_s = at(rr, QT0, 4, NQ)

            def mask_rows(h):
                dve.tensor_scalar(at(rr, W0_M + 512 * (h % 2), 512), f(at(rr, W0_S + 1024 + 512 * (h // HPC), 512)),
                                  head_rows[:, h % HPC, :], None, ALU.mult).then_inc(s["w0_mask"], 1)

            dve.wait_ge(s["w0_lo"], 2)
            mask_rows(0)
            mask_rows(1)
            for jc in (0, 1):
                dve.wait_ge(s["h1_hi"], jc + 1)
                dve.scalar_tensor_tensor(out=q_s[:, 2 + jc, :], in0=ps[:, jc, 0:NQ], scalar=SCALE0,
                                         in1=f(q_s[:, jc, :]), op0=ALU.mult, op1=ALU.subtract)\
                    .then_inc(s["h1_lo"], 1)

            def load_stats(b, c0, c1):
                if c0 == 0:
                    dve.wait_ge(s["raw_in"], 32 * (b + 1))
                    dve.wait_ge(s["stat_t"], b)
                for c in range(c0, c1):
                    ins = dve.bn_stats(bn[:, c, :], raw[:, c, :])
                if c1 == CH:
                    ins.then_inc(s["bn_done"], 1)
                    wait_apart(dve, s["bn_done"], b + 1)
                    for c in range(CH):
                        ins = dve.bn_aggr(mv[:, :, c], bn[:, c, :])
                    ins.then_inc(s["aggr_done"], 1)

            load_stats(0, 0, CH)

            def q_back(h, bank, scale):
                dve.tensor_scalar(qo_head(h)[:, 1, :, :], ps[:, bank, 0:NQ].rearrange("p (b q) -> p b q", b=B),
                                  scale, None, ALU.mult).then_inc(s["qe_dve"], 1)

            for h in range(H):
                dve.wait_ge(s["m2"], h + 1)
                if h < H - 2:
                    mask_rows(h + 2)
                q_back(h, 3 + 2 * (h % 2), 1.0)
            drain(dve, 2)

            def scale_tokens(b, k):
                if k == 0:
                    dve.wait_ge(s["std_ready"], 2 * b + 2)
                for c in range(GRP * k, GRP * (k + 1)):
                    ins = dve.tensor_scalar(raw[:, c, :], raw[:, c, :], mv[:, 1, c:c + 1], None, ALU.mult)
                ins.then_inc(s["a_ready"], 1)

            def mask_bias(b):
                dve.wait_ge(s["mask_in"], 16 * (b + 1))
                dve.tensor_scalar(mask_b, mask_u8[:, :], -1.0, 3e38, ALU.add, ALU.mult).then_inc(s["mask_ready"], 1)
                dve.wait_ge(s["mask_ready"], b + 1)

            def split_ct(r, b):
                bc = r * B + b
                for j in (0, 2):
                    v = slice(SB * j, SB * (j + 1))
                    dve.wait_ge(s["ct_hi"], 3 * bc + j + 1)
                    dve.tensor_tensor(ct[:, 1, :, v], raw_t[:, :, v], f(ct[:, 0, :, v]), ALU.subtract)\
                        .then_inc(s["ct_lo_v"], 1)

            def split_cx(r, b):
                v = slice(GRP, 2 * GRP)
                dve.wait_ge(s["cx_hi"], 3 * (r * B + b) + 2)
                dve.tensor_tensor(cx[:, v, D:2 * D], raw[:, v, :], f(cx[:, v, 0:D]), ALU.subtract)\
                    .then_inc(s["cx_lo_v"], 1)

            def split_q(r, t, g):
                gg = r * GT + g
                dve.wait_ge(s["q_hi"], gg + 1)
                q = QBUF[t]
                dve.tensor_tensor(qt[:, 2 * q + 1, :, :], qo_tile(g), f(qt[:, 2 * q, :, :]), ALU.subtract)\
                    .then_inc(s["q_lo"], 1)

            def row_max(r, g, j):
                gg = r * GT + g
                if r:
                    dve.wait_ge(s["scores"], 3 * gg + j + 1)
                if r == 0:
                    v = prob[:, SB * j:SB * (j + 1)]
                    if not isinstance(g, int) or g:
                        dve.wait_ge(s["tr"], 3 * gg - 2 + j)
                    wait_apart(dve, s["scores"], 3 * gg + j + 1)
                    dve.tensor_tensor_reduce(out=v, in0=ps[:, j, 0:SB], in1=mask_b[:, SB * j:SB * (j + 1)], scale=1.0,
                                             scalar=-3.4e38, op0=ALU.add, op1=ALU.max, accum_out=mx4[:, j:j + 1])\
                        .then_inc(s["red"], 1)
                else:
                    dve.tensor_reduce(mx4[:, j:j + 1], ps[:, j, 0:SB], AX.X, ALU.max).then_inc(s["red"], 1)

            def neg_max(r, g):
                gg = r * GT + g
                n = 3
                if r:
                    n = 4
                    dve.tensor_copy(mx4[:, 3:4], lbq[:, bass.ds(g, 1)]).then_inc(s["sum_ready"], 1)
                    dve.wait_ge(s["sum_ready"], 2 * (gg - GT) + 1)
                dve.wait_ge(s["red"], 3 * gg + 3)
                dve.tensor_reduce(negm[:, :], mx4[:, 0:n], AX.X, ALU.max, negate=True).then_inc(s["neg_ready"], 1)

            def sums(r, g):
                gg = r * GT + g
                dve.wait_ge(s["exp_done"], gg + 1)
                dve.wait_ge(s["o_ready"], r * (GT + 1) + g + 1)
                if r == 0:
                    dve.reciprocal(rinv[:, :], rowsum[:, :]).then_inc(s["rinv_ready"], 1)
                else:
                    dve.tensor_tensor(total[:, :], rowsum[:, :], extra[:, :], ALU.add).then_inc(s["sum_ready"], 1)
                    dve.wait_ge(s["sum_ready"], 2 * (gg - GT) + 2)
                    dve.reciprocal(rinv[:, :], total[:, :]).then_inc(s["pb_ready"], 1)
                    dve.wait_ge(s["pb_ready"], gg - GT + 1)
                    dve.tensor_tensor(pbq[:, bass.ds(g, 1)], extra[:, :], rinv[:, :], ALU.mult)\
                        .then_inc(s["rinv_ready"], 1)

            def low_probs(r, g, k):
                gg = r * GT + g
                dve.wait_ge(s["p_hi"], 3 * gg + k + 1)
                v = slice(GRP * k, GRP * (k + 1))
                dve.tensor_tensor(pt[:, 1, v, :], ps[:, 3 + k, :].rearrange("p (c q) -> p c q", q=P),
                                  f(pt[:, 0, v, :]), ALU.subtract).then_inc(s["p_lo"], 1)

            def batch(r, b, last):
                for t in range(TILES):
                    g = TILES * b + t
                    gg = r * GT + g
                    end = last and t == TILES - 1
                    if r == 0 and t == TILES - 1 and not last:
                        mask_bias(b + 1)
                    for k in range(3):
                        if not end:
                            row_max(r, g + 1, k)
                        if k == 2 and not end:
                            neg_max(r, g + 1)
                        low_probs(r, g, k)
                    if not (last and t >= TILES - 2):
                        split_q(r, (t + 2) % TILES, g + 2)
                    if r == 0 and not last:
                        if t == 1:
                            load_stats(b + 1, 0, 5)
                        if t == 2:
                            load_stats(b + 1, 5, CH)
                    if t == 5 and not last:
                        split_ct(r, b + 1)
                    dve.wait_ge(s["o_low_ready"], gg + 1)
                    dve.wait_ge(s["rinv_ready"], gg + 1)
                    dve.wait_ge(s["o_t"], r * (GT + 1) + g + 1)
                    dve.scalar_tensor_tensor(out=o_row[:, :], in0=ps[:, 6, 0:D], scalar=rinv[:, :], in1=o_low[:, :],
                                             op0=ALU.mult, op1=ALU.add).then_inc(s["o_ready"], 1)
                    if not end:
                        sums(r, g + 1)
                    if r == 0 and not last and t >= 4:
                        scale_tokens(b + 1, t - 4)
                    if t == TILES - 1 and not last:
                        split_cx(r, b + 1)

            def run(r):
                dve.memset(prob[:, S:CH * P], 0.0)
                dve.memset(o_row[:, :], 0.0).then_inc(s["o_ready"], 1)
                if r == 0:
                    split_ct(r, 0)
                    mask_bias(0)
                    for k in range(3):
                        scale_tokens(0, k)
                split_cx(r, 0)
                for k in range(3):
                    row_max(r, 0, k)
                if r:
                    dve.wait_ge(s["small_pe"], 3 * (r - 1) + 2)
                    dve.tensor_copy(lbq[:, :], ps[:, 3, 0:GT]).then_inc(s["small_dve"], 1)
                    dve.wait_ge(s["small_dve"], 5 * (r - 1) + 3)
                neg_max(r, 0)
                sums(r, 0)
                with dve.Fori(0, B - 1) as b:
                    batch(r, b, False)
                batch(r, B - 1, True)

            def split_heads(i, n, slot):
                dve.wait_ge(s["oh_hi"], H * i + n + 1)
                v = (oh if i else oh0)[:, 2 * slot:2 * slot + 2, :]
                v = v.rearrange("p s (e b q) -> p s e b q", e=DH, b=B)
                for e in range(DH):
                    ins = dve.tensor_tensor(v[:, 1, e, :, :], qo_head(n)[:, e, :, :], f(v[:, 0, e, :, :]), ALU.subtract)
                ins.then_inc(s["oh_lo"], 1)

            split_q(0, 0, 0)
            split_q(0, 1, 1)
            run(0)
            drain(dve, 3)
            dve.wait_ge(s["w0_in"], 80)
            for e in range(DH):
                ins = dve.tensor_scalar(w0[:, 4 + e, :], w0[:, e, :], V["g0"][:, e:e + 1], None, ALU.mult)
            ins.then_inc(s["w0_centred"], 1)
            dve.wait_ge(s["w0_mean"], 1)
            dve.tensor_copy(bias0[:, :], ps[:, 5, 0:2])
            dve.tensor_tensor(w0[:, 4:6, :], w0[:, 4:6, :], ps[:, 4:5, 0:D].to_broadcast([P, DH, D]), ALU.subtract)\
                .then_inc(s["w0_centred"], 1)
            for h in range(H):
                split_heads(0, h, h % 3)
            for jc in (0, 1):
                dve.wait_ge(s["h1_hi"], 2 + jc + 1)
                dve.scalar_tensor_tensor(out=q_s[:, 2 + jc, :], in0=ps[:, jc, 0:NQ], scalar=bias0[:, jc:jc + 1],
                                         in1=f(q_s[:, jc, :]), op0=ALU.add, op1=ALU.subtract).then_inc(s["h1_lo"], 1)
            dve.wait_ge(s["y_done"], 1)
            for e in range(DH):
                dve.scalar_tensor_tensor(out=xt[:, e, :], in0=ps[:, 2 + e, 0:NQ], scalar=gate_t[:, 1:2],
                                         in1=xt[:, e, :], op0=ALU.mult, op1=ALU.add).then_inc(s["x_ready"], 1)
            drain(dve, 4)

            def norm(n, scale, offset):
                k = LN_V * n
                dve.wait_ge(s["ln_pe"], 3 * n + 1)
                dve.tensor_tensor(xc, xt[:, :, :], ps[:, 0:1, 0:NQ].to_broadcast([P, DH, NQ]), ALU.subtract)\
                    .then_inc(s["ln_dve"], 1)
                dve.wait_ge(s["ln_dve"], k + 1)
                dve.tensor_tensor(sq, xc, xc, ALU.mult).then_inc(s["ln_dve"], 1)
                dve.wait_ge(s["ln_pe"], 3 * n + 2)
                dve.tensor_scalar(rs4, ps[0:QC, 1, 0:NQ // QC], EPS, None, ALU.add).then_inc(s["ln_dve"], 1)
                dve.wait_ge(s["ln_pow"], n + 1)
                dve.scalar_tensor_tensor(out=diag,
                                         in0=ident[0:QC, 0:QC].rearrange("p (o q) -> p o q", o=1)
                                         .to_broadcast([QC, NQ // QC, QC]),
                                         scalar=float(D),
                                         in1=rs4.rearrange("p (c o) -> p c o", o=1).to_broadcast([QC, NQ // QC, QC]),
                                         op0=ALU.mult, op1=ALU.mult).then_inc(s["ln_dve"], 1)
                dve.wait_ge(s["ln_pe"], 3 * n + 3)
                for e in range(DH):
                    dve.scalar_tensor_tensor(out=ht[:, e, :], in0=xc[:, e, :], scalar=scale[:, e:e + 1],
                                             in1=ps[:, 2, 0:NQ], op0=ALU.mult, op1=ALU.mult)\
                        .then_inc(s["ln_dve"], 1)
                for e in range(DH):
                    dve.wait_ge(s["h_hi"], DH * n + e + 1)
                    dve.scalar_tensor_tensor(out=hs[:, 1, e, :], in0=ht[:, e, :], scalar=offset[:, e:e + 1],
                                             in1=f(hs[:, 0, e, :]), op0=ALU.add, op1=ALU.subtract)\
                        .then_inc(s["h_lo"], 1)

            def first_split(kind, i, base, n, slot, fresh):
                dve.wait_ge(s["h1_hi"], 4 + base + n + 1)
                if kind == "m":
                    if not fresh:
                        dve.wait_ge(s["m2"], M2_0 + base + n - 1)
                    dve.tensor_copy(h1[:, 2 * slot, :], g32[:, slot, :]).then_inc(s["gelu_done"], 1)
                    dve.wait_ge(s["gelu_done"], n + 1)
                    dve.tensor_tensor(h1[:, 2 * slot + 1, :], g32[:, slot, :], f(h1[:, 2 * slot, :]), ALU.subtract)\
                        .then_inc(s["h1_lo"], 1)
                else:
                    col = hb[:, 2 * (i - 1) + (kind == "o"), bass.ds(n, 1)]
                    dve.scalar_tensor_tensor(out=h1[:, 2 * slot + 1, :], in0=ps[:, slot, 0:NQ], scalar=col,
                                             in1=f(h1[:, 2 * slot, :]), op0=ALU.add, op1=ALU.subtract)\
                        .then_inc(s["h1_lo"], 1)

            def extra_key(i, n, slot):
                j = A_BASE[i] // 2 + n
                dve.wait_ge(s["dk_ready"], j + 1)
                if not isinstance(j, int) or j:
                    dve.wait_ge(s["u_ready"], j)
                dve.tensor_tensor(dk_prod, w_raw[:, slot, 0:D].rearrange("p (e k) -> p e k", e=DH),
                                  dk_raw[:, slot:slot + 1, 0:P].to_broadcast([P, DH, P]), ALU.mult).then_inc(s["prod_ready"], 1)
                dve.wait_ge(s["prod_ready"], j + 1)
                dve.tensor_reduce(u_k[:, :, bass.ds(n, 1)], dk_prod, AX.X, ALU.add).then_inc(s["u_ready"], 1)

            def extra_value(i, n, slot, fresh):
                if not fresh:
                    dve.wait_ge(s["m1"], M1_0 + O_BASE[i] + n - 1)
                dve.tensor_scalar(dv_m[0:80, slot, :], dvr[:, :], hsel[0:80, bass.ds(n, 1)], None, ALU.mult)\
                    .then_inc(s["dv_ready"], 1)

            def head_constants(i):
                dve.wait_ge(s["small_in"], 144 * (i - 1) + 48)
                dve.tensor_tensor(cb[:, 3 * P:4 * P], cb[:, P:2 * P], cb[:, 2 * P:3 * P], ALU.subtract)\
                    .then_inc(s["fix_v"], 1)
                dve.wait_ge(s["fix_v"], 9 * (i - 1) + 1)
                dve.tensor_tensor(cb[:, 3 * P:4 * P], cb[:, 3 * P:4 * P], cb[:, 0:P], ALU.mult).then_inc(s["fix_v"], 1)
                dve.wait_ge(s["fix_v"], 9 * (i - 1) + 2)
                dve.tensor_reduce(cbv[:, :], cb[:, 3 * P:4 * P], AX.X, ALU.add).then_inc(s["small_dve"], 1)
                for v in (dv, dv2, pb_f):
                    dve.memset(v, 0.0).then_inc(s["fix_v"], 1)

            def products(kind, i, steps, base):
                def group(m, first, last):
                    for slot in range(NS):
                        n = NS * m + slot
                        if kind == "o" and not (last and slot >= NS - 2):
                            split_heads(i, n + 2, slot % 2)
                            extra_value(i, n + 2, slot % 2, False)
                        if not (last and slot == NS - 1):
                            if kind == "a":
                                extra_key(i, n + 1, (slot + 1) % NS)
                            first_split(kind, i, base, n + 1, (slot + 1) % 2, first and slot == 0)
                        if kind == "a":
                            dve.wait_ge(s["m2"], M2_0 + base + n + 1)
                            q_back(n, 3 + 2 * (slot % 2), SCALE)
                if kind == "o":
                    for n in (0, 1):
                        split_heads(i, n, n)
                        extra_value(i, n, n, True)
                    dve.wait_ge(s["small_dma"], 96 * i)
                    dve.tensor_copy(pb_s[:, :], pb_f).then_inc(s["fix_v"], 1)
                    dve.wait_ge(s["fix_v"], 9 * i)
                    dve.tensor_tensor(pb_s[32:64, :], pb_f[32:64, :], f(pb_s[32:64, :]), ALU.subtract)\
                        .then_inc(s["small_dve"], 1)
                if kind == "a":
                    split_ct(i, 0)
                    extra_key(i, 0, 0)
                first_split(kind, i, base, 0, 0, True)
                if kind == "a":
                    head_constants(i)
                groups(dve, steps, group)

            def add_output(bias, base, steps):
                dve.wait_ge(s["m2"], M2_0 + base + steps)
                for e in range(DH):
                    dve.scalar_tensor_tensor(out=xt[:, e, :], in0=ps[:, 6 + e, 0:NQ], scalar=bias[:, e:e + 1],
                                             in1=xt[:, e, :], op0=ALU.add, op1=ALU.add).then_inc(s["x_ready"], 1)

            for i in (1, 2):
                norm(i - 1, V[f"s{i}"], V[f"o{i}"])
                products("a", i, H, A_BASE[i])
                drain(dve, 3 * i + 2)
                split_q(i, 0, 0)
                split_q(i, 1, 1)
                dve.wait_ge(s["small_dve"], 5 * (i - 1) + 1)
                dve.wait_ge(s["small_pe"], 3 * (i - 1) + 1)
                dve.tensor_scalar(lb_s[:, :], ps[0:H, 3, 0:NQ], cbv[:, :], SCALE, ALU.add, ALU.mult)\
                    .then_inc(s["small_dve"], 1)
                run(i)
                drain(dve, 3 * i + 3)
                dve.wait_ge(s["small_pe"], 3 * (i - 1) + 3)
                dve.tensor_copy(tiles_row[:, :], ps[0:GT, 2, 0:P]).then_inc(s["small_dve"], 1)
                dve.wait_ge(s["small_in"], 144 * i)
                dve.tensor_tensor(dv2, dv, dv2, ALU.subtract).then_inc(s["fix_v"], 1)
                dve.wait_ge(s["fix_v"], 9 * (i - 1) + 6)
                dve.tensor_copy(dv_hi[:, :], dv2).then_inc(s["fix_v"], 1)
                dve.wait_ge(s["fix_v"], 9 * (i - 1) + 7)
                dve.tensor_copy(dvr[0:64, :], f(dv_hi[0:64, :]))
                dve.tensor_tensor(dvr[64:80, :], dv2[64:80, :], f(dv_hi[64:80, :]), ALU.subtract)\
                    .then_inc(s["fix_v"], 1)
                dve.wait_ge(s["fix_v"], 9 * (i - 1) + 8)
                products("o", i, H, O_BASE[i])
                add_output(V[f"bo{i}"], O_BASE[i], H)
                drain(dve, 3 * i + 4)
            norm(2, V["sm"], V["om"])
            products("m", 0, F // P, M_BASE)
            add_output(V["bf2"], M_BASE, F // P)
            drain(dve, 11)


def kernel(**inputs):
    import numpy as np
    import concourse.bacc as bacc
    from concourse.bass_utils import run_bass_kernel_spmd

    x = {k: np.asarray(v) for k, v in inputs.items()}
    l0, l1 = "L0_xattn_", "L1_xattn_"

    def cols(a, n):
        return np.ascontiguousarray(a.reshape(n, -1).T)

    ctx = x["ctx_2048"]
    arrays = {
        "xt": np.ascontiguousarray(x["x"].reshape(NQ, D).T),
        "ctx": np.ascontiguousarray(ctx),
        "ctx_t": np.ascontiguousarray(ctx.transpose(0, 2, 1)),
        "mask": np.ascontiguousarray(x["mask_BxS2_bf1"]).view(np.uint8),
        "gate": x[l0 + "gate"].reshape(1),
        "wq0t": np.ascontiguousarray(x[l0 + "Wq"].T),
        "wk0": np.ascontiguousarray(x[l0 + "Wk"]),
        "wv0t": np.ascontiguousarray(x[l0 + "Wv"].T),
        "wo0t": np.ascontiguousarray(x[l0 + "Wo"].T),
        "g0row": x[l0 + "ln_gamma"],
        "g0": cols(x[l0 + "ln_gamma"], 2), "b0": cols(x[l0 + "ln_beta"], 2),
        "sm": cols(x[l1 + "ln_mlp_scale"], 2), "om": cols(x[l1 + "ln_mlp_offset"], 2),
        "fc1": np.ascontiguousarray(x[l1 + "w_fc1"]), "fc2": np.ascontiguousarray(x[l1 + "w_fc2"]),
        "bf1": cols(x[l1 + "b_fc1"], 8), "bf2": cols(x[l1 + "b_fc2"], 2),
    }
    for i in (1, 2):
        arrays.update({
            f"s{i}": cols(x[f"{l1}ln{i}_scale"], 2), f"o{i}": cols(x[f"{l1}ln{i}_offset"], 2),
            f"wq{i}": np.ascontiguousarray(x[f"{l1}wq{i}"]),
            f"wk{i}": np.ascontiguousarray(x[f"{l1}wk{i}"].T),
            f"wv{i}": np.ascontiguousarray(x[f"{l1}wv{i}"]),
            f"wo{i}": np.ascontiguousarray(x[f"{l1}wo{i}"]),
            f"bq{i}": cols(x[f"{l1}bq{i}"], H), f"bv{i}": cols(x[f"{l1}bv{i}"], H),
            f"bq{i}h": x[f"{l1}bq{i}"].reshape(H, K), f"bv{i}h": x[f"{l1}bv{i}"].reshape(H, K),
            f"bk{i}": x[f"{l1}bk{i}"].reshape(H, K),
            f"biask{i}": x[f"{l1}bias_k{i}"].reshape(H, K), f"biasv{i}": x[f"{l1}bias_v{i}"].reshape(H, K),
            f"bo{i}": cols(x[f"{l1}bo{i}"], 2),
        })
    nc = bacc.Bacc("TRN2", target_bir_lowering=False, num_devices=1)
    io = {}
    for name, a in arrays.items():
        io[name] = nc.dram_tensor(f"in_{name}", a.shape, mybir.dt.from_np(a.dtype), kind="ExternalInput").ap()
    io["out"] = nc.dram_tensor("out_yt", (D, NQ), F32, kind="ExternalOutput").ap()
    io["lb_d"] = nc.dram_tensor("lb_scratch", (B * ROWS,), F32).ap()
    io["pb_d"] = nc.dram_tensor("pb_scratch", (B * ROWS,), F32).ap()
    io["st_d"] = nc.dram_tensor("stat_scratch", (CH, P), F32).ap()
    build(nc, io)
    r = run_bass_kernel_spmd(nc, [{f"in_{n}": a for n, a in arrays.items()}], core_ids=[0])
    return np.ascontiguousarray(r.results[0]["out_yt"].T).reshape(B, TQ, D)
```
